# Optimizing a Trainium2 kernel written in Bass

```python
import numpy as np
import jax
import jax.numpy as jnp

def _softmax(x, axis=-1):
    return jax.nn.softmax(x, axis=axis)

def _gelu(x):
    return jax.nn.gelu(x, approximate=True)

def _silu(x):
    return jax.nn.silu(x)

def _sigmoid(x):
    return jax.nn.sigmoid(x)

def _layernorm(x, axis=-1, eps=1e-05):
    m = jnp.mean(x, axis=axis, keepdims=True)
    v = jnp.var(x, axis=axis, keepdims=True)
    return (x - m) / jnp.sqrt(v + eps)

def _scatter_add(tgt, idx, src, axis=0):
    return tgt.at[idx].add(src)

def _segment_sum(src, seg, n):
    return jax.ops.segment_sum(src, seg, n)
kernel_name = 'mk_cond_resid_d4_seqx_r8_b43668'

def setup_inputs(seed: int=0):
    np.random.seed(seed)
    _w = jnp.asarray

    def _rec_inputs():
        import jax
        import jax.numpy as jnp
        _rk = jax.random.key(seed)
        x = -1.394e-06 + 0.9999 * jax.random.normal(jax.random.fold_in(_rk, 1), (128, 32, 256), jnp.float32)
        _lenS = 32 - jax.random.randint(jax.random.fold_in(_rk, 7), (128,), 0, max(1, 32 // 4) + 1, jnp.int32)
        _lenS2 = 32 - jax.random.randint(jax.random.fold_in(_rk, 8), (128,), 0, max(1, 32 // 4) + 1, jnp.int32)
        cond_2048 = -0.00499425 + 1.0058 * jax.random.normal(jax.random.fold_in(_rk, 11), (128, 256), jnp.float32)
        return (x, cond_2048)
    x, cond_2048 = _rec_inputs()

    def _L0_cond_setup():
        import jax, jax.numpy as jnp
        import numpy as np
        B, T, D = (16, 128, 256)
        key = jax.random.key(seed)
        k0, k1, k2, k3 = jax.random.split(key, 4)
        scale = 1.0 / np.sqrt(D)
        return {'initial_state': jax.random.normal(k0, (B, D), jnp.float32), 'inputs': jax.random.normal(k1, (B, T, D), jnp.float32), 'W_ih': jax.random.normal(k2, (D, 3 * D), jnp.float32) * scale, 'W_hh': jax.random.normal(k3, (D, 3 * D), jnp.float32) * scale, 'b_ih': jnp.zeros((3 * D,), jnp.float32), 'b_hh': jnp.zeros((3 * D,), jnp.float32)}
    _L0_cond_all = _L0_cond_setup()
    _L0_cond_in = {k: v for k, v in _L0_cond_all.items() if k in ('W_ih', 'W_hh', 'b_ih', 'b_hh')}
    del _L0_cond_all

    def _L1_cond_setup():
        import jax, jax.numpy as jnp
        import numpy as np
        DIM = 256
        H = 16
        DH = 128
        INNER = H * DH
        MLP = 4 * DIM
        B, T = (2, 256)
        EPS = 1e-06

        def _ln(x):
            mu = jnp.mean(x, axis=-1, keepdims=True)
            var = jnp.var(x, axis=-1, keepdims=True)
            return (x - mu) * jax.lax.rsqrt(var + EPS)
        key = jax.random.key(seed)
        ks = jax.random.split(key, 12)
        s = 0.02
        return {'x': jax.random.normal(ks[0], (B, T, DIM), jnp.float32), 'timestep_embed': jax.random.normal(ks[1], (B, DIM), jnp.float32), 'ada_w': jax.random.normal(ks[2], (DIM, 6 * DIM), jnp.float32) * s, 'ada_b': jnp.zeros((6 * DIM,), jnp.float32), 'qkv_w': jax.random.normal(ks[3], (DIM, 3 * INNER), jnp.float32) * s, 'qkv_b': jnp.zeros((3 * INNER,), jnp.float32), 'out_w': jax.random.normal(ks[4], (INNER, DIM), jnp.float32) * s, 'out_b': jnp.zeros((DIM,), jnp.float32), 'ffn_w1': jax.random.normal(ks[5], (DIM, MLP), jnp.float32) * s, 'ffn_b1': jnp.zeros((MLP,), jnp.float32), 'ffn_w2': jax.random.normal(ks[6], (MLP, DIM), jnp.float32) * s, 'ffn_b2': jnp.zeros((DIM,), jnp.float32)}
    _L1_cond_all = _L1_cond_setup()
    _L1_cond_in = {k: v for k, v in _L1_cond_all.items() if k in ('ada_w', 'ada_b', 'qkv_w', 'qkv_b', 'out_w', 'out_b', 'ffn_w1', 'ffn_b1', 'ffn_w2', 'ffn_b2')}
    del _L1_cond_all

    def _L2_cond_setup():
        import jax, jax.numpy as jnp
        import numpy as np
        HEADS = 16
        EPS = 1e-06

        def _rms_norm(x, g):
            xf = x.astype(jnp.float32)
            y = xf * jax.lax.rsqrt(jnp.mean(xf * xf, axis=-1, keepdims=True) + EPS)
            return y.astype(x.dtype) * g
        key = jax.random.key(seed)
        ks = jax.random.split(key, 6)
        b, n, dim, emb_dim = (4, 256, 256, 256)
        d_head = dim // HEADS
        return {'x': jax.random.normal(ks[0], (b, n, dim), jnp.float32), 'emb': jax.random.normal(ks[1], (b, 1, emb_dim), jnp.float32), 'W_emb': jax.random.normal(ks[2], (emb_dim, 2 * dim), jnp.float32) * emb_dim ** (-0.5), 'b_emb': jnp.zeros((2 * dim,), jnp.float32), 'g_norm': jnp.ones((dim,), jnp.float32), 'W_qkv': jax.random.normal(ks[3], (dim, 3 * dim), jnp.float32) * dim ** (-0.5), 'g_q': jnp.ones((d_head,), jnp.float32), 'g_k': jnp.ones((d_head,), jnp.float32), 'W_out': jax.random.normal(ks[4], (dim, dim), jnp.float32) * dim ** (-0.5)}
    _L2_cond_all = _L2_cond_setup()
    _L2_cond_in = {k: v for k, v in _L2_cond_all.items() if k in ('W_emb', 'b_emb', 'g_norm', 'W_qkv', 'g_q', 'g_k', 'W_out')}
    del _L2_cond_all

    def _L3_cond_setup():
        import jax, jax.numpy as jnp
        import numpy as np
        DT = 0.01
        EPSILON = 0.08
        ALPHA = 0.7
        BETA = 0.8
        CLAMP = 20.0
        B, T, N = (32, 128, 256)

        def _derivative(q, p, drive, coupling, bias):
            i_couple = jnp.tanh(q) @ coupling.T
            dq = q - q ** 3 / 3.0 - p + drive + i_couple + bias
            dp = EPSILON * (q + ALPHA - BETA * p)
            return (dq, dp)

        def _rk4_step(q, p, drive, coupling, bias):
            dq1, dp1 = _derivative(q, p, drive, coupling, bias)
            dq2, dp2 = _derivative(q + 0.5 * DT * dq1, p + 0.5 * DT * dp1, drive, coupling, bias)
            dq3, dp3 = _derivative(q + 0.5 * DT * dq2, p + 0.5 * DT * dp2, drive, coupling, bias)
            dq4, dp4 = _derivative(q + DT * dq3, p + DT * dp3, drive, coupling, bias)
            q_next = q + DT / 6.0 * (dq1 + 2 * dq2 + 2 * dq3 + dq4)
            p_next = p + DT / 6.0 * (dp1 + 2 * dp2 + 2 * dp3 + dp4)
            q_next = jnp.clip(q_next, -CLAMP, CLAMP)
            p_next = jnp.clip(p_next, -CLAMP, CLAMP)
            return (q_next, p_next)
        key = jax.random.key(seed)
        k1, k2, k3, k4 = jax.random.split(key, 4)
        return {'q0': jax.random.normal(k1, (B, N), dtype=jnp.float32), 'p0': jax.random.normal(k2, (B, N), dtype=jnp.float32), 'input_drive_seq': jax.random.normal(k3, (B, T, N), dtype=jnp.float32), 'coupling': jax.random.normal(k4, (N, N), dtype=jnp.float32) * 0.01, 'bias': jnp.zeros((N,), dtype=jnp.float32)}
    _L3_cond_all = _L3_cond_setup()
    _L3_cond_in = {k: v for k, v in _L3_cond_all.items() if k in ('coupling', 'bias')}
    del _L3_cond_all
    return {'x': x, 'cond_2048': cond_2048, 'L0_cond_W_ih': _L0_cond_in['W_ih'], 'L0_cond_W_hh': _L0_cond_in['W_hh'], 'L0_cond_b_ih': _L0_cond_in['b_ih'], 'L0_cond_b_hh': _L0_cond_in['b_hh'], 'L1_cond_ada_w': _L1_cond_in['ada_w'], 'L1_cond_ada_b': _L1_cond_in['ada_b'], 'L1_cond_qkv_w': _L1_cond_in['qkv_w'], 'L1_cond_qkv_b': _L1_cond_in['qkv_b'], 'L1_cond_out_w': _L1_cond_in['out_w'], 'L1_cond_out_b': _L1_cond_in['out_b'], 'L1_cond_ffn_w1': _L1_cond_in['ffn_w1'], 'L1_cond_ffn_b1': _L1_cond_in['ffn_b1'], 'L1_cond_ffn_w2': _L1_cond_in['ffn_w2'], 'L1_cond_ffn_b2': _L1_cond_in['ffn_b2'], 'L2_cond_W_emb': _L2_cond_in['W_emb'], 'L2_cond_b_emb': _L2_cond_in['b_emb'], 'L2_cond_g_norm': _L2_cond_in['g_norm'], 'L2_cond_W_qkv': _L2_cond_in['W_qkv'], 'L2_cond_g_q': _L2_cond_in['g_q'], 'L2_cond_g_k': _L2_cond_in['g_k'], 'L2_cond_W_out': _L2_cond_in['W_out'], 'L3_cond_coupling': _L3_cond_in['coupling'], 'L3_cond_bias': _L3_cond_in['bias']}

def reference(x, cond_2048, L0_cond_W_ih, L0_cond_W_hh, L0_cond_b_ih, L0_cond_b_hh, L1_cond_ada_w, L1_cond_ada_b, L1_cond_qkv_w, L1_cond_qkv_b, L1_cond_out_w, L1_cond_out_b, L1_cond_ffn_w1, L1_cond_ffn_b1, L1_cond_ffn_w2, L1_cond_ffn_b2, L2_cond_W_emb, L2_cond_b_emb, L2_cond_g_norm, L2_cond_W_qkv, L2_cond_g_q, L2_cond_g_k, L2_cond_W_out, L3_cond_coupling, L3_cond_bias):
    import jax
    import jax.numpy as jnp

    def _L0_cond_ref(initial_state, inputs, W_ih, W_hh, b_ih, b_hh):
        import jax, jax.numpy as jnp
        import numpy as np
        B, T, D = (16, 128, 256)
        "ScanOverTime(GRU cell): sequential per-timestep module call with\n            dict-state passing; merge_dict_trees stacks the per-step\n            'state_predicted' tensors along axis=1 -> [B, T, D]."

        def cell(h, x):
            gi = x @ W_ih + b_ih
            gh = h @ W_hh + b_hh
            i_r, i_z, i_n = jnp.split(gi, 3, axis=-1)
            h_r, h_z, h_n = jnp.split(gh, 3, axis=-1)
            r = jax.nn.sigmoid(i_r + h_r)
            z = jax.nn.sigmoid(i_z + h_z)
            n = jnp.tanh(i_n + r * h_n)
            h_new = (1.0 - z) * n + z * h
            return (h_new, h_new)
        xs = jnp.swapaxes(inputs, 0, 1)
        _, hs = jax.lax.scan(cell, initial_state, xs)
        return jnp.swapaxes(hs, 0, 1)

    def _L1_cond_ref(x, timestep_embed, ada_w, ada_b, qkv_w, qkv_b, out_w, out_b, ffn_w1, ffn_b1, ffn_w2, ffn_b2):
        import jax, jax.numpy as jnp
        import numpy as np
        DIM = 256
        H = 16
        DH = 128
        INNER = H * DH
        MLP = 4 * DIM
        B, T = (2, 256)
        EPS = 1e-06

        def _ln(x):
            mu = jnp.mean(x, axis=-1, keepdims=True)
            var = jnp.var(x, axis=-1, keepdims=True)
            return (x - mu) * jax.lax.rsqrt(var + EPS)
        Bc, Tc, D = x.shape
        ada = (timestep_embed @ ada_w + ada_b)[:, None, :]
        shift1, scale1, gate1, shift2, scale2, gate2 = jnp.split(ada, 6, axis=-1)
        x1 = _ln(x) * (1.0 + scale1) + shift1
        qkv = (x1 @ qkv_w + qkv_b).reshape(Bc, Tc, 3, H, DH)
        q, k, v = (qkv[:, :, 0], qkv[:, :, 1], qkv[:, :, 2])
        scale = DH ** (-0.5)
        attn = jnp.einsum('bthd,bshd->bhts', q, k) * scale
        attn = jax.nn.softmax(attn, axis=-1)
        attn_out = jnp.einsum('bhts,bshd->bthd', attn, v).reshape(Bc, Tc, INNER)
        attn_out = attn_out @ out_w + out_b
        x = x + gate1 * attn_out
        x2 = _ln(x) * (1.0 + scale2) + shift2
        h = jax.nn.gelu(x2 @ ffn_w1 + ffn_b1, approximate=False)
        x = x + gate2 * (h @ ffn_w2 + ffn_b2)
        return x

    def _L2_cond_ref(x, emb, W_emb, b_emb, g_norm, W_qkv, g_q, g_k, W_out):
        import jax, jax.numpy as jnp
        import numpy as np
        HEADS = 16
        EPS = 1e-06

        def _rms_norm(x, g):
            xf = x.astype(jnp.float32)
            y = xf * jax.lax.rsqrt(jnp.mean(xf * xf, axis=-1, keepdims=True) + EPS)
            return y.astype(x.dtype) * g
        b, n, dim = x.shape
        h = HEADS
        d = dim // h
        scale_shift = emb @ W_emb + b_emb
        scale, shift = jnp.split(scale_shift, 2, axis=-1)
        xn = _rms_norm(x, g_norm) * (1.0 + scale) + shift
        qkv = xn @ W_qkv
        qkv = qkv.reshape(b, n, 3, h, d)
        q, k, v = jnp.moveaxis(qkv, 2, 0)
        q = jnp.swapaxes(q, 1, 2)
        k = jnp.swapaxes(k, 1, 2)
        v = jnp.swapaxes(v, 1, 2)
        q = _rms_norm(q, g_q)
        k = _rms_norm(k, g_k)
        logits = jnp.einsum('bhqd,bhkd->bhqk', q, k) * d ** (-0.5)
        attn = jax.nn.softmax(logits, axis=-1)
        o = jnp.einsum('bhqk,bhkd->bhqd', attn, v)
        o = jnp.swapaxes(o, 1, 2).reshape(b, n, dim)
        return o + o @ W_out

    def _L3_cond_ref(q0, p0, input_drive_seq, coupling, bias):
        import jax, jax.numpy as jnp
        import numpy as np
        DT = 0.01
        EPSILON = 0.08
        ALPHA = 0.7
        BETA = 0.8
        CLAMP = 20.0
        B, T, N = (32, 128, 256)

        def _derivative(q, p, drive, coupling, bias):
            i_couple = jnp.tanh(q) @ coupling.T
            dq = q - q ** 3 / 3.0 - p + drive + i_couple + bias
            dp = EPSILON * (q + ALPHA - BETA * p)
            return (dq, dp)

        def _rk4_step(q, p, drive, coupling, bias):
            dq1, dp1 = _derivative(q, p, drive, coupling, bias)
            dq2, dp2 = _derivative(q + 0.5 * DT * dq1, p + 0.5 * DT * dp1, drive, coupling, bias)
            dq3, dp3 = _derivative(q + 0.5 * DT * dq2, p + 0.5 * DT * dp2, drive, coupling, bias)
            dq4, dp4 = _derivative(q + DT * dq3, p + DT * dp3, drive, coupling, bias)
            q_next = q + DT / 6.0 * (dq1 + 2 * dq2 + 2 * dq3 + dq4)
            p_next = p + DT / 6.0 * (dp1 + 2 * dp2 + 2 * dp3 + dp4)
            q_next = jnp.clip(q_next, -CLAMP, CLAMP)
            p_next = jnp.clip(p_next, -CLAMP, CLAMP)
            return (q_next, p_next)
        drive_tbn = jnp.swapaxes(input_drive_seq, 0, 1)

        def scan_fn(carry, drive):
            q, p = carry
            q, p = _rk4_step(q, p, drive, coupling, bias)
            return ((q, p), q)
        (_, _), q_trace_tbn = jax.lax.scan(scan_fn, (q0, p0), drive_tbn)
        return jnp.swapaxes(q_trace_tbn, 0, 1)
    x = x + _L0_cond_ref(cond_2048, x, L0_cond_W_ih, L0_cond_W_hh, L0_cond_b_ih, L0_cond_b_hh)
    x = x + _L1_cond_ref(x, cond_2048, L1_cond_ada_w, L1_cond_ada_b, L1_cond_qkv_w, L1_cond_qkv_b, L1_cond_out_w, L1_cond_out_b, L1_cond_ffn_w1, L1_cond_ffn_b1, L1_cond_ffn_w2, L1_cond_ffn_b2)
    x = x + _L2_cond_ref(x, cond_2048[:, None, :], L2_cond_W_emb, L2_cond_b_emb, L2_cond_g_norm, L2_cond_W_qkv, L2_cond_g_q, L2_cond_g_k, L2_cond_W_out)
    x = x + _L3_cond_ref(cond_2048, cond_2048, x, L3_cond_coupling, L3_cond_bias)
    return x

_drawn_inputs = setup_inputs


def setup_inputs(seed=0):
    import zlib

    import numpy as np

    out = dict(_drawn_inputs(seed))
    spreads = {'L0_cond_b_ih': (0.0, 0.1),
     'L0_cond_b_hh': (0.0, 0.271),
     'L1_cond_ada_b': (0.0, 0.601),
     'L1_cond_qkv_b': (0.0, 0.44),
     'L1_cond_out_b': (0.0, 0.45),
     'L1_cond_ffn_b1': (0.0, 0.8),
     'L1_cond_ffn_b2': (0.0, 0.427),
     'L2_cond_b_emb': (0.0, 0.1),
     'L2_cond_g_norm': (1.0, 0.2),
     'L2_cond_g_q': (1.0, 0.6),
     'L2_cond_g_k': (1.0, 0.6),
     'L3_cond_bias': (0.0, 0.8)}
    factors = {'L1_cond_ffn_w1': 3.662, 'L1_cond_ffn_w2': 3.187, 'L3_cond_coupling': 8.0}
    for name, (base, spread) in spreads.items():
        noise = np.random.default_rng([zlib.crc32(name.encode()), seed]).standard_normal(out[name].shape)
        drawn = base * np.exp(spread * noise) if base else spread * noise
        out[name] = jnp.asarray(drawn.astype(out[name].dtype))
    for name, factor in factors.items():
        out[name] = (out[name] * factor).astype(out[name].dtype)
    return out
```

```python
from contextlib import ExitStack

import concourse.bass as bass
from concourse import mybir

ALU = mybir.AluOpType
ACT = mybir.ActivationFunctionType
F32 = mybir.dt.float32
AX_X = mybir.AxisListType.X

B, T, D = 128, 32, 256
P = 128
C = D // P
LOT_B = 16
LOTS = B // LOT_B
LOT = LOT_B * T
G = LOT // P
GB = P // T
H = 16
DH1 = 128
DH2 = D // H
INNER = H * DH1
QUAD = 4
QUADS = H // QUAD
MLP = 4 * D
HC = P // DH2
EPS = 1e-6

DT, EPSILON, ALPHA, BETA, CLAMP = 0.01, 0.08, 0.7, 0.8, 20.0

ROWS = {}
for _name, _n in (("b_ih", 6), ("b_hh", 6), ("ada_b", 12), ("qkv_b", 48), ("out_b", 2), ("ffn_b1", 8),
                  ("ffn_b2", 2), ("b_emb", 4), ("g_norm", 2), ("bias", 2), ("g_q", 1), ("g_k", 1)):
    ROWS[_name] = (sum(n for _, n in ROWS.values()), _n)
N_ROWS = sum(n for _, n in ROWS.values())

SHIFT1, SCALE1, GATE1, SHIFT2, SCALE2, GATE2, SCALE3, SHIFT3 = range(0, 16, 2)


class Signal:

    def __init__(self, sem, per=0):
        self.sem, self.per = sem, per

    def at(self, turn, k):
        return turn * self.per + k


class Chain:

    def __init__(self, eng, sem):
        self.eng, self.sem, self.base, self.k = eng, sem, 0, 0

    def start(self, base):
        self.base, self.k = base, 0

    def link(self, ins):
        ins.then_inc(self.sem, 1)
        self.k += 1
        self.eng.wait_ge(self.sem, self.base + self.k)


def lot_banks():
    fills = [("xin", 0, "act"), ("xin", 1, "act"), ("m1", 0, "dve"), ("m1", 1, "dve")]

    def qk(q):
        return [(n, QUAD * q + h, "act") for h in range(QUAD) for n in ("q", "k")]

    def v(q):
        return [("v", G * q + g, "dve") for g in range(G)]

    fills += qk(0) + v(0)
    for q in range(QUADS):
        if q < QUADS - 1:
            fills += qk(q + 1)
        fills += [("o", QUAD * q + h, "act") for h in range(QUAD)]
        if q < QUADS - 1:
            fills += v(q + 1)
    fills += [("y", 0, "dve"), ("y", 1, "dve"), ("m2", 0, "dve"), ("m2", 1, "dve")]
    fills += [("h", m, "act") for m in range(MLP // P)]
    fills += [("f", 0, "dve"), ("f", 1, "dve"), ("m3", 0, "dve"), ("m3", 1, "dve")]
    fills += [("qk2", g, "act") for g in range(G)] + [("v2", 0, "act"), ("t2", 0, "dve")]
    for g in range(G):
        if g < G - 1:
            fills += [("t2", g + 1, "dve")]
        fills += [("o2", g, "act")]
        if g < G - 1:
            fills += [("v2", g + 1, "act")]
        fills += [("w2", g, "dve")]
    return fills + [("xo", 0, "act"), ("xo", 1, "act")]


FILLS = lot_banks()
WORK_BANKS = 4
ORDINAL = {(n, i): k + 1 for k, (n, i, _) in enumerate(FILLS)}
EMPTIES = {}
for _who in ("act", "dve"):
    for _k, (_n, _i, _w) in enumerate([f for f in FILLS if f[2] == _who]):
        EMPTIES[(_n, _i)] = (_who, _k + 1)
PER_EMPTIED = {w: sum(f[2] == w for f in FILLS) for w in ("act", "dve")}

DVE_LINKS = 43


def build(nc, A, out):
    with ExitStack() as ctx:
        def sb(name, shape, dt=F32):
            return ctx.enter_context(nc.sbuf_tensor(name, shape, dt))

        def sem(name, per=0):
            return Signal(ctx.enter_context(nc.semaphore(name)), per)

        bank = [ctx.enter_context(nc.psum_tensor(f"bank{i}", [P, 512], F32)) for i in range(8)]
        work_bank, y_bank, s_bank = bank[0:4], bank[4:6], bank[6:8]

        x_feat = sb("x_feat", [P, C, T, B])
        w_qkv = sb("w_qkv", [P, C, 3 * INNER])
        w_out = sb("w_out", [P, H, D])
        w_f1 = sb("w_f1", [P, C, MLP])
        w_f2 = sb("w_f2", [P, MLP // P, D])
        w_qkv2 = sb("w_qkv2", [P, C, 3 * D])
        w_out2 = sb("w_out2", [P, C, D])
        coupT = sb("coupT", [P, C, D])
        mod = sb("mod", [P, 16, B])
        col = sb("col", [P, N_ROWS])
        bsum = sb("bsum", [P, 4])
        ident = sb("ident", [P, P])
        condT = sb("condT", [P, C, B])
        k_mask = sb("k_mask", [P, HC])
        minus_half = sb("minus_half", [P, 2 * H])

        arena = sb("arena", [P, 17024])

        def view(name, at, size):
            assert at + size <= 17024

            return arena[:, at:at + size]

        x_rows = view("x_rows", 0, T * D).rearrange("p (t d) -> p t d", t=T)
        ada_w = view("ada_w", 8192, 3072).rearrange("p (c n) -> p c n", c=C)
        w_emb = view("w_emb", 11264, 1024).rearrange("p (c n) -> p c n", c=C)
        coup_rows = view("coup_rows", 12288, 512).rearrange("p (c n) -> p c n", c=C)
        w_ih = view("w_ih", 12800, 1536).rearrange("p (c n) -> p c n", c=C)
        w_hh = view("w_hh", 14336, 1536).rearrange("p (c n) -> p c n", c=C)
        cond = view("cond", 15872, 256)
        rows = view("rows", 16128, 128)
        gq_row = view("gq_row", 16256, 128)
        h_buf = view("h_buf", 0, 512).rearrange("p (s c b) -> p s c b", s=2, c=C)
        gate_r = view("gate_r", 512, 256).rearrange("p (c b) -> p c b", c=C)
        gate_z = view("gate_z", 768, 256).rearrange("p (c b) -> p c b", c=C)
        one_z = view("one_z", 1024, 256).rearrange("p (c b) -> p c b", c=C)
        z_h = view("z_h", 1280, 256).rearrange("p (c b) -> p c b", c=C)
        pre_n = view("pre_n", 1536, 256).rearrange("p (c b) -> p c b", c=C)
        cand = view("cand", 1792, 256).rearrange("p (c b) -> p c b", c=C)
        x_lot = view("x_lot", 0, 1024).rearrange("p (c n) -> p c n", c=C)
        x0_tok = view("x0_tok", 1024, 1024).rearrange("p (g d) -> p g d", g=G)
        x_tok = view("x_tok", 2048, 1024).rearrange("p (g d) -> p g d", g=G)
        xm = view("xm", 3072, 1024).rearrange("p (c n) -> p c n", c=C)
        qT = view("qT", 4096, 2048).rearrange("p (h n) -> p h n", h=QUAD)
        kT = view("kT", 6144, 2048).rearrange("p (h n) -> p h n", h=QUAD)
        hT = view("hT", 4096, 4096).rearrange("p (m n) -> p m n", m=MLP // P)
        qk2 = view("qk2", 4096, 2048).rearrange("p (g n) -> p g n", g=G)
        qk_sq = view("qk_sq", 6144, 512)
        qk_n = view("qk_n", 6656, 1024).rearrange("p (s n) -> p s n", s=2)
        q2T = view("q2T", 7680, 512).rearrange("p (s c n) -> p s c n", s=2, c=C)
        v_tok = view("v_tok", 8192, 2048).rearrange("p (g n) -> p g n", g=G)
        yT = view("yT", 8192, 1024).rearrange("p (c n) -> p c n", c=C)
        prob = view("prob", 10240, 512)
        probT = view("probT", 10752, 2048).rearrange("p (h n) -> p h n", h=H)
        oT = view("oT", 12800, 2048).rearrange("p (h n) -> p h n", h=QUAD)
        xn = view("xn", 12800, 1024).rearrange("p (g d) -> p g d", g=G)
        k_wide = view("k_wide", 12800, 2048).rearrange("p (c b h t) -> p c b h t", c=C, b=GB, h=HC)
        v_wide = view("v_wide", 14848, 2048).rearrange("p (h n) -> p h n", h=H)
        v_diag = [arena[:, 14848 + c * HC * P:14848 + c * HC * P + HC * (P + DH2)].rearrange("p (h n) -> p h n", h=HC)[:, :, 0:DH2]
                  for c in range(C)]
        q_of = [view(f"q{i}", 256 * i, 256).rearrange("p (c b) -> p c b", c=C) for i in range(4)]
        p_of = [view(f"p{i}", 1024 + 256 * i, 256).rearrange("p (c b) -> p c b", c=C) for i in range(4)]
        names = ("tanh", "sq", "u", "v", "base", "drive", "m", "px", "py", "e", "f", "g", "pe", "pf", "pg", "raw", "p_raw", "outT")
        net = {n: view(n, 2048 + 256 * k, 256).rearrange("p (c b) -> p c b", c=C) for k, n in enumerate(names)}
        out_rows = view("out_rows", 8192, 256)

        o2T = sb("o2T", [P, C, P])
        tick = sb("tick", [P, 3])
        stats = sb("stats", [P, G, 6])
        mean_var = sb("mean_var", [P, G, 2])
        spread = sb("spread", [P, G])
        rstd = sb("rstd", [P, G])
        soft_max = sb("soft_max", [P, 16])
        soft_sum = sb("soft_sum", [P, 16])
        soft_inv = sb("soft_inv", [P, 16])
        ss2 = sb("ss2", [P, 2 * H])
        rstd2 = sb("rstd2", [P, 2 * H])

        cond_in, rows_in, ada_in, emb_in, coup_in = (sem(n) for n in ("cond_in", "rows_in", "ada_in", "emb_in", "coup_in"))
        gru_in = sem("gru_in")
        x_in = [sem(f"x_in{i}") for i in range(4)]
        lot_w_in, lot_w2_in = sem("lot_w_in"), sem("lot_w2_in")
        consts, ident_step = sem("consts"), sem("ident_step")
        set_filled, set_act, set_dve = sem("set_filled"), sem("set_act"), sem("set_dve")
        set_chain = sem("set_chain")
        gates_ready = sem("gates_ready", 3)
        r_ready, z_ready, n_ready = sem("r_ready", 2), sem("z_ready", 2), sem("n_ready", 2)
        r_used = sem("r_used", 2)
        pre_ready, one_z_ready = sem("pre_ready", 2), sem("one_z_ready", 1)
        z_h_ready, prod_ready = sem("z_h_ready", 1), sem("prod_ready", 2)
        h_ready, x_added = sem("h_ready", 2), sem("x_added", 1)
        staged = sem("staged", C)
        filled = sem("filled", len(FILLS))
        emptied = {"act": sem("act_emptied", PER_EMPTIED["act"]), "dve": sem("dve_emptied", PER_EMPTIED["dve"])}
        spread_ready, rstd_ready, xn_ready, mod_ready = sem("spread_ready", 3), sem("rstd_ready", 3), sem("xn_ready", 12), sem("mod_ready", 6)
        scores_ready, shifted, exp_ready, probT_ready = sem("scores_ready", 8), sem("shifted", 8), sem("exp_ready", 8), sem("probT_ready", 8)
        oT_used, y_ready, yT_ready = sem("oT_used", QUADS - 1), sem("y_ready", 2), sem("yT_ready", 4)
        doubled = sem("doubled", 1)
        sq_ready, ss2_ready, rstd2_ready, qkn_ready = sem("sq_ready", G), sem("ss2_ready", G), sem("rstd2_ready", G), sem("qkn_ready", G)
        dve_chain = sem("dve_chain", DVE_LINKS)
        zeroed = sem("zeroed")
        drive_ready = sem("drive_ready", C)
        tanh_ready, sq_net, u_ready, px_ready = sem("tanh_ready", 8), sem("sq_net", 4), sem("u_ready", 4), sem("px_ready", 4)
        m_ready, coupled, q_ready = sem("m_ready", 4), sem("coupled", 8), sem("q_ready", 8)
        py_ready, p_ready = sem("py_ready", 4), sem("p_ready", 4)
        v_ready, base_ready, clip_step = sem("v_ready", 4), sem("base_ready", 4), sem("clip_step", 6)
        e_ready, pe_ready, f_ready, g_ready, pf_ready, pg_ready = (sem(n, 1) for n in ("e_ready", "pe_ready", "f_ready", "g_ready", "pf_ready", "pg_ready"))
        outT_ready, turned, out_ready, out_sent, rows_free = sem("outT_ready", 1), sem("turned", 1), sem("out_ready", 1), sem("out_sent", 16), sem("rows_free", 1)

        def row(name):
            at, n = ROWS[name]
            return rows[at:at + n, :]

        def column(name, k=0):
            at, _ = ROWS[name]
            return col[:, at + k:at + k + 1]

        block = ctx.enter_context(nc.Block())

        X_PAIRS = T // 2
        order = ["turn", "coup"] + [f"x{i}" for i in range(X_PAIRS)] + [f"mod{i}" for i in range(4)]
        set_bank = {n: bank[i % 8] for i, n in enumerate(order)}
        set_who = {n: ("act" if n.startswith("x") and int(n[1:]) % 2 else "dve") for n in order}
        set_ord = {n: i + 1 for i, n in enumerate(order)}
        set_emptied = {}
        for who in ("act", "dve"):
            for k, n in enumerate([n for n in order if set_who[n] == who]):
                set_emptied[n] = k + 1
        SET_ACT, SET_DVE = (sum(set_who[n] == w for n in order) for w in ("act", "dve"))

        @block.sync
        def _(sp):
            sp.dma_start(cond, A["cond_2048"]).then_inc(cond_in.sem, 16)
            names = {"b_ih": "L0_cond_b_ih", "b_hh": "L0_cond_b_hh", "ada_b": "L1_cond_ada_b", "qkv_b": "L1_cond_qkv_b",
                     "out_b": "L1_cond_out_b", "ffn_b1": "L1_cond_ffn_b1", "ffn_b2": "L1_cond_ffn_b2",
                     "b_emb": "L2_cond_b_emb", "g_norm": "L2_cond_g_norm", "bias": "L3_cond_bias"}
            for name, arg in names.items():
                sp.dma_start(row(name), A[arg].rearrange("(c p) -> c p", p=P)).then_inc(rows_in.sem, 16)
            for name, arg in (("g_q", "L2_cond_g_q"), ("g_k", "L2_cond_g_k")):
                src = A[arg].rearrange("(a o d) -> a o d", a=1, o=1).to_broadcast([1, HC, DH2])
                sp.dma_start(row(name).rearrange("a (h d) -> a h d", d=DH2), src).then_inc(rows_in.sem, 16)
            for i in range(4):
                sp.dma_start(x_rows[:, 8 * i:8 * i + 8, :], A["x"][:, 8 * i:8 * i + 8, :]).then_inc(x_in[i].sem, 16)
                if i == 0:
                    sp.dma_start(coup_rows, A["L3_cond_coupling"].rearrange("(c p) n -> p c n", p=P)).then_inc(coup_in.sem, 16)
            sp.dma_start(ada_w, A["L1_cond_ada_w"].rearrange("(c p) n -> p c n", p=P)).then_inc(ada_in.sem, 16)
            sp.dma_start(w_emb, A["L2_cond_W_emb"].rearrange("(c p) n -> p c n", p=P)).then_inc(emb_in.sem, 16)
            sp.dma_start(w_ih, A["L0_cond_W_ih"].rearrange("(c p) n -> p c n", p=P)).then_inc(gru_in.sem, 16)
            sp.dma_start(w_hh, A["L0_cond_W_hh"].rearrange("(c p) n -> p c n", p=P)).then_inc(gru_in.sem, 16)
            sp.dma_start(w_out2[:, :, :], A["L2_cond_W_out"].rearrange("(c p) n -> p c n", p=P)).then_inc(lot_w2_in.sem, 16)
            sp.dma_start(w_qkv2[:, :, :], A["L2_cond_W_qkv"].rearrange("(c p) n -> p c n", p=P)).then_inc(lot_w_in.sem, 16)
            sp.dma_start(w_qkv[:, :, :], A["L1_cond_qkv_w"].rearrange("(c p) n -> p c n", p=P)).then_inc(lot_w_in.sem, 16)
            sp.dma_start(w_out[:, :, :], A["L1_cond_out_w"].rearrange("(h p) n -> p h n", p=P)).then_inc(lot_w_in.sem, 16)
            sp.dma_start(w_f1[:, :, :], A["L1_cond_ffn_w1"].rearrange("(c p) n -> p c n", p=P)).then_inc(lot_w_in.sem, 16)
            sp.dma_start(w_f2[:, :, :], A["L1_cond_ffn_w2"].rearrange("(m p) n -> p m n", p=P)).then_inc(lot_w_in.sem, 16)
            sp.sem_inc(rows_free.sem, 1)
            with sp.Fori(0, T) as t:
                sp.wait_ge(out_ready.sem, out_ready.at(t, 1))
                sp.dma_start(out[:, bass.ds(t, 1), :].rearrange("b t d -> b (t d)"), out_rows).then_inc(out_sent.sem, 16)
                sp.wait_ge(out_sent.sem, out_sent.at(t, 16))
                sp.sem_inc(rows_free.sem, 1)
            sp.wait_ge(out_sent.sem, 16 * T)

        @block.gpsimd
        def _(pool):
            pool.memset(ident[:, :], 0.0).then_inc(ident_step.sem, 1)
            pool.memset(k_mask[:, :], 1.0).then_inc(ident_step.sem, 1)
            pool.memset(minus_half[:, :], -0.5).then_inc(ident_step.sem, 1)
            pool.wait_ge(ident_step.sem, 3)
            pool.affine_select(out=k_mask[:, :], in_=k_mask[:, :], compare_op=ALU.is_ge, fill=0.0,
                               base=0, pattern=[[-DH2, HC]], channel_multiplier=1).then_inc(ident_step.sem, 1)
            pool.wait_ge(ident_step.sem, 4)
            pool.affine_select(out=k_mask[:, :], in_=k_mask[:, :], compare_op=ALU.is_ge, fill=0.0,
                               base=DH2 - 1, pattern=[[DH2, HC]], channel_multiplier=-1).then_inc(consts.sem, 1)
            pool.affine_select(out=ident[:, :], in_=ident[:, :], compare_op=ALU.not_equal, fill=1.0,
                               base=0, pattern=[[-1, P]], channel_multiplier=1).then_inc(consts.sem, 1)

            pool.sem_inc(x_added.sem, 2)
            with pool.Fori(0, T // 2) as i:
                for par in range(2):
                    t = i * 2 + par
                    pool.wait_ge(h_ready.sem, h_ready.at(t, 4))
                    xt = x_feat[:, :, bass.ds(t, 1), :].rearrange("p c t b -> p c (t b)")
                    pool.tensor_tensor(xt, xt, h_buf[:, 1 - par], ALU.add).then_inc(x_added.sem, 1)

            pool.wait_ge(x_added.sem, T + 2)
            pool.memset(probT, 0.0).then_inc(zeroed.sem, 1)
            pool.memset(v_wide, 0.0).then_inc(zeroed.sem, 1)
            with pool.Fori(0, LOTS) as s:
                for norm in range(3):
                    pool.wait_ge(spread_ready.sem, spread_ready.at(s, norm + 1))
                    pool.tensor_tensor(rstd[:, :], spread[:, :], minus_half[:, 0:G], ALU.pow).then_inc(rstd_ready.sem, 1)
                    if norm == 1:
                        pool.tensor_tensor(x0_tok, x0_tok, x_tok, ALU.add).then_inc(doubled.sem, 1)
                for g in range(G):
                    pool.wait_ge(ss2_ready.sem, ss2_ready.at(s, g + 1))
                    pool.tensor_tensor(rstd2[:, :], ss2[:, :], minus_half[:, :], ALU.pow).then_inc(rstd2_ready.sem, 1)

            with pool.Fori(0, T) as t:
                for i in range(4):
                    if i == 0:
                        pool.wait_ge(drive_ready.sem, drive_ready.at(t, C))
                    pool.wait_ge(p_ready.sem, p_ready.at(t, i + 1))
                    pool.tensor_tensor(net["m"], net["drive"], p_of[i], ALU.subtract).then_inc(m_ready.sem, 1)
                    if i == 3:
                        pool.wait_ge(q_ready.sem, q_ready.at(t, 2 * i + 2))
                        pool.tensor_tensor(net["f"], q_of[3], q_of[0], ALU.subtract).then_inc(f_ready.sem, 1)
                        pool.wait_ge(e_ready.sem, e_ready.at(t, 1))
                        pool.wait_ge(f_ready.sem, f_ready.at(t, 1))
                        pool.tensor_tensor(net["g"], net["f"], net["e"], ALU.add).then_inc(g_ready.sem, 1)
                        pool.tensor_tensor(net["pf"], p_of[3], p_of[0], ALU.subtract).then_inc(pf_ready.sem, 1)
                        pool.wait_ge(pe_ready.sem, pe_ready.at(t, 1))
                        pool.wait_ge(pf_ready.sem, pf_ready.at(t, 1))
                        pool.tensor_tensor(net["pg"], net["pf"], net["pe"], ALU.add).then_inc(pg_ready.sem, 1)
                        pool.wait_ge(pg_ready.sem, pg_ready.at(t, 1))
                    pool.wait_ge(px_ready.sem, px_ready.at(t, i + 1))
                    pool.tensor_tensor(net["py"], net["px"], p_of[0] if i < 3 else net["pg"], ALU.add).then_inc(py_ready.sem, 1)
                pool.wait_ge(q_ready.sem, q_ready.at(t, 10))
                xt = x_feat[:, :, bass.ds(t, 1), :].rearrange("p c t b -> p c (t b)")
                pool.tensor_tensor(net["outT"], xt, q_of[0], ALU.add).then_inc(outT_ready.sem, 1)

        def set_fill(pe, name):
            at = order.index(name)
            if at >= 8:
                before = order[at - 8]
                pe.wait_ge({"act": set_act, "dve": set_dve}[set_who[before]].sem, set_emptied[before])
            return set_bank[name]

        @block.tensor
        def _(pe):
            mm = pe.matmul
            pe.wait_ge(consts.sem, 2)
            pe.wait_ge(cond_in.sem, 16)
            pe.wait_ge(rows_in.sem, 16 * 12)
            ps = set_fill(pe, "turn")
            for c in range(C):
                pe.transpose(ps[:, c * P:(c + 1) * P], cond[:, c * P:(c + 1) * P], ident[:, :])
            pe.transpose(ps[:, 256:256 + N_ROWS], rows[0:N_ROWS, :], ident[0:N_ROWS, 0:N_ROWS]).then_inc(set_filled.sem, 1)
            pe.wait_ge(coup_in.sem, 16)
            ps = set_fill(pe, "coup")
            for c in range(C):
                for j in range(C):
                    last = pe.transpose(ps[:, c * D + j * P:c * D + (j + 1) * P], coup_rows[:, j, c * P:(c + 1) * P], ident[:, :])
            last.then_inc(set_filled.sem, 1)
            for i in range(X_PAIRS):
                if i % 4 == 0:
                    pe.wait_ge(x_in[i // 4].sem, 16)
                ps = set_fill(pe, f"x{i}")
                for tt in range(2):
                    for c in range(C):
                        last = pe.transpose(ps[:, (c * 2 + tt) * P:(c * 2 + tt + 1) * P], x_rows[:, 2 * i + tt, c * P:(c + 1) * P], ident[:, :])
                last.then_inc(set_filled.sem, 1)
            pe.wait_ge(ada_in.sem, 16)
            pe.wait_ge(emb_in.sem, 16)
            for j in range(16):
                if j % 4 == 0:
                    ps = set_fill(pe, f"mod{j // 4}")
                for c in range(C):
                    w = ada_w[:, c, j * P:(j + 1) * P] if j < 12 else w_emb[:, c, (j - 12) * P:(j - 11) * P]
                    last = mm(ps[:, (j % 4) * B:(j % 4 + 1) * B], w, condT[:, c, :], start=(c == 0), stop=(c == C - 1))
                if j % 4 == 3:
                    last.then_inc(set_filled.sem, 1)

            pe.wait_ge(gru_in.sem, 32)
            pe.wait_ge(set_act.sem, SET_ACT)
            pe.wait_ge(set_dve.sem, SET_DVE)

            def gru_input(par, t):
                xt = lambda c: x_feat[:, c, bass.ds(t, 1), :].rearrange("p t b -> p (t b)") if not isinstance(t, int) else x_feat[:, c, t, :]
                for k, j0 in ((0, 0), (1, 2), (2, 4)):
                    for j in range(2):
                        for c in range(C):
                            last = mm(bank[4 * par + k][:, j * B:(j + 1) * B], w_ih[:, c, (j0 + j) * P:(j0 + j + 1) * P], xt(c),
                                      start=(j == 0 and c == 0), stop=(k == 2 and j == 1 and c == 1), skip_group_check=True)
                return last

            def gru_hidden(par, t):
                pe.wait_ge(h_ready.sem, h_ready.at(t, 2))
                for k, j0 in ((0, 0), (3, 4), (1, 2)):
                    for c in range(C):
                        for j in range(2):
                            last = mm(bank[4 * par + k][:, j * B:(j + 1) * B], w_hh[:, c, (j0 + j) * P:(j0 + j + 1) * P], h_buf[:, par, c, :],
                                      start=(k == 3 and j == 0 and c == 0), stop=(j == 1 and c == 1), skip_group_check=True)
                    last.then_inc(gates_ready.sem, 1)

            gru_input(0, 0)
            with pe.Fori(0, T // 2 - 1) as i:
                gru_hidden(0, i * 2)
                gru_input(1, i * 2 + 1)
                gru_hidden(1, i * 2 + 1)
                gru_input(0, i * 2 + 2)
            gru_hidden(0, T - 2)
            gru_input(1, T - 1)
            gru_hidden(1, T - 1)

            pe.wait_ge(lot_w_in.sem, 16 * 5)
            pe.wait_ge(set_dve.sem, SET_DVE + 1)
            with pe.Fori(0, LOTS) as s:
                at = [0]

                def fill(name, i):
                    k = at[0]
                    assert FILLS[k][:2] == (name, i), (FILLS[k], name, i)
                    if k >= WORK_BANKS:
                        who, n = EMPTIES[FILLS[k - WORK_BANKS][:2]]
                        pe.wait_ge(emptied[who].sem, emptied[who].at(s, n))
                    at[0] += 1
                    return work_bank[k % WORK_BANKS]

                def has_emptied(name, i):
                    who, n = EMPTIES[(name, i)]
                    pe.wait_ge(emptied[who].sem, emptied[who].at(s, n))

                def to_tokens(name, src):
                    for j in range(2):
                        ps = fill(name, j)
                        for gg in range(2):
                            for c in range(C):
                                last = pe.transpose(ps[:, gg * D + c * P:gg * D + (c + 1) * P], src[:, c, (2 * j + gg) * P:(2 * j + gg + 1) * P], ident[:, :])
                        last.then_inc(filled.sem, 1)

                def to_features(name, src):
                    for c in range(C):
                        ps = fill(name, c)
                        for g in range(G):
                            last = pe.transpose(ps[:, g * P:(g + 1) * P], src[:, g, c * P:(c + 1) * P], ident[:, :])
                        last.then_inc(filled.sem, 1)

                def project(name, i, w):
                    ps = fill(name, i)
                    for c in range(C):
                        last = mm(ps[:, :], w[:, c, :], xm[:, c, :], start=(c == 0), stop=(c == C - 1))
                    last.then_inc(filled.sem, 1)

                def q_and_k(q):
                    for h in range(QUAD * q, QUAD * q + QUAD):
                        project("q", h, w_qkv[:, :, h * DH1:(h + 1) * DH1])
                        project("k", h, w_qkv[:, :, INNER + h * DH1:INNER + (h + 1) * DH1])

                def values(q):
                    for g in range(G):
                        ps = fill("v", G * q + g)
                        for c in range(C):
                            last = mm(ps[:, :], xm[:, c, g * P:(g + 1) * P], w_qkv[:, c, 2 * INNER + q * 512:2 * INNER + (q + 1) * 512],
                                      start=(c == 0), stop=(c == C - 1))
                        last.then_inc(filled.sem, 1)

                pe.wait_ge(staged.sem, staged.at(s, C))
                to_tokens("xin", x_lot)
                pe.wait_ge(xn_ready.sem, xn_ready.at(s, G))
                to_features("m1", xn)
                pe.wait_ge(mod_ready.sem, mod_ready.at(s, C))
                q_and_k(0)
                values(0)
                for q in range(QUADS):
                    has_emptied("k", QUAD * q + QUAD - 1)
                    ps = s_bank[q % 2]
                    for g in range(G):
                        for h in range(QUAD):
                            for b in range(GB):
                                tok = slice(g * P + b * T, g * P + (b + 1) * T)
                                at_col = (g * QUAD + h) * T
                                last = mm(ps[b * T:(b + 1) * T, at_col:at_col + T], qT[:, h, tok], kT[:, h, tok], start=True, stop=True)
                    last.then_inc(scores_ready.sem, 1)
                    if q < QUADS - 1:
                        q_and_k(q + 1)
                    pe.wait_ge(probT_ready.sem, probT_ready.at(s, q + 1))
                    has_emptied("v", G * q + G - 1)
                    for h in range(QUAD):
                        ps = fill("o", QUAD * q + h)
                        for g in range(G):
                            last = mm(ps[:, g * P:(g + 1) * P], v_tok[:, g, h * DH1:(h + 1) * DH1], probT[:, g * QUAD + h, :], start=True, stop=True)
                        last.then_inc(filled.sem, 1)
                    if q < QUADS - 1:
                        values(q + 1)
                    for h in range(QUAD):
                        has_emptied("o", QUAD * q + h)
                        for c in range(C):
                            last = mm(y_bank[c][:, :], w_out[:, QUAD * q + h, c * P:(c + 1) * P], oT[:, h, :],
                                      start=(q == 0 and h == 0), stop=(q == QUADS - 1 and h == QUAD - 1))
                    last.then_inc((oT_used if q < QUADS - 1 else y_ready).sem, 1)
                pe.wait_ge(yT_ready.sem, yT_ready.at(s, C))
                to_tokens("y", yT)
                pe.wait_ge(xn_ready.sem, xn_ready.at(s, 2 * G))
                to_features("m2", xn)
                pe.wait_ge(mod_ready.sem, mod_ready.at(s, 2 * C))
                for m in range(MLP // P):
                    project("h", m, w_f1[:, :, m * P:(m + 1) * P])
                for m in range(MLP // P):
                    has_emptied("h", m)
                    for c in range(C):
                        last = mm(y_bank[c][:, :], w_f2[:, m, c * P:(c + 1) * P], hT[:, m, :], start=(m == 0), stop=(m == MLP // P - 1))
                last.then_inc(y_ready.sem, 1)
                pe.wait_ge(yT_ready.sem, yT_ready.at(s, 2 * C))
                to_tokens("f", yT)
                pe.wait_ge(xn_ready.sem, xn_ready.at(s, 3 * G))
                to_features("m3", xn)
                pe.wait_ge(mod_ready.sem, mod_ready.at(s, 3 * C))
                for g in range(G):
                    ps = fill("qk2", g)
                    for c in range(C):
                        last = mm(ps[:, :], xm[:, c, g * P:(g + 1) * P], w_qkv2[:, c, 0:2 * D], start=(c == 0), stop=(c == C - 1))
                    last.then_inc(filled.sem, 1)

                def values2(g):
                    ps = fill("v2", g)
                    for c in range(C):
                        last = mm(ps[:, 0:D], xm[:, c, g * P:(g + 1) * P], w_qkv2[:, c, 2 * D:3 * D], start=(c == 0), stop=(c == C - 1))
                    last.then_inc(filled.sem, 1)

                def turn2(g):
                    pe.wait_ge(qkn_ready.sem, qkn_ready.at(s, g + 1))
                    ps = fill("t2", g)
                    for k in range(4):
                        last = pe.transpose(ps[:, k * P:(k + 1) * P], qk_n[:, g % 2, k * P:(k + 1) * P], ident[:, :])
                    last.then_inc(filled.sem, 1)

                values2(0)
                turn2(0)
                for g in range(G):
                    has_emptied("t2", g)
                    ps = s_bank[g % 2]
                    for c in range(C):
                        for b in range(GB):
                            last = mm(ps[b * T:(b + 1) * T, c * D:(c + 1) * D], q2T[:, g % 2, c, b * T:(b + 1) * T],
                                      k_wide[:, c, b, :, :].rearrange("p h t -> p (h t)"), start=True, stop=True)
                    last.then_inc(scores_ready.sem, 1)
                    if g < G - 1:
                        turn2(g + 1)
                    pe.wait_ge(probT_ready.sem, probT_ready.at(s, QUADS + g + 1))
                    has_emptied("v2", g)
                    ps = fill("o2", g)
                    for c in range(C):
                        for h in range(HC):
                            last = mm(ps[:, c * P:(c + 1) * P], v_wide[:, c * HC + h, :], probT[:, c * HC + h, :],
                                      start=(h == 0), stop=(h == HC - 1))
                    last.then_inc(filled.sem, 1)
                    if g < G - 1:
                        values2(g + 1)
                    has_emptied("o2", g)
                    ps = fill("w2", g)
                    for c in range(C):
                        last = mm(ps[:, 0:D], o2T[:, c, :], w_out2[:, c, :], start=(c == 0), stop=(c == C - 1))
                    last.then_inc(filled.sem, 1)
                has_emptied("w2", G - 1)
                to_features("xo", x_tok)
                assert at[0] == len(FILLS)

            pe.wait_ge(emptied["act"].sem, emptied["act"].at(LOTS, 0))
            def turn_out(t):
                pe.wait_ge(outT_ready.sem, outT_ready.at(t, 1))
                for c in range(C):
                    last = pe.transpose(bank[4][:, c * P:(c + 1) * P], net["outT"][:, c, :], ident[:, :])
                last.then_inc(turned.sem, 1)

            def net_step(t, before):
                for i in range(4):
                    if i == 1 and before is not None:
                        turn_out(before)
                    pair = bank[2 * (i % 2):2 * (i % 2) + 2]
                    for k in range(C):
                        pe.wait_ge(tanh_ready.sem, tanh_ready.at(t, 2 * i + k + 1))
                        for j in range(C):
                            mm(pair[j][:, 0:B], coupT[:, k, j * P:(j + 1) * P], net["tanh"][:, k, :], start=(k == 0), stop=False, skip_group_check=True)
                    pe.wait_ge(m_ready.sem, m_ready.at(t, i + 1))
                    for j in range(C):
                        mm(pair[j][:, 0:B], ident[:, :], net["m"][:, j, :], start=False, stop=True, skip_group_check=True).then_inc(coupled.sem, 1)

            net_step(0, None)
            with pe.Fori(1, T) as t:
                net_step(t, t - 1)
            turn_out(T - 1)

        @block.scalar
        def _(act):
            def filled_set(name):
                act.wait_ge(set_filled.sem, set_ord[name])
                return set_bank[name]

            for i in range(1, X_PAIRS, 2):
                ps = filled_set(f"x{i}")
                act.activation(x_feat[:, :, 2 * i:2 * i + 2, :], ps[:, :].rearrange("p (c t b) -> p c t b", c=C, t=2), ACT.Copy).then_inc(set_act.sem, 1)

            act.wait_ge(set_dve.sem, SET_DVE)
            with act.Fori(0, T // 2) as i:
                for par in range(2):
                    t = i * 2 + par
                    act.wait_ge(gates_ready.sem, gates_ready.at(t, 1))
                    for c in range(C):
                        act.activation(gate_r[:, c, :], bank[4 * par][:, c * B:(c + 1) * B], ACT.Sigmoid, bias=bsum[:, c:c + 1]).then_inc(r_ready.sem, 1)
                    act.wait_ge(gates_ready.sem, gates_ready.at(t, 3))
                    for c in range(C):
                        act.activation(gate_z[:, c, :], bank[4 * par + 1][:, c * B:(c + 1) * B], ACT.Sigmoid, bias=bsum[:, 2 + c:3 + c]).then_inc(z_ready.sem, 1)
                    for c in range(C):
                        act.wait_ge(pre_ready.sem, pre_ready.at(t, c + 1))
                        act.activation(cand[:, c, :], pre_n[:, c, :], ACT.Tanh).then_inc(n_ready.sem, 1)
                        if c == 0:
                            act.wait_ge(z_ready.sem, z_ready.at(t, 2))
                            act.activation(one_z, gate_z, ACT.Copy, scale=-1.0, bias=1.0).then_inc(one_z_ready.sem, 1)

            act.wait_ge(x_added.sem, T + 2)
            with act.Fori(0, LOTS) as s:
                def is_filled(name, i):
                    act.wait_ge(filled.sem, filled.at(s, ORDINAL[(name, i)]))
                    return work_bank[(ORDINAL[(name, i)] - 1) % WORK_BANKS]

                def empty(name, i, dst, src, func, **kw):
                    act.activation(dst, src, func, **kw).then_inc(emptied["act"].sem, 1)

                for c in range(C):
                    act.activation(x_lot[:, c, :].rearrange("p (b t) -> p b t", t=T),
                                   x_feat[:, c, :, bass.ds(s * LOT_B, LOT_B)].rearrange("p t b -> p b t"), ACT.Copy).then_inc(staged.sem, 1)
                for j in range(2):
                    ps = is_filled("xin", j)
                    empty("xin", j, x0_tok[:, 2 * j:2 * j + 2, :].rearrange("p g d -> p (g d)"), ps[:, :], ACT.Copy)

                def q_and_k(q):
                    if q > 0:
                        act.wait_ge(scores_ready.sem, scores_ready.at(s, q))
                    for h in range(QUAD * q, QUAD * q + QUAD):
                        for name, dst, k in (("q", qT, h), ("k", kT, H + h)):
                            ps = is_filled(name, h)
                            empty(name, h, dst[:, h % QUAD, :], ps[:, :], ACT.Identity, bias=column("qkv_b", k))

                def exps(k):
                    act.wait_ge(shifted.sem, shifted.at(s, k + 1))
                    act.activation(prob, prob, ACT.Exp, scale=float(DH1 if k < QUADS else DH2) ** -0.5).then_inc(exp_ready.sem, 1)

                q_and_k(0)
                for q in range(QUADS):
                    exps(q)
                    if q < QUADS - 1:
                        q_and_k(q + 1)
                    if q > 0:
                        act.wait_ge(oT_used.sem, oT_used.at(s, q))
                    for h in range(QUAD * q, QUAD * q + QUAD):
                        ps = is_filled("o", h)
                        empty("o", h, oT[:, h % QUAD, :], ps[:, :], ACT.Identity, bias=column("qkv_b", 2 * H + h))
                for m in range(MLP // P):
                    ps = is_filled("h", m)
                    empty("h", m, hT[:, m, :], ps[:, :], ACT.Gelu, bias=column("ffn_b1", m))
                for g in range(G):
                    ps = is_filled("qk2", g)
                    empty("qk2", g, qk2[:, g, :], ps[:, :], ACT.Copy)

                def squares(g):
                    if g == 0:
                        act.wait_ge(emptied["act"].sem, emptied["act"].at(s, EMPTIES[("qk2", G - 1)][1]))
                    if g > 0:
                        act.wait_ge(ss2_ready.sem, ss2_ready.at(s, g))
                    act.activation(qk_sq, qk2[:, g, :], ACT.Square).then_inc(sq_ready.sem, 1)

                def values2(g):
                    ps = is_filled("v2", g)
                    for c in range(C):
                        ins = act.activation(v_diag[c], ps[:, c * P:(c + 1) * P].rearrange("p (h d) -> p h d", d=DH2), ACT.Copy)
                    ins.then_inc(emptied["act"].sem, 1)

                squares(0)
                values2(0)
                for g in range(G):
                    if g < G - 1:
                        squares(g + 1)
                    exps(QUADS + g)
                    ps = is_filled("o2", g)
                    empty("o2", g, o2T[:, :, :].rearrange("p c n -> p (c n)"), ps[:, 0:D], ACT.Copy)
                    if g < G - 1:
                        values2(g + 1)
                for c in range(C):
                    ps = is_filled("xo", c)
                    act.activation(tick[:, 1 + c:2 + c], minus_half[:, 0:1], ACT.Copy)
                    empty("xo", c, x_feat[:, c, :, bass.ds(s * LOT_B, LOT_B)], ps[:, :].rearrange("p (b t) -> p t b", t=T), ACT.Copy)

            act.wait_ge(q_ready.sem, 2)
            act.wait_ge(emptied["act"].sem, emptied["act"].at(LOTS, 0))
            def send_out(t):
                act.wait_ge(turned.sem, turned.at(t, 1))
                act.wait_ge(rows_free.sem, rows_free.at(t, 1))
                act.activation(out_rows, bank[4][:, 0:D], ACT.Copy).then_inc(out_ready.sem, 1)

            def net_step(t, before):
                for i in range(4):
                    step = (DT / 2, DT / 2, DT, DT / 2)[i]
                    for c in range(C):
                        act.wait_ge(q_ready.sem, q_ready.at(t, 2 * i + c + 1))
                        act.activation(net["tanh"][:, c, :], q_of[i][:, c, :], ACT.Tanh).then_inc(tanh_ready.sem, 1)
                    if i == 0:
                        for c in range(C):
                            act.activation(net["drive"][:, c, :], x_feat[:, c, bass.ds(t, 1), :].rearrange("p t b -> p (t b)"), ACT.Identity,
                                           bias=column("bias", c)).then_inc(drive_ready.sem, 1)
                    act.activation(net["sq"], q_of[i], ACT.Square).then_inc(sq_net.sem, 1)
                    act.wait_ge(sq_net.sem, sq_net.at(t, i + 1))
                    act.activation(net["u"], net["sq"], ACT.Copy, scale=-1 / 3, bias=1.0).then_inc(u_ready.sem, 1)
                    act.wait_ge(p_ready.sem, p_ready.at(t, i + 1))
                    act.activation(net["px"], q_of[i], ACT.Copy, scale=step * EPSILON, bias=step * EPSILON * ALPHA).then_inc(px_ready.sem, 1)
                    if i == 1 and before is not None:
                        send_out(before)

            net_step(0, None)
            with act.Fori(1, T) as t:
                net_step(t, t - 1)
            send_out(T - 1)

        @block.vector
        def _(dve):
            chain = Chain(dve, set_chain.sem)
            link = chain.link

            def filled_set(name):
                dve.wait_ge(set_filled.sem, set_ord[name])
                return set_bank[name]

            ps = filled_set("turn")
            dve.wait_ge(consts.sem, 2)
            link(dve.tensor_copy(condT[:, :, :].rearrange("p c b -> p (c b)"), ps[:, 0:C * B]))
            dve.tensor_copy(col[:, :], ps[:, 256:256 + N_ROWS]).then_inc(set_dve.sem, 1)
            dve.wait_ge(set_dve.sem, 1)
            at_ih, at_hh = ROWS["b_ih"][0], ROWS["b_hh"][0]
            link(dve.tensor_tensor(bsum[:, :], col[:, at_ih:at_ih + 4], col[:, at_hh:at_hh + 4], ALU.add))
            link(dve.tensor_scalar(k_mask[:, :], k_mask[:, :], column("g_k"), None, ALU.mult))
            ps = filled_set("coup")
            dve.tensor_copy(coupT[:, :, :].rearrange("p c n -> p (c n)"), ps[:, :]).then_inc(set_dve.sem, 1)
            for i in range(0, X_PAIRS, 2):
                ps = filled_set(f"x{i}")
                dve.tensor_copy(x_feat[:, :, 2 * i:2 * i + 2, :], ps[:, :].rearrange("p (c t b) -> p c t b", c=C, t=2)).then_inc(set_dve.sem, 1)
            for j in range(16):
                if j % 4 == 0:
                    ps = filled_set(f"mod{j // 4}")
                src = ps[:, (j % 4) * B:(j % 4 + 1) * B]
                bias = column("ada_b", j) if j < 12 else column("b_emb", j - 12)
                if j // 2 * 2 in (SCALE1, SCALE2, SCALE3):
                    ins = dve.tensor_scalar(mod[:, j, :], src, bias, 1.0, ALU.add, ALU.add)
                else:
                    ins = dve.tensor_scalar(mod[:, j, :], src, bias, None, ALU.add)
                if j % 4 == 3:
                    ins.then_inc(set_dve.sem, 1)
                else:
                    link(ins)
            for c in range(C):
                link(dve.tensor_scalar(mod[:, SCALE3 + c, :], mod[:, SCALE3 + c, :], column("g_norm", c), None, ALU.mult))
            dve.wait_ge(set_act.sem, SET_ACT)
            for c in range(C):
                dve.tensor_copy(h_buf[:, 0, c, :], condT[:, c, :]).then_inc(h_ready.sem, 1)
            dve.wait_ge(lot_w2_in.sem, 16)
            for c in range(C):
                ins = dve.tensor_tensor(w_out2[:, c, c * P:(c + 1) * P], w_out2[:, c, c * P:(c + 1) * P], ident[:, :], ALU.add)
                if c == C - 1:
                    ins.then_inc(set_dve.sem, 1)
                else:
                    link(ins)

            with dve.Fori(0, T // 2) as i:
                for par in range(2):
                    t = i * 2 + par
                    dve.wait_ge(gates_ready.sem, gates_ready.at(t, 2))
                    for c in range(C):
                        dve.wait_ge(r_ready.sem, r_ready.at(t, c + 1))
                        dve.scalar_tensor_tensor(pre_n[:, c, :], bank[4 * par + 3][:, c * B:(c + 1) * B], column("b_hh", 4 + c), gate_r[:, c, :],
                                                 ALU.add, ALU.mult).then_inc(r_used.sem, 1)
                    for c in range(C):
                        dve.wait_ge(r_used.sem, r_used.at(t, c + 1))
                        dve.scalar_tensor_tensor(pre_n[:, c, :], bank[4 * par + 2][:, c * B:(c + 1) * B], column("b_ih", 4 + c), pre_n[:, c, :],
                                                 ALU.add, ALU.add).then_inc(pre_ready.sem, 1)
                    dve.wait_ge(z_ready.sem, z_ready.at(t, 2))
                    dve.tensor_tensor(z_h, gate_z, h_buf[:, par], ALU.mult).then_inc(z_h_ready.sem, 1)
                    dve.wait_ge(one_z_ready.sem, one_z_ready.at(t, 1))
                    for c in range(C):
                        dve.wait_ge(n_ready.sem, n_ready.at(t, c + 1))
                        dve.tensor_tensor(cand[:, c, :], cand[:, c, :], one_z[:, c, :], ALU.mult).then_inc(prod_ready.sem, 1)
                    dve.wait_ge(x_added.sem, x_added.at(t, 1))
                    for c in range(C):
                        dve.wait_ge(prod_ready.sem, prod_ready.at(t, c + 1))
                        dve.tensor_tensor(h_buf[:, 1 - par, c, :], cand[:, c, :], z_h[:, c, :], ALU.add).then_inc(h_ready.sem, 1)

            dve.wait_ge(zeroed.sem, 2)
            with dve.Fori(0, LOTS) as s:
                chain = Chain(dve, dve_chain.sem)
                chain.start(s * DVE_LINKS)
                link = chain.link

                def is_filled(name, i):
                    dve.wait_ge(filled.sem, filled.at(s, ORDINAL[(name, i)]))
                    return work_bank[(ORDINAL[(name, i)] - 1) % WORK_BANKS]

                def of_lot(k, c):
                    return mod[:, k + c, bass.ds(s * LOT_B, LOT_B)].rearrange("p (b o) -> p b o", o=1).to_broadcast([P, LOT_B, T])

                def tokens(ap):
                    return ap.rearrange("p (b t) -> p b t", t=T)

                def normalise(norm, src, about_mean):
                    for g in range(G):
                        ins = dve.bn_stats(stats[:, g, :], src[:, g, :])
                    link(ins)
                    dve.memset(tick[:, 0:1], 0.0)
                    for g in range(G):
                        ins = dve.bn_aggr(mean_var[:, g, :], stats[:, g, :])
                    link(ins)
                    mean, var = mean_var[:, :, 0], mean_var[:, :, 1]
                    if about_mean:
                        dve.tensor_scalar(spread[:, :], var, EPS, None, ALU.add).then_inc(spread_ready.sem, 1)
                    else:
                        link(dve.tensor_tensor(spread[:, :], mean, mean, ALU.mult))
                        dve.scalar_tensor_tensor(spread[:, :], spread[:, :], EPS, var, ALU.add, ALU.add).then_inc(spread_ready.sem, 1)
                    dve.wait_ge(rstd_ready.sem, rstd_ready.at(s, norm + 1))
                    for g in range(G):
                        if about_mean:
                            ins = dve.tensor_scalar(xn[:, g, :], src[:, g, :], mean_var[:, g, 0:1], rstd[:, g:g + 1], ALU.subtract, ALU.mult)
                        else:
                            ins = dve.tensor_scalar(xn[:, g, :], src[:, g, :], rstd[:, g:g + 1], None, ALU.mult)
                        ins.then_inc(xn_ready.sem, 1)

                def modulate(name, scale, shift):
                    for c in range(C):
                        ps = is_filled(name, c)
                        dve.tensor_tensor(tokens(xm[:, c, :]), tokens(ps[:, :]), of_lot(scale, c), ALU.mult).then_inc(emptied["dve"].sem, 1)
                        dve.wait_ge(emptied["dve"].sem, emptied["dve"].at(s, EMPTIES[(name, c)][1]))
                        dve.tensor_tensor(tokens(xm[:, c, :]), tokens(xm[:, c, :]), of_lot(shift, c), ALU.add).then_inc(mod_ready.sem, 1)

                def heads(ap):
                    return ap.rearrange("p (h t) -> p h t", t=T)

                def per_head(ap):
                    return ap.rearrange("p (h o) -> p h o", o=1).to_broadcast([P, 16, T])

                def softmax(k):
                    ps = s_bank[k % 2]
                    dve.wait_ge(scores_ready.sem, scores_ready.at(s, k + 1))
                    link(dve.tensor_reduce(soft_max[:, :], heads(ps[:, :]), AX_X, ALU.max))
                    dve.tensor_tensor(heads(prob), heads(ps[:, :]), per_head(soft_max[:, :]), ALU.subtract).then_inc(shifted.sem, 1)
                    dve.wait_ge(exp_ready.sem, exp_ready.at(s, k + 1))
                    link(dve.tensor_reduce(soft_sum[:, :], heads(prob), AX_X, ALU.add))
                    link(dve.reciprocal(soft_inv[:, :], soft_sum[:, :]))
                    link(dve.tensor_tensor(heads(prob), heads(prob), per_head(soft_inv[:, :]), ALU.mult))
                    for b in range(GB):
                        rows_b = slice(b * T, (b + 1) * T)
                        ins = dve.transpose(probT[rows_b, :, b * T:(b + 1) * T], heads(prob)[rows_b, :, :])
                    ins.then_inc(probT_ready.sem, 1)

                def values(q):
                    for g in range(G):
                        ps = is_filled("v", G * q + g)
                        dve.tensor_copy(v_tok[:, g, :], ps[:, :]).then_inc(emptied["dve"].sem, 1)

                def gate(which, bias, k):
                    dve.wait_ge(y_ready.sem, y_ready.at(s, which + 1))
                    for c in range(C):
                        dve.scalar_tensor_tensor(tokens(yT[:, c, :]), tokens(y_bank[c][:, :]), column(bias, c), of_lot(k, c),
                                                 ALU.add, ALU.mult).then_inc(yT_ready.sem, 1)

                def add_tokens(name, other):
                    for j in range(2):
                        ps = is_filled(name, j)
                        pair = slice(2 * j, 2 * j + 2)
                        dve.tensor_tensor(x_tok[:, pair, :].rearrange("p g d -> p (g d)"), ps[:, :],
                                          other[:, pair, :].rearrange("p g d -> p (g d)"), ALU.add).then_inc(emptied["dve"].sem, 1)
                    dve.wait_ge(emptied["dve"].sem, emptied["dve"].at(s, EMPTIES[(name, 1)][1]))

                who, n = EMPTIES[("xin", 1)]
                dve.wait_ge(emptied["act"].sem, emptied["act"].at(s, n))
                normalise(0, x0_tok, True)
                modulate("m1", SCALE1, SHIFT1)
                values(0)
                for q in range(QUADS):
                    softmax(q)
                    if q < QUADS - 1:
                        dve.wait_ge(filled.sem, filled.at(s, ORDINAL[("o", QUAD * q + QUAD - 1)]))
                        values(q + 1)
                gate(0, "out_b", GATE1)
                add_tokens("y", x0_tok)
                normalise(1, x_tok, True)
                modulate("m2", SCALE2, SHIFT2)
                gate(1, "ffn_b2", GATE2)
                dve.wait_ge(doubled.sem, doubled.at(s, 1))
                add_tokens("f", x0_tok)
                normalise(2, x_tok, False)
                modulate("m3", SCALE3, SHIFT3)

                def norm_heads(g):
                    dve.wait_ge(sq_ready.sem, sq_ready.at(s, g + 1))
                    link(dve.tensor_reduce(ss2[:, :], qk_sq.rearrange("p (h d) -> p h d", d=DH2), AX_X, ALU.add))
                    dve.tensor_scalar(ss2[:, :], ss2[:, :], 1.0 / DH2, EPS, ALU.mult, ALU.add).then_inc(ss2_ready.sem, 1)
                    dve.wait_ge(rstd2_ready.sem, rstd2_ready.at(s, g + 1))
                    dve.tensor_tensor(qk_n[:, g % 2, :].rearrange("p (h d) -> p h d", d=DH2), qk2[:, g, :].rearrange("p (h d) -> p h d", d=DH2),
                                      rstd2[:, :].rearrange("p (h o) -> p h o", o=1).to_broadcast([P, 2 * H, DH2]), ALU.mult).then_inc(qkn_ready.sem, 1)

                def widen(g):
                    if g > 0:
                        dve.wait_ge(scores_ready.sem, scores_ready.at(s, QUADS + g))
                    ps = is_filled("t2", g)
                    dve.tensor_scalar(q2T[:, g % 2, :, :].rearrange("p c n -> p (c n)"), ps[:, 0:D], column("g_q"), None, ALU.mult)
                    for c in range(C):
                        for b in range(GB):
                            src = ps[:, D + c * P + b * T:D + c * P + (b + 1) * T].rearrange("p (o t) -> p o t", o=1).to_broadcast([P, HC, T])
                            mask = k_mask[:, :].rearrange("p (h o) -> p h o", o=1).to_broadcast([P, HC, T])
                            ins = dve.tensor_tensor(k_wide[:, c, b, :, :], src, mask, ALU.mult)
                    ins.then_inc(emptied["dve"].sem, 1)

                norm_heads(0)
                widen(0)
                for g in range(G):
                    if g < G - 1:
                        norm_heads(g + 1)
                    softmax(QUADS + g)
                    if g < G - 1:
                        widen(g + 1)
                    ps = is_filled("w2", g)
                    dve.tensor_tensor(x_tok[:, g, :], ps[:, 0:D], x_tok[:, g, :], ALU.add).then_inc(emptied["dve"].sem, 1)
                assert chain.k == DVE_LINKS, chain.k

            dve.wait_ge(emptied["act"].sem, emptied["act"].at(LOTS, 0))
            for c in range(C):
                dve.tensor_copy(q_of[0][:, c, :], condT[:, c, :]).then_inc(q_ready.sem, 1)
            dve.tensor_copy(p_of[0], condT[:, :, :]).then_inc(p_ready.sem, 1)
            with dve.Fori(0, T) as t:
                for i in range(4):
                    step = (DT / 2, DT / 2, DT, DT / 2)[i]
                    pair = bank[2 * (i % 2):2 * (i % 2) + 2]
                    if i == 2:
                        dve.wait_ge(q_ready.sem, q_ready.at(t, 6))
                        dve.scalar_tensor_tensor(net["e"], q_of[2], 2.0, q_of[1], ALU.mult, ALU.add).then_inc(e_ready.sem, 1)
                    if i == 3:
                        dve.wait_ge(p_ready.sem, p_ready.at(t, 4))
                        dve.scalar_tensor_tensor(net["pe"], p_of[2], 2.0, p_of[1], ALU.mult, ALU.add).then_inc(pe_ready.sem, 1)
                    dve.wait_ge(u_ready.sem, u_ready.at(t, i + 1))
                    dve.tensor_tensor(net["v"], net["u"], q_of[i], ALU.mult).then_inc(v_ready.sem, 1)
                    dve.wait_ge(v_ready.sem, v_ready.at(t, i + 1))
                    if i == 3:
                        dve.wait_ge(g_ready.sem, g_ready.at(t, 1))
                    dve.scalar_tensor_tensor(net["base"], net["v"], step, q_of[0] if i < 3 else net["g"], ALU.mult, ALU.add).then_inc(base_ready.sem, 1)
                    dve.wait_ge(base_ready.sem, base_ready.at(t, i + 1))
                    for c in range(C):
                        dve.wait_ge(coupled.sem, coupled.at(t, 2 * i + c + 1))
                        dst = q_of[i + 1] if i < 3 else net["raw"]
                        dve.scalar_tensor_tensor(dst[:, c, :], pair[c][:, 0:B], step, net["base"][:, c, :], ALU.mult, ALU.add)\
                           .then_inc(q_ready.sem if i < 3 else clip_step.sem, 1)
                    if i == 3:
                        for c in range(C):
                            dve.wait_ge(clip_step.sem, clip_step.at(t, c + 1))
                            dve.tensor_scalar(net["raw"][:, c, :], net["raw"][:, c, :], 1 / 3, CLAMP, ALU.mult, ALU.min).then_inc(clip_step.sem, 1)
                        for c in range(C):
                            dve.wait_ge(clip_step.sem, clip_step.at(t, c + 3))
                            dve.tensor_scalar(q_of[0][:, c, :], net["raw"][:, c, :], -CLAMP, None, ALU.max).then_inc(q_ready.sem, 1)
                    dve.wait_ge(py_ready.sem, py_ready.at(t, i + 1))
                    dst = p_of[i + 1] if i < 3 else net["p_raw"]
                    dve.scalar_tensor_tensor(dst, p_of[i], -step * EPSILON * BETA, net["py"], ALU.mult, ALU.add)\
                       .then_inc(p_ready.sem if i < 3 else clip_step.sem, 1)
                dve.wait_ge(clip_step.sem, clip_step.at(t, 5))
                dve.tensor_scalar(net["p_raw"], net["p_raw"], 1 / 3, CLAMP, ALU.mult, ALU.min).then_inc(clip_step.sem, 1)
                dve.wait_ge(clip_step.sem, clip_step.at(t, 6))
                dve.tensor_scalar(p_of[0], net["p_raw"], -CLAMP, None, ALU.max).then_inc(p_ready.sem, 1)


_INS = ["x", "cond_2048", "L0_cond_W_ih", "L0_cond_W_hh", "L0_cond_b_ih", "L0_cond_b_hh", "L1_cond_ada_w", "L1_cond_ada_b",
        "L1_cond_qkv_w", "L1_cond_qkv_b", "L1_cond_out_w", "L1_cond_out_b", "L1_cond_ffn_w1", "L1_cond_ffn_b1",
        "L1_cond_ffn_w2", "L1_cond_ffn_b2", "L2_cond_W_emb", "L2_cond_b_emb", "L2_cond_g_norm", "L2_cond_W_qkv",
        "L2_cond_g_q", "L2_cond_g_k", "L2_cond_W_out", "L3_cond_coupling", "L3_cond_bias"]


def kernel(**inputs):
    import numpy as _np
    import concourse.bacc as _bacc
    from concourse import mybir as _mybir
    from concourse.bass_utils import run_bass_kernel_spmd as _run

    nc = _bacc.Bacc("TRN2", target_bir_lowering=False, num_devices=1)
    arrays, args = {}, {}
    for name in _INS:
        a = _np.ascontiguousarray(inputs[name])
        arrays[f"in_{name}"] = a
        args[name] = nc.dram_tensor(f"in_{name}", a.shape, _mybir.dt.from_np(a.dtype), kind="ExternalInput").ap()
    out = nc.dram_tensor("out_x", (B, T, D), F32, kind="ExternalOutput").ap()
    build(nc, args, out)
    r = _run(nc, [arrays], core_ids=[0])
    return r.results[0]["out_x"]
```

```python
from contextlib import ExitStack

import concourse.bass as bass
from concourse import mybir

ALU = mybir.AluOpType
ACT = mybir.ActivationFunctionType
F32 = mybir.dt.float32
AX_X = mybir.AxisListType.X

B, T, D = 128, 32, 256
P = 128
C = D // P
LOT_B = 16
LOTS = B // LOT_B
LOT = LOT_B * T
G = LOT // P
GB = P // T
H = 16
DH1 = 128
DH2 = D // H
INNER = H * DH1
QUAD = 4
QUADS = H // QUAD
MLP = 4 * D
HC = P // DH2
EPS = 1e-6

DT, EPSILON, ALPHA, BETA, CLAMP = 0.01, 0.08, 0.7, 0.8, 20.0
STEP = (DT / 2, DT / 2, DT, DT / 6)

ROWS = {}
for _name, _n in (("b_ih", 6), ("b_hh", 6), ("ada_b", 12), ("qkv_b", 48), ("out_b", 2), ("ffn_b1", 8),
                  ("ffn_b2", 2), ("b_emb", 4), ("g_norm", 2), ("bias", 2), ("g_q", 1), ("g_k", 1)):
    ROWS[_name] = (sum(n for _, n in ROWS.values()), _n)
N_ROWS = sum(n for _, n in ROWS.values())

SHIFT1, SCALE1, GATE1, SHIFT2, SCALE2, GATE2, SCALE3, SHIFT3 = range(0, 16, 2)


class Signal:

    def __init__(self, sem, per=0):
        self.sem, self.per = sem, per

    def at(self, turn, k):
        return turn * self.per + k


class Chain:

    def __init__(self, eng, sem):
        self.eng, self.sem, self.base, self.k = eng, sem, 0, 0

    def start(self, base):
        self.base, self.k = base, 0

    def link(self, ins):
        ins.then_inc(self.sem, 1)
        self.k += 1
        self.eng.wait_ge(self.sem, self.base + self.k)


def first_fills():
    def qk(q):
        return [(n, QUAD * q + h, "act") for h in range(QUAD) for n in ("q", "k")]

    def v(q):
        return [("v", G * q + g, "dve") for g in range(G)]

    fills = qk(0) + v(0)
    for q in range(QUADS):
        fills += [("s", q, "dve")]
        if q < QUADS - 1:
            fills += qk(q + 1)
        fills += [("o", QUAD * q + h, "act") for h in range(QUAD)]
        if q < QUADS - 1:
            fills += v(q + 1)
    fills += [("y", 0, "dve"), ("y", 1, "dve"), ("m2", 0, "dve"), ("m2", 1, "dve")]
    fills += [("h", m, "act") for m in range(MLP // P)]
    return fills + [("xin", 0, "act"), ("xin", 1, "act"), ("m1", 0, "dve"), ("m1", 1, "dve")]


def second_fills():
    fills = [("f", 0, "dve"), ("f", 1, "dve"), ("m3", 0, "dve"), ("m3", 1, "dve")]
    fills += [("qk", g, "act") for g in range(G)]
    for g in range(G):
        if g > 0:
            fills += [("w", g - 1, "dve")]
        fills += [("t", g, "dve"), ("v", g, "act"), ("s", g, "dve"), ("o", g, "act")]
    return fills + [("w", G - 1, "dve"), ("xo", 0, "act"), ("xo", 1, "act")]


class Ring:

    def __init__(self, fills, banks, filled, emptied, lead=0):
        self.fills, self.banks, self.filled_sem, self.emptied_sem = fills, banks, filled, emptied
        self.lead = lead
        self.ordinal = {f[:2]: k + 1 for k, f in enumerate(fills)}
        self.who = {f[:2]: f[2] for f in fills}
        self.per = {w: sum(f[2] == w for f in fills) for w in ("act", "dve")}
        first = fills[len(fills) - (lead or len(banks)):]
        self.ahead = {w: sum(f[2] == w for f in first) for w in ("act", "dve")}
        self.nth = {}
        for w in ("act", "dve"):
            for k, f in enumerate([f for f in fills if f[2] == w]):
                self.nth[f[:2]] = k + 1
        self.next = 0

    def bank(self, name, i):
        return self.banks[(self.ordinal[(name, i)] - 1 - len(self.fills)) % len(self.banks)]

    def filled(self, turn, name, i):
        return turn * len(self.fills) + (self.ordinal[(name, i)] + self.lead)

    def emptied(self, turn, name, i):
        return turn * self.per[self.who[(name, i)]] + (self.nth[(name, i)] + self.ahead[self.who[(name, i)]])

    def wait_filled(self, eng, turn, name, i):
        eng.wait_ge(self.filled_sem, self.filled(turn, name, i))
        return self.bank(name, i)

    def wait_emptied(self, eng, turn, name, i):
        eng.wait_ge(self.emptied_sem[self.who[(name, i)]], self.emptied(turn, name, i))

    def wait_free(self, eng, turn, name, i):
        k = self.ordinal[(name, i)] - 1
        same = [j for j in range(len(self.fills)) if (j - k) % len(self.banks) == 0 and j < k]
        if same:
            self.wait_emptied(eng, turn, *self.fills[same[-1]][:2])
        else:
            mine = self.bank(name, i)
            before = [f[:2] for f in self.fills if self.bank(*f[:2]) is mine]
            self.wait_emptied(eng, turn - 1, *before[-1])
        return self.bank(name, i)


CHAIN1, CHAIN2 = 20, 23


def build(nc, A, out):
    with ExitStack() as ctx:
        def sb(name, shape, dt=F32):
            return ctx.enter_context(nc.sbuf_tensor(name, shape, dt))

        def sem(name, per=0):
            return Signal(ctx.enter_context(nc.semaphore(name)), per)

        bank = [ctx.enter_context(nc.psum_tensor(f"bank{i}", [P, 512], F32)) for i in range(8)]
        y_bank = bank[4:6]

        x_feat = sb("x_feat", [P, C, T, B])
        w_qkv = sb("w_qkv", [P, C, 3 * INNER])
        w_out = sb("w_out", [P, H, D])
        w_f1 = sb("w_f1", [P, C, MLP])
        w_f2 = sb("w_f2", [P, MLP // P, D])
        w_qkv2 = sb("w_qkv2", [P, C, 3 * D])
        w_out2 = sb("w_out2", [P, C, D])
        coupT = sb("coupT", [P, C, D])
        mod = sb("mod", [P, 16, B])
        col = sb("col", [P, N_ROWS])
        bsum = sb("bsum", [P, 4])
        ident = sb("ident", [P, P])
        condT = sb("condT", [P, C, B])
        k_mask = sb("k_mask", [P, HC])
        minus_half = sb("minus_half", [P, 2 * H])

        arena = sb("arena", [P, 22144])

        def view(name, at, size):
            assert at + size <= 22144

            return arena[:, at:at + size]

        x_rows = view("x_rows", 0, T * D).rearrange("p (t d) -> p t d", t=T)
        ada_w = view("ada_w", 8192, 3072).rearrange("p (c n) -> p c n", c=C)
        w_emb = view("w_emb", 11264, 1024).rearrange("p (c n) -> p c n", c=C)
        coup_rows = view("coup_rows", 12288, 512).rearrange("p (c n) -> p c n", c=C)
        w_ih = view("w_ih", 12800, 1536).rearrange("p (c n) -> p c n", c=C)
        w_hh = view("w_hh", 14336, 1536).rearrange("p (c n) -> p c n", c=C)
        cond = view("cond", 15872, 256)
        rows = view("rows", 16128, 128)
        gq_row = view("gq_row", 16256, 128)
        h_buf = view("h_buf", 0, 512).rearrange("p (s c b) -> p s c b", s=2, c=C)
        gate_r = view("gate_r", 512, 256).rearrange("p (c b) -> p c b", c=C)
        gate_z = view("gate_z", 768, 256).rearrange("p (c b) -> p c b", c=C)
        one_z = view("one_z", 1024, 256).rearrange("p (c b) -> p c b", c=C)
        z_h = view("z_h", 1280, 256).rearrange("p (c b) -> p c b", c=C)
        pre_n = view("pre_n", 1536, 256).rearrange("p (c b) -> p c b", c=C)
        cand = view("cand", 1792, 256).rearrange("p (c b) -> p c b", c=C)
        x0_tok = view("x0_tok", 0, 1024).rearrange("p (g d) -> p g d", g=G)
        xm = view("xm", 1024, 1024).rearrange("p (c n) -> p c n", c=C)
        qT = view("qT", 2048, 2048).rearrange("p (h n) -> p h n", h=QUAD)
        kT = view("kT", 4096, 2048).rearrange("p (h n) -> p h n", h=QUAD)
        hT = view("hT", 2048, 4096).rearrange("p (m n) -> p m n", m=MLP // P)
        v_tok = view("v_tok", 6144, 2048).rearrange("p (g n) -> p g n", g=G)
        yT = view("yT", 6144, 1024).rearrange("p (c n) -> p c n", c=C)
        x_tok = view("x_tok", 7168, 1024).rearrange("p (g d) -> p g d", g=G)
        prob = view("prob", 8192, 512)
        probT = view("probT", 8704, 2048).rearrange("p (h n) -> p h n", h=H)
        oT = view("oT", 10752, 2048).rearrange("p (h n) -> p h n", h=QUAD)
        x_lot = view("x_lot", 10752, 1024).rearrange("p (c n) -> p c n", c=C)
        xn = view("xn", 10752, 1024).rearrange("p (g d) -> p g d", g=G)
        xn3 = view("xn3", 11776, 1024).rearrange("p (g d) -> p g d", g=G)
        x2_tok = view("x2_tok", 12800, 1024).rearrange("p (g d) -> p g d", g=G)
        xm3 = view("xm3", 13824, 1024).rearrange("p (c n) -> p c n", c=C)
        qk2 = view("qk2", 14848, 2048).rearrange("p (g n) -> p g n", g=G)
        q2T = view("q2T", 16896, 512).rearrange("p (s c n) -> p s c n", s=2, c=C)
        prob2 = view("prob2", 17408, 512)
        qk_sq = prob2
        k_wide = view("k_wide", 17920, 2048).rearrange("p (c b h t) -> p c b h t", c=C, b=GB, h=HC)
        V_WIDE = 19968
        v_wide = view("v_wide", V_WIDE, 2048).rearrange("p (h n) -> p h n", h=H)
        v_diag = [arena[:, V_WIDE + c * HC * P:V_WIDE + c * HC * P + HC * (P + DH2)].rearrange("p (h n) -> p h n", h=HC)[:, :, 0:DH2]
                  for c in range(C)]
        q_of = [view(f"q{i}", 256 * i, 256).rearrange("p (c b) -> p c b", c=C) for i in range(4)]
        p_of = [view(f"p{i}", 1024 + 256 * i, 256).rearrange("p (c b) -> p c b", c=C) for i in range(4)]
        names = ("drive", "tanh", "sq", "v", "base", "q_sum", "q_rise", "q_rise3", "q_twice3", "q_part3", "q_raw",
                 "p_fall", "p_rest", "p_rise", "p_twice", "p_part", "p_raw", "outT")
        net = {n: view(n, 2048 + 256 * k, 256).rearrange("p (c b) -> p c b", c=C) for k, n in enumerate(names)}
        minus_ident = view("minus_ident", 6912, P)
        out_rows = view("out_rows", 8192, 256)

        o2T = sb("o2T", [P, C, P])
        tick = sb("tick", [P, 4])
        stats = sb("stats", [P, G, 6])
        mean_var = sb("mean_var", [P, G, 2])
        spread = sb("spread", [P, G])
        rstd = sb("rstd", [P, G])
        stats3, mean_var3, spread3, rstd3 = (sb(n, s) for n, s in (("stats3", [P, G, 6]), ("mean_var3", [P, G, 2]), ("spread3", [P, G]), ("rstd3", [P, G])))
        soft_max = sb("soft_max", [P, 2, 16])
        soft_sum = sb("soft_sum", [P, 2, 16])
        soft_inv = sb("soft_inv", [P, 2, 16])
        ss2 = sb("ss2", [P, G, 2 * H])
        rstd2 = sb("rstd2", [P, G, 2 * H])

        cond_in, rows_in, ada_in, emb_in, coup_in = (sem(n) for n in ("cond_in", "rows_in", "ada_in", "emb_in", "coup_in"))
        gru_in = sem("gru_in")
        x_in = [sem(f"x_in{i}") for i in range(4)]
        lot_w_in, lot_w2_in = sem("lot_w_in"), sem("lot_w2_in")
        consts, ident_step = sem("consts"), sem("ident_step")
        set_filled, set_act, set_dve = sem("set_filled"), sem("set_act"), sem("set_dve")
        set_chain = sem("set_chain")
        gates_ready = sem("gates_ready", 3)
        r_ready, z_ready, n_ready = sem("r_ready", 2), sem("z_ready", 2), sem("n_ready", 2)
        r_used = sem("r_used", 2)
        pre_ready, one_z_ready = sem("pre_ready", 2), sem("one_z_ready", 1)
        z_h_ready, prod_ready = sem("z_h_ready", 1), sem("prod_ready", 2)
        h_ready, x_added = sem("h_ready", 2), sem("x_added", 1)
        staged = sem("staged", C)
        fills1, fills2 = first_fills(), second_fills()
        ring1 = Ring(fills1, bank[0:4], sem("filled1").sem, {w: sem(w + "_emptied1").sem for w in ("act", "dve")}, lead=4)
        ring2 = Ring(fills2, bank[6:8], sem("filled2").sem, {w: sem(w + "_emptied2").sem for w in ("act", "dve")})
        spread_ready, rstd_ready, xn_ready, mod_ready = sem("spread_ready", 2), sem("rstd_ready", 2), sem("xn_ready", 2 * G), sem("mod_ready", 2 * C)
        spread3_ready, rstd3_ready, xn3_ready, mod3_ready = sem("spread3_ready", 1), sem("rstd3_ready", 1), sem("xn3_ready", G), sem("mod3_ready", C)
        exp_ready, probT_ready = sem("exp_ready", QUADS), sem("probT_ready", QUADS)
        exp2_ready, probT2_ready = sem("exp2_ready", G), sem("probT2_ready", G)
        oT_used, y_ready, yT_ready = sem("oT_used", QUADS - 1), sem("y_ready", 2), sem("yT_ready", 4)
        doubled = sem("doubled", 1)
        sq_ready, ss2_ready, rstd2_ready, qkn_ready = sem("sq_ready", G), sem("ss2_ready", G), sem("rstd2_ready", G), sem("qkn_ready", G)
        chain1, chain2 = sem("chain1", CHAIN1), sem("chain2", CHAIN2)
        zeroed = sem("zeroed")
        drive_ready, drive_used = sem("drive_ready", C), sem("drive_used", 1)
        tanh_ready, q_sq_ready, coupled, q_ready = (sem(n, 4 * C) for n in ("tanh_ready", "q_sq_ready", "coupled", "q_ready"))
        v_ready, base_ready = sem("v_ready", 4 * C), sem("base_ready", 4 * C)
        p_ready, p_fall_ready, p_rest_ready = sem("p_ready", 4), sem("p_fall_ready", 4), sem("p_rest_ready", 4)
        q_rise_ready, q_rise3_ready, q_twice3_ready, q_part3_ready, q_sum_ready = (
            sem(n, 1) for n in ("q_rise_ready", "q_rise3_ready", "q_twice3_ready", "q_part3_ready", "q_sum_ready"))
        p_rise_ready, p_twice_ready, p_part_ready, p_clip = sem("p_rise_ready", 1), sem("p_twice_ready", 1), sem("p_part_ready", 1), sem("p_clip", 2)
        q_raw_ready, minus_ready = sem("q_raw_ready", C), sem("minus_ready")
        outT_ready, turned, out_ready, out_sent, rows_free = sem("outT_ready", 1), sem("turned", 1), sem("out_ready", 1), sem("out_sent", 16), sem("rows_free", 1)

        def row(name):
            at, n = ROWS[name]
            return rows[at:at + n, :]

        def column(name, k=0):
            at, _ = ROWS[name]
            return col[:, at + k:at + k + 1]

        block = ctx.enter_context(nc.Block())

        X_PAIRS = T // 2
        order = ["turn", "coup"] + [f"x{i}" for i in range(X_PAIRS)] + [f"mod{i}" for i in range(4)]
        set_bank = {n: bank[i % 8] for i, n in enumerate(order)}
        set_who = {n: ("act" if n.startswith("x") and int(n[1:]) % 2 else "dve") for n in order}
        set_ord = {n: i + 1 for i, n in enumerate(order)}
        set_emptied = {}
        for who in ("act", "dve"):
            for k, n in enumerate([n for n in order if set_who[n] == who]):
                set_emptied[n] = k + 1
        SET_ACT, SET_DVE = (sum(set_who[n] == w for n in order) for w in ("act", "dve"))

        @block.sync
        def _(sp):
            sp.dma_start(cond, A["cond_2048"]).then_inc(cond_in.sem, 16)
            names = {"b_ih": "L0_cond_b_ih", "b_hh": "L0_cond_b_hh", "ada_b": "L1_cond_ada_b", "qkv_b": "L1_cond_qkv_b",
                     "out_b": "L1_cond_out_b", "ffn_b1": "L1_cond_ffn_b1", "ffn_b2": "L1_cond_ffn_b2",
                     "b_emb": "L2_cond_b_emb", "g_norm": "L2_cond_g_norm", "bias": "L3_cond_bias"}
            for name, arg in names.items():
                sp.dma_start(row(name), A[arg].rearrange("(c p) -> c p", p=P)).then_inc(rows_in.sem, 16)
            for name, arg in (("g_q", "L2_cond_g_q"), ("g_k", "L2_cond_g_k")):
                src = A[arg].rearrange("(a o d) -> a o d", a=1, o=1).to_broadcast([1, HC, DH2])
                sp.dma_start(row(name).rearrange("a (h d) -> a h d", d=DH2), src).then_inc(rows_in.sem, 16)
            for i in range(4):
                sp.dma_start(x_rows[:, 8 * i:8 * i + 8, :], A["x"][:, 8 * i:8 * i + 8, :]).then_inc(x_in[i].sem, 16)
                if i == 0:
                    sp.dma_start(coup_rows, A["L3_cond_coupling"].rearrange("(c p) n -> p c n", p=P)).then_inc(coup_in.sem, 16)
            sp.dma_start(ada_w, A["L1_cond_ada_w"].rearrange("(c p) n -> p c n", p=P)).then_inc(ada_in.sem, 16)
            sp.dma_start(w_emb, A["L2_cond_W_emb"].rearrange("(c p) n -> p c n", p=P)).then_inc(emb_in.sem, 16)
            sp.dma_start(w_ih, A["L0_cond_W_ih"].rearrange("(c p) n -> p c n", p=P)).then_inc(gru_in.sem, 16)
            sp.dma_start(w_hh, A["L0_cond_W_hh"].rearrange("(c p) n -> p c n", p=P)).then_inc(gru_in.sem, 16)
            sp.dma_start(w_out2[:, :, :], A["L2_cond_W_out"].rearrange("(c p) n -> p c n", p=P)).then_inc(lot_w2_in.sem, 16)
            sp.dma_start(w_qkv2[:, :, :], A["L2_cond_W_qkv"].rearrange("(c p) n -> p c n", p=P)).then_inc(lot_w_in.sem, 16)
            sp.dma_start(w_qkv[:, :, :], A["L1_cond_qkv_w"].rearrange("(c p) n -> p c n", p=P)).then_inc(lot_w_in.sem, 16)
            sp.dma_start(w_out[:, :, :], A["L1_cond_out_w"].rearrange("(h p) n -> p h n", p=P)).then_inc(lot_w_in.sem, 16)
            sp.dma_start(w_f1[:, :, :], A["L1_cond_ffn_w1"].rearrange("(c p) n -> p c n", p=P)).then_inc(lot_w_in.sem, 16)
            sp.dma_start(w_f2[:, :, :], A["L1_cond_ffn_w2"].rearrange("(m p) n -> p m n", p=P)).then_inc(lot_w_in.sem, 16)
            sp.sem_inc(rows_free.sem, 1)
            with sp.Fori(0, T) as t:
                sp.wait_ge(out_ready.sem, out_ready.at(t, 1))
                sp.dma_start(out[:, bass.ds(t, 1), :].rearrange("b t d -> b (t d)"), out_rows).then_inc(out_sent.sem, 16)
                sp.wait_ge(out_sent.sem, out_sent.at(t, 16))
                sp.sem_inc(rows_free.sem, 1)
            sp.wait_ge(out_sent.sem, 16 * T)

        @block.gpsimd
        def _(pool):
            pool.memset(ident[:, :], 0.0).then_inc(ident_step.sem, 1)
            pool.memset(k_mask[:, :], 1.0).then_inc(ident_step.sem, 1)
            pool.memset(minus_half[:, :], -0.5).then_inc(ident_step.sem, 1)
            pool.wait_ge(ident_step.sem, 3)
            pool.affine_select(out=k_mask[:, :], in_=k_mask[:, :], compare_op=ALU.is_ge, fill=0.0,
                               base=0, pattern=[[-DH2, HC]], channel_multiplier=1).then_inc(ident_step.sem, 1)
            pool.wait_ge(ident_step.sem, 4)
            pool.affine_select(out=k_mask[:, :], in_=k_mask[:, :], compare_op=ALU.is_ge, fill=0.0,
                               base=DH2 - 1, pattern=[[DH2, HC]], channel_multiplier=-1).then_inc(consts.sem, 1)
            pool.affine_select(out=ident[:, :], in_=ident[:, :], compare_op=ALU.not_equal, fill=1.0,
                               base=0, pattern=[[-1, P]], channel_multiplier=1).then_inc(consts.sem, 1)

            pool.sem_inc(x_added.sem, 2)
            with pool.Fori(0, T // 2) as i:
                for par in range(2):
                    t = i * 2 + par
                    pool.wait_ge(h_ready.sem, h_ready.at(t, 4))
                    xt = x_feat[:, :, bass.ds(t, 1), :].rearrange("p c t b -> p c (t b)")
                    pool.tensor_tensor(xt, xt, h_buf[:, 1 - par], ALU.add).then_inc(x_added.sem, 1)

            pool.wait_ge(x_added.sem, T + 2)
            pool.memset(probT, 0.0).then_inc(zeroed.sem, 1)
            pool.memset(v_wide, 0.0).then_inc(zeroed.sem, 1)
            pool.wait_ge(zeroed.sem, 2)

            def power(src, dst, dst_ready):
                n = src.shape[1]
                pool.tensor_tensor(dst, src, minus_half[:, 0:n], ALU.pow).then_inc(dst_ready.sem, 1)

            def lead_in(s):
                pool.wait_ge(spread_ready.sem, spread_ready.at(s, 1))
                power(spread[:, :], rstd[:, :], rstd_ready)

            def lot(s, r, ahead):
                if r is not None:
                    pool.wait_ge(spread3_ready.sem, spread3_ready.at(r, 1))
                    power(spread3[:, :], rstd3[:, :], rstd3_ready)
                    for g in range(G):
                        pool.wait_ge(ss2_ready.sem, ss2_ready.at(r, g + 1))
                        power(ss2[:, g, :], rstd2[:, g, :], rstd2_ready)
                if s is not None:
                    pool.wait_ge(spread_ready.sem, spread_ready.at(s, 2))
                    power(spread[:, :], rstd[:, :], rstd_ready)
                    if r is not None:
                        pool.wait_ge(ring2.filled_sem, ring2.filled(r, "xo", 1))
                    pool.tensor_tensor(x2_tok, x0_tok, x_tok, ALU.add).then_inc(doubled.sem, 1)
                if ahead is not None:
                    lead_in(ahead)

            lead_in(0)
            lot(0, None, 1)
            with pool.Fori(1, LOTS - 1) as s:
                lot(s, s - 1, s + 1)
            lot(LOTS - 1, LOTS - 2, None)
            lot(None, LOTS - 1, None)

            def sum_out(t):
                pool.wait_ge(q_ready.sem, q_ready.at(t, 4 * C + C))
                xt = x_feat[:, :, bass.ds(t, 1), :].rearrange("p c t b -> p c (t b)")
                pool.tensor_tensor(net["outT"], xt, q_of[0], ALU.add).then_inc(outT_ready.sem, 1)

            def net_step(t, before):
                for i in range(4):
                    if i == 0 and before is not None:
                        sum_out(before)
                    if i == 1:
                        pool.wait_ge(q_ready.sem, q_ready.at(t, C + C))
                        pool.tensor_tensor(net["q_rise"], q_of[1], q_of[0], ALU.subtract).then_inc(q_rise_ready.sem, 1)
                    if i == 3:
                        pool.wait_ge(p_rise_ready.sem, p_rise_ready.at(t, 1))
                        pool.wait_ge(p_twice_ready.sem, p_twice_ready.at(t, 1))
                        pool.tensor_tensor(net["p_part"], net["p_rise"], net["p_twice"], ALU.add).then_inc(p_part_ready.sem, 1)
                        pool.wait_ge(p_part_ready.sem, p_part_ready.at(t, 1))
                    pool.wait_ge(p_fall_ready.sem, p_fall_ready.at(t, i + 1))
                    pool.tensor_tensor(net["p_rest"], net["p_fall"], p_of[0] if i < 3 else net["p_part"], ALU.add).then_inc(p_rest_ready.sem, 1)
                    if i == 1:
                        pool.wait_ge(p_ready.sem, p_ready.at(t, 2))
                        pool.tensor_tensor(net["p_rise"], p_of[1], p_of[0], ALU.subtract).then_inc(p_rise_ready.sem, 1)
                    if i == 2:
                        pool.wait_ge(q_rise3_ready.sem, q_rise3_ready.at(t, 1))
                        pool.wait_ge(q_twice3_ready.sem, q_twice3_ready.at(t, 1))
                        pool.tensor_tensor(net["q_part3"], net["q_rise3"], net["q_twice3"], ALU.add).then_inc(q_part3_ready.sem, 1)

            net_step(0, None)
            with pool.Fori(1, T) as t:
                net_step(t, t - 1)
            sum_out(T - 1)

        def set_fill(pe, name):
            at = order.index(name)
            if at >= 8:
                before = order[at - 8]
                pe.wait_ge({"act": set_act, "dve": set_dve}[set_who[before]].sem, set_emptied[before])
            return set_bank[name]

        @block.tensor
        def _(pe):
            mm = pe.matmul
            pe.wait_ge(consts.sem, 2)
            pe.wait_ge(cond_in.sem, 16)
            pe.wait_ge(rows_in.sem, 16 * 12)
            ps = set_fill(pe, "turn")
            for c in range(C):
                pe.transpose(ps[:, c * P:(c + 1) * P], cond[:, c * P:(c + 1) * P], ident[:, :])
            pe.transpose(ps[:, 256:256 + N_ROWS], rows[0:N_ROWS, :], ident[0:N_ROWS, 0:N_ROWS]).then_inc(set_filled.sem, 1)
            pe.wait_ge(coup_in.sem, 16)
            ps = set_fill(pe, "coup")
            for c in range(C):
                for j in range(C):
                    last = pe.transpose(ps[:, c * D + j * P:c * D + (j + 1) * P], coup_rows[:, j, c * P:(c + 1) * P], ident[:, :])
            last.then_inc(set_filled.sem, 1)
            for i in range(X_PAIRS):
                if i % 4 == 0:
                    pe.wait_ge(x_in[i // 4].sem, 16)
                ps = set_fill(pe, f"x{i}")
                for tt in range(2):
                    for c in range(C):
                        last = pe.transpose(ps[:, (c * 2 + tt) * P:(c * 2 + tt + 1) * P], x_rows[:, 2 * i + tt, c * P:(c + 1) * P], ident[:, :])
                last.then_inc(set_filled.sem, 1)
            pe.wait_ge(ada_in.sem, 16)
            pe.wait_ge(emb_in.sem, 16)
            for j in range(16):
                if j % 4 == 0:
                    ps = set_fill(pe, f"mod{j // 4}")
                for c in range(C):
                    w = ada_w[:, c, j * P:(j + 1) * P] if j < 12 else w_emb[:, c, (j - 12) * P:(j - 11) * P]
                    last = mm(ps[:, (j % 4) * B:(j % 4 + 1) * B], w, condT[:, c, :], start=(c == 0), stop=(c == C - 1))
                if j % 4 == 3:
                    last.then_inc(set_filled.sem, 1)

            pe.wait_ge(gru_in.sem, 32)
            pe.wait_ge(set_act.sem, SET_ACT)
            pe.wait_ge(set_dve.sem, SET_DVE)

            def gru_input(par, t):
                xt = lambda c: x_feat[:, c, bass.ds(t, 1), :].rearrange("p t b -> p (t b)") if not isinstance(t, int) else x_feat[:, c, t, :]
                for k, j0 in ((0, 0), (1, 2), (2, 4)):
                    for j in range(2):
                        for c in range(C):
                            last = mm(bank[4 * par + k][:, j * B:(j + 1) * B], w_ih[:, c, (j0 + j) * P:(j0 + j + 1) * P], xt(c),
                                      start=(j == 0 and c == 0), stop=(k == 2 and j == 1 and c == 1), skip_group_check=True)
                return last

            def gru_hidden(par, t):
                pe.wait_ge(h_ready.sem, h_ready.at(t, 2))
                for k, j0 in ((0, 0), (3, 4), (1, 2)):
                    for c in range(C):
                        for j in range(2):
                            last = mm(bank[4 * par + k][:, j * B:(j + 1) * B], w_hh[:, c, (j0 + j) * P:(j0 + j + 1) * P], h_buf[:, par, c, :],
                                      start=(k == 3 and j == 0 and c == 0), stop=(j == 1 and c == 1), skip_group_check=True)
                    last.then_inc(gates_ready.sem, 1)

            gru_input(0, 0)
            with pe.Fori(0, T // 2 - 1) as i:
                gru_hidden(0, i * 2)
                gru_input(1, i * 2 + 1)
                gru_hidden(1, i * 2 + 1)
                gru_input(0, i * 2 + 2)
            gru_hidden(0, T - 2)
            gru_input(1, T - 1)
            gru_hidden(1, T - 1)

            pe.wait_ge(lot_w_in.sem, 16 * 5)
            pe.wait_ge(set_dve.sem, SET_DVE + 1)
            def begin(ring, s, name, i):
                if isinstance(s, int) and s < 0:
                    return ring.bank(name, i)
                return ring.wait_free(pe, s, name, i)

            def to_tokens(ring, s, name, src):
                for j in range(2):
                    ps = begin(ring, s, name, j)
                    for gg in range(2):
                        for c in range(C):
                            last = pe.transpose(ps[:, gg * D + c * P:gg * D + (c + 1) * P], src[:, c, (2 * j + gg) * P:(2 * j + gg + 1) * P], ident[:, :])
                    last.then_inc(ring.filled_sem, 1)

            def to_features(ring, s, name, src):
                for c in range(C):
                    ps = begin(ring, s, name, c)
                    for g in range(G):
                        last = pe.transpose(ps[:, g * P:(g + 1) * P], src[:, g, c * P:(c + 1) * P], ident[:, :])
                    last.then_inc(ring.filled_sem, 1)

            def project(s, name, i, w):
                ps = begin(ring1, s, name, i)
                for c in range(C):
                    last = mm(ps[:, :], w[:, c, :], xm[:, c, :], start=(c == 0), stop=(c == C - 1))
                last.then_inc(ring1.filled_sem, 1)

            def q_and_k(s, q):
                for h in range(QUAD * q, QUAD * q + QUAD):
                    project(s, "q", h, w_qkv[:, :, h * DH1:(h + 1) * DH1])
                    project(s, "k", h, w_qkv[:, :, INNER + h * DH1:INNER + (h + 1) * DH1])

            def values(s, q):
                for g in range(G):
                    ps = begin(ring1, s, "v", G * q + g)
                    for c in range(C):
                        last = mm(ps[:, :], xm[:, c, g * P:(g + 1) * P], w_qkv[:, c, 2 * INNER + q * 512:2 * INNER + (q + 1) * 512],
                                  start=(c == 0), stop=(c == C - 1))
                    last.then_inc(ring1.filled_sem, 1)

            def scores(s, q):
                ring1.wait_emptied(pe, s, "k", QUAD * q + QUAD - 1)
                ps = begin(ring1, s, "s", q)
                for g in range(G):
                    for h in range(QUAD):
                        for b in range(GB):
                            tok = slice(g * P + b * T, g * P + (b + 1) * T)
                            at_col = (g * QUAD + h) * T
                            last = mm(ps[b * T:(b + 1) * T, at_col:at_col + T], qT[:, h, tok], kT[:, h, tok], start=True, stop=True)
                last.then_inc(ring1.filled_sem, 1)

            def attend(s, q):
                pe.wait_ge(probT_ready.sem, probT_ready.at(s, q + 1))
                ring1.wait_emptied(pe, s, "v", G * q + G - 1)
                for h in range(QUAD):
                    ps = begin(ring1, s, "o", QUAD * q + h)
                    for g in range(G):
                        last = mm(ps[:, g * P:(g + 1) * P], v_tok[:, g, h * DH1:(h + 1) * DH1], probT[:, g * QUAD + h, :], start=True, stop=True)
                    last.then_inc(ring1.filled_sem, 1)

            def project_out(s, q):
                for h in range(QUAD):
                    ring1.wait_emptied(pe, s, "o", QUAD * q + h)
                    for c in range(C):
                        last = mm(y_bank[c][:, :], w_out[:, QUAD * q + h, c * P:(c + 1) * P], oT[:, h, :],
                                  start=(q == 0 and h == 0), stop=(q == QUADS - 1 and h == QUAD - 1))
                last.then_inc((oT_used if q < QUADS - 1 else y_ready).sem, 1)

            def mlp(s, ahead):
                for m in range(MLP // P):
                    project(s, "h", m, w_f1[:, :, m * P:(m + 1) * P])
                if ahead is not None:
                    lead_tokens(ahead)
                for m in range(MLP // P):
                    ring1.wait_emptied(pe, s, "h", m)
                    for c in range(C):
                        last = mm(y_bank[c][:, :], w_f2[:, m, c * P:(c + 1) * P], hT[:, m, :], start=(m == 0), stop=(m == MLP // P - 1))
                    if m == 5 and ahead is not None:
                        lead_features(ahead)
                last.then_inc(y_ready.sem, 1)

            def lead_tokens(s):
                pe.wait_ge(staged.sem, staged.at(s, C))
                to_tokens(ring1, s - 1, "xin", x_lot)

            def lead_features(s):
                pe.wait_ge(xn_ready.sem, xn_ready.at(s, G))
                to_features(ring1, s - 1, "m1", xn)

            def project2(r):
                for g in range(G):
                    ps = begin(ring2, r, "qk", g)
                    for c in range(C):
                        last = mm(ps[:, :], xm3[:, c, g * P:(g + 1) * P], w_qkv2[:, c, 0:2 * D], start=(c == 0), stop=(c == C - 1))
                    last.then_inc(ring2.filled_sem, 1)

            def turn2(r, g):
                pe.wait_ge(qkn_ready.sem, qkn_ready.at(r, g + 1))
                ps = begin(ring2, r, "t", g)
                for k in range(4):
                    last = pe.transpose(ps[:, k * P:(k + 1) * P], qk2[:, g, k * P:(k + 1) * P], ident[:, :])
                last.then_inc(ring2.filled_sem, 1)

            def values2(r, g):
                ps = begin(ring2, r, "v", g)
                for c in range(C):
                    last = mm(ps[:, 0:D], xm3[:, c, g * P:(g + 1) * P], w_qkv2[:, c, 2 * D:3 * D], start=(c == 0), stop=(c == C - 1))
                last.then_inc(ring2.filled_sem, 1)

            def scores2(r, g):
                ring2.wait_emptied(pe, r, "t", g)
                ps = begin(ring2, r, "s", g)
                for c in range(C):
                    for b in range(GB):
                        last = mm(ps[b * T:(b + 1) * T, c * D:(c + 1) * D], q2T[:, g % 2, c, b * T:(b + 1) * T],
                                  k_wide[:, c, b, :, :].rearrange("p h t -> p (h t)"), start=True, stop=True)
                last.then_inc(ring2.filled_sem, 1)

            def attend2(r, g):
                pe.wait_ge(probT2_ready.sem, probT2_ready.at(r, g + 1))
                ring2.wait_emptied(pe, r, "v", g)
                ps = begin(ring2, r, "o", g)
                for c in range(C):
                    for h in range(HC):
                        last = mm(ps[:, c * P:(c + 1) * P], v_wide[:, c * HC + h, :], probT[:, c * HC + h, :],
                                  start=(h == 0), stop=(h == HC - 1))
                last.then_inc(ring2.filled_sem, 1)

            def project_out2(r, g):
                ring2.wait_emptied(pe, r, "o", g)
                ps = begin(ring2, r, "w", g)
                for c in range(C):
                    last = mm(ps[:, 0:D], o2T[:, c, :], w_out2[:, c, :], start=(c == 0), stop=(c == C - 1))
                last.then_inc(ring2.filled_sem, 1)

            def lot(s, r, ahead):
                both = s is not None and r is not None
                if r is not None:
                    pe.wait_ge(yT_ready.sem, yT_ready.at(r, 2 * C))
                    to_tokens(ring2, r, "f", yT)
                if s is not None:
                    pe.wait_ge(mod_ready.sem, mod_ready.at(s, C))
                    q_and_k(s, 0)
                if r is not None:
                    pe.wait_ge(xn3_ready.sem, xn3_ready.at(r, G))
                    to_features(ring2, r, "m3", xn3)
                if s is not None:
                    values(s, 0)
                if r is not None:
                    pe.wait_ge(mod3_ready.sem, mod3_ready.at(r, C))
                    project2(r)
                for q in range(QUADS):
                    if s is not None:
                        scores(s, q)
                    if r is not None and q > 0:
                        project_out2(r, q - 1)
                    if s is not None:
                        if q > 0:
                            project_out(s, q - 1)
                        if q < QUADS - 1:
                            q_and_k(s, q + 1)
                    if r is not None:
                        turn2(r, q)
                        values2(r, q)
                    if s is not None:
                        attend(s, q)
                    if r is not None:
                        scores2(r, q)
                    if s is not None:
                        if q < QUADS - 1:
                            values(s, q + 1)
                        else:
                            project_out(s, q)
                            pe.wait_ge(yT_ready.sem, yT_ready.at(s, C))
                            to_tokens(ring1, s, "y", yT)
                    if r is not None:
                        attend2(r, q)
                if r is not None:
                    project_out2(r, QUADS - 1)
                    ring2.wait_emptied(pe, r, "w", G - 1)
                    to_features(ring2, r, "xo", x2_tok)
                if s is not None:
                    pe.wait_ge(xn_ready.sem, xn_ready.at(s, 2 * G))
                    to_features(ring1, s, "m2", xn)
                    pe.wait_ge(mod_ready.sem, mod_ready.at(s, 2 * C))
                    mlp(s, ahead)

            lead_tokens(0)
            lead_features(0)
            lot(0, None, 1)
            with pe.Fori(1, LOTS - 1) as s:
                lot(s, s - 1, s + 1)
            lot(LOTS - 1, LOTS - 2, None)
            lot(None, LOTS - 1, None)

            ring2.wait_emptied(pe, LOTS - 1, "xo", 1)
            def turn_out(t):
                pe.wait_ge(outT_ready.sem, outT_ready.at(t, 1))
                for c in range(C):
                    last = pe.transpose(bank[4][:, c * P:(c + 1) * P], net["outT"][:, c, :], ident[:, :])
                last.then_inc(turned.sem, 1)

            def net_step(t, before):
                for i in range(4):
                    pair = bank[2 * (i % 2):2 * (i % 2) + 2]
                    if i == 0:
                        pe.wait_ge(drive_ready.sem, drive_ready.at(t, C))
                    for j in range(C):
                        last = mm(pair[j][:, 0:B], ident[:, :], net["drive"][:, j, :], start=True, stop=False, skip_group_check=True)
                    if i == 3:
                        last.then_inc(drive_used.sem, 1)
                    for k in range(C):
                        if k == 1:
                            pe.wait_ge(p_ready.sem, p_ready.at(t, i + 1))
                            for j in range(C):
                                mm(pair[j][:, 0:B], minus_ident, p_of[i][:, j, :], start=False, stop=False, skip_group_check=True)
                        pe.wait_ge(tanh_ready.sem, tanh_ready.at(t, C * i + k + 1))
                        for j in range(C):
                            last = mm(pair[j][:, 0:B], coupT[:, k, j * P:(j + 1) * P], net["tanh"][:, k, :], start=False, stop=(k == C - 1), skip_group_check=True)
                            if k == C - 1:
                                last.then_inc(coupled.sem, 1)
                    if i == 1 and before is not None:
                        turn_out(before)

            pe.wait_ge(minus_ready.sem, 1)
            net_step(0, None)
            with pe.Fori(1, T) as t:
                net_step(t, t - 1)
            turn_out(T - 1)

        @block.scalar
        def _(act):
            def filled_set(name):
                act.wait_ge(set_filled.sem, set_ord[name])
                return set_bank[name]

            for i in range(1, X_PAIRS, 2):
                ps = filled_set(f"x{i}")
                act.activation(x_feat[:, :, 2 * i:2 * i + 2, :], ps[:, :].rearrange("p (c t b) -> p c t b", c=C, t=2), ACT.Copy).then_inc(set_act.sem, 1)

            act.wait_ge(set_dve.sem, SET_DVE)
            with act.Fori(0, T // 2) as i:
                for par in range(2):
                    t = i * 2 + par
                    act.wait_ge(gates_ready.sem, gates_ready.at(t, 1))
                    for c in range(C):
                        act.activation(gate_r[:, c, :], bank[4 * par][:, c * B:(c + 1) * B], ACT.Sigmoid, bias=bsum[:, c:c + 1]).then_inc(r_ready.sem, 1)
                    act.wait_ge(gates_ready.sem, gates_ready.at(t, 3))
                    for c in range(C):
                        act.activation(gate_z[:, c, :], bank[4 * par + 1][:, c * B:(c + 1) * B], ACT.Sigmoid, bias=bsum[:, 2 + c:3 + c]).then_inc(z_ready.sem, 1)
                    for c in range(C):
                        act.wait_ge(pre_ready.sem, pre_ready.at(t, c + 1))
                        act.activation(cand[:, c, :], pre_n[:, c, :], ACT.Tanh).then_inc(n_ready.sem, 1)
                        if c == 0:
                            act.wait_ge(z_ready.sem, z_ready.at(t, 2))
                            act.activation(one_z, gate_z, ACT.Copy, scale=-1.0, bias=1.0).then_inc(one_z_ready.sem, 1)

            act.wait_ge(x_added.sem, T + 2)
            act.wait_ge(zeroed.sem, 2)
            act.sem_inc(ring2.emptied_sem["act"], 2)

            def empty(ring, s, name, i, dst, width, func, **kw):
                ps = ring.wait_filled(act, s, name, i)
                act.activation(dst, ps[:, 0:width], func, **kw).then_inc(ring.emptied_sem["act"], 1)

            def stage(s):
                if not isinstance(s, int) or s > 0:
                    act.wait_ge(ring1.filled_sem, ring1.filled(s - 1, "m2", 1))
                    act.activation(tick[:, 3:4], minus_half[:, 0:1], ACT.Copy)
                for c in range(C):
                    act.activation(x_lot[:, c, :].rearrange("p (b t) -> p b t", t=T),
                                   x_feat[:, c, :, bass.ds(s * LOT_B, LOT_B)].rearrange("p t b -> p b t"), ACT.Copy).then_inc(staged.sem, 1)

            def lead(s):
                if not isinstance(s, int) or s > 0:
                    act.wait_ge(doubled.sem, doubled.at(s - 1, 1))
                for j in range(2):
                    empty(ring1, s - 1, "xin", j, x0_tok[:, 2 * j:2 * j + 2, :].rearrange("p g d -> p (g d)"), 512, ACT.Copy)

            def q_and_k(s, q):
                if q > 0:
                    ring1.wait_filled(act, s, "s", q - 1)
                for h in range(QUAD * q, QUAD * q + QUAD):
                    for name, dst, k in (("q", qT, h), ("k", kT, H + h)):
                        empty(ring1, s, name, h, dst[:, h % QUAD, :], 512, ACT.Identity, bias=column("qkv_b", k))

            def exps(prob, shifted, ready, width):
                act.wait_ge(*shifted)
                act.activation(prob, prob, ACT.Exp, scale=float(width) ** -0.5).then_inc(ready.sem, 1)

            def outputs(s, q):
                if q > 0:
                    act.wait_ge(oT_used.sem, oT_used.at(s, q))
                for h in range(QUAD * q, QUAD * q + QUAD):
                    empty(ring1, s, "o", h, oT[:, h % QUAD, :], 512, ACT.Identity, bias=column("qkv_b", 2 * H + h))

            def project2(r):
                for g in range(G):
                    empty(ring2, r, "qk", g, qk2[:, g, :], 512, ACT.Copy)
                    ring2.wait_emptied(act, r, "qk", g)
                    if g > 0:
                        act.wait_ge(ss2_ready.sem, ss2_ready.at(r, g))
                    act.activation(qk_sq, qk2[:, g, :], ACT.Square).then_inc(sq_ready.sem, 1)

            def values2(r, g):
                ps = ring2.wait_filled(act, r, "v", g)
                for c in range(C):
                    ins = act.activation(v_diag[c], ps[:, c * P:(c + 1) * P].rearrange("p (h d) -> p h d", d=DH2), ACT.Copy)
                ins.then_inc(ring2.emptied_sem["act"], 1)

            def lot(s, r, ahead):
                if s is not None:
                    q_and_k(s, 0)
                if r is not None:
                    project2(r)
                for q in range(QUADS):
                    if s is not None:
                        exps(prob, (ring1.emptied_sem["dve"], ring1.emptied(s, "s", q)), exp_ready, DH1)
                        if q < QUADS - 1:
                            q_and_k(s, q + 1)
                    if r is not None:
                        values2(r, q)
                    if s is not None:
                        outputs(s, q)
                    if r is not None:
                        exps(prob2, (ring2.emptied_sem["dve"], ring2.emptied(r, "s", q)), exp2_ready, DH2)
                        empty(ring2, r, "o", q, o2T[:, :, :].rearrange("p c n -> p (c n)"), D, ACT.Copy)
                if r is not None:
                    for c in range(C):
                        ps = ring2.wait_filled(act, r, "xo", c)
                        act.activation(tick[:, 1 + c:2 + c], minus_half[:, 0:1], ACT.Copy)
                        act.activation(x_feat[:, c, :, bass.ds(r * LOT_B, LOT_B)], ps[:, :].rearrange("p (b t) -> p t b", t=T), ACT.Copy)\
                           .then_inc(ring2.emptied_sem["act"], 1)
                if ahead is not None:
                    stage(ahead)
                if s is not None:
                    for m in range(MLP // P):
                        empty(ring1, s, "h", m, hT[:, m, :], 512, ACT.Gelu, bias=column("ffn_b1", m))
                if ahead is not None:
                    lead(ahead)

            stage(0)
            lead(0)
            lot(0, None, 1)
            with act.Fori(1, LOTS - 1) as s:
                lot(s, s - 1, s + 1)
            lot(LOTS - 1, LOTS - 2, None)
            lot(None, LOTS - 1, None)

            ring2.wait_emptied(act, LOTS - 1, "xo", 1)

            def send_out(t):
                act.wait_ge(turned.sem, turned.at(t, 1))
                act.wait_ge(rows_free.sem, rows_free.at(t, 1))
                act.activation(out_rows, bank[4][:, 0:D], ACT.Copy).then_inc(out_ready.sem, 1)

            def drive(t):
                for c in range(C):
                    act.activation(net["drive"][:, c, :], x_feat[:, c, bass.ds(t, 1), :].rearrange("p t b -> p (t b)"), ACT.Identity,
                                   bias=column("bias", c)).then_inc(drive_ready.sem, 1)

            def net_step(t, before, ahead):
                for i in range(4):
                    for c in range(C):
                        act.wait_ge(q_ready.sem, q_ready.at(t, C * i + c + 1))
                        act.activation(net["tanh"][:, c, :], q_of[i][:, c, :], ACT.Tanh).then_inc(tanh_ready.sem, 1)
                        act.activation(net["sq"][:, c, :], q_of[i][:, c, :], ACT.Square).then_inc(q_sq_ready.sem, 1)
                    act.wait_ge(p_ready.sem, p_ready.at(t, i + 1))
                    if i < 3:
                        act.activation(net["p_fall"], p_of[i], ACT.Copy, scale=-STEP[i] * EPSILON * BETA, bias=STEP[i] * EPSILON * ALPHA)\
                           .then_inc(p_fall_ready.sem, 1)
                    else:
                        act.activation(net["p_fall"], p_of[i], ACT.Copy, scale=1 - DT / 2 * EPSILON * BETA, bias=DT / 2 * EPSILON * ALPHA)\
                           .then_inc(p_fall_ready.sem, 1)
                    if i == 1 and before is not None:
                        send_out(before)
                    if i == 2:
                        act.activation(net["q_twice3"], q_of[2], ACT.Copy, scale=2 / 3).then_inc(q_twice3_ready.sem, 1)
                        act.wait_ge(q_rise_ready.sem, q_rise_ready.at(t, 1))
                        act.activation(net["q_rise3"], net["q_rise"], ACT.Copy, scale=1 / 3).then_inc(q_rise3_ready.sem, 1)
                        act.activation(net["p_twice"], p_of[2], ACT.Copy, scale=2.0).then_inc(p_twice_ready.sem, 1)
                    if i == 3 and ahead is not None:
                        act.wait_ge(drive_used.sem, drive_used.at(t, 1))
                        act.activation(tick[:, 1:2], minus_half[:, 0:1], ACT.Copy)
                        drive(ahead)

            act.activation(minus_ident, ident[:, :], ACT.Copy, scale=-1.0).then_inc(minus_ready.sem, 1)
            drive(0)
            net_step(0, None, 1)
            with act.Fori(1, T - 1) as t:
                net_step(t, t - 1, t + 1)
            net_step(T - 1, T - 2, None)
            send_out(T - 1)

        @block.vector
        def _(dve):
            chain = Chain(dve, set_chain.sem)
            link = chain.link

            def filled_set(name):
                dve.wait_ge(set_filled.sem, set_ord[name])
                return set_bank[name]

            ps = filled_set("turn")
            dve.wait_ge(consts.sem, 2)
            link(dve.tensor_copy(condT[:, :, :].rearrange("p c b -> p (c b)"), ps[:, 0:C * B]))
            dve.tensor_copy(col[:, :], ps[:, 256:256 + N_ROWS]).then_inc(set_dve.sem, 1)
            dve.wait_ge(set_dve.sem, 1)
            at_ih, at_hh = ROWS["b_ih"][0], ROWS["b_hh"][0]
            link(dve.tensor_tensor(bsum[:, :], col[:, at_ih:at_ih + 4], col[:, at_hh:at_hh + 4], ALU.add))
            link(dve.tensor_scalar(k_mask[:, :], k_mask[:, :], column("g_k"), None, ALU.mult))
            ps = filled_set("coup")
            dve.tensor_copy(coupT[:, :, :].rearrange("p c n -> p (c n)"), ps[:, :]).then_inc(set_dve.sem, 1)
            for i in range(0, X_PAIRS, 2):
                ps = filled_set(f"x{i}")
                dve.tensor_copy(x_feat[:, :, 2 * i:2 * i + 2, :], ps[:, :].rearrange("p (c t b) -> p c t b", c=C, t=2)).then_inc(set_dve.sem, 1)
            for j in range(16):
                if j % 4 == 0:
                    ps = filled_set(f"mod{j // 4}")
                src = ps[:, (j % 4) * B:(j % 4 + 1) * B]
                bias = column("ada_b", j) if j < 12 else column("b_emb", j - 12)
                if j // 2 * 2 in (SCALE1, SCALE2, SCALE3):
                    ins = dve.tensor_scalar(mod[:, j, :], src, bias, 1.0, ALU.add, ALU.add)
                else:
                    ins = dve.tensor_scalar(mod[:, j, :], src, bias, None, ALU.add)
                if j % 4 == 3:
                    ins.then_inc(set_dve.sem, 1)
                else:
                    link(ins)
            for c in range(C):
                link(dve.tensor_scalar(mod[:, SCALE3 + c, :], mod[:, SCALE3 + c, :], column("g_norm", c), None, ALU.mult))
            dve.wait_ge(set_act.sem, SET_ACT)
            for c in range(C):
                dve.tensor_copy(h_buf[:, 0, c, :], condT[:, c, :]).then_inc(h_ready.sem, 1)
            dve.wait_ge(lot_w2_in.sem, 16)
            for c in range(C):
                ins = dve.tensor_tensor(w_out2[:, c, c * P:(c + 1) * P], w_out2[:, c, c * P:(c + 1) * P], ident[:, :], ALU.add)
                if c == C - 1:
                    ins.then_inc(set_dve.sem, 1)
                else:
                    link(ins)

            with dve.Fori(0, T // 2) as i:
                for par in range(2):
                    t = i * 2 + par
                    dve.wait_ge(gates_ready.sem, gates_ready.at(t, 2))
                    for c in range(C):
                        dve.wait_ge(r_ready.sem, r_ready.at(t, c + 1))
                        dve.scalar_tensor_tensor(pre_n[:, c, :], bank[4 * par + 3][:, c * B:(c + 1) * B], column("b_hh", 4 + c), gate_r[:, c, :],
                                                 ALU.add, ALU.mult).then_inc(r_used.sem, 1)
                    for c in range(C):
                        dve.wait_ge(r_used.sem, r_used.at(t, c + 1))
                        dve.scalar_tensor_tensor(pre_n[:, c, :], bank[4 * par + 2][:, c * B:(c + 1) * B], column("b_ih", 4 + c), pre_n[:, c, :],
                                                 ALU.add, ALU.add).then_inc(pre_ready.sem, 1)
                    dve.wait_ge(z_ready.sem, z_ready.at(t, 2))
                    dve.tensor_tensor(z_h, gate_z, h_buf[:, par], ALU.mult).then_inc(z_h_ready.sem, 1)
                    dve.wait_ge(one_z_ready.sem, one_z_ready.at(t, 1))
                    for c in range(C):
                        dve.wait_ge(n_ready.sem, n_ready.at(t, c + 1))
                        dve.tensor_tensor(cand[:, c, :], cand[:, c, :], one_z[:, c, :], ALU.mult).then_inc(prod_ready.sem, 1)
                    dve.wait_ge(x_added.sem, x_added.at(t, 1))
                    for c in range(C):
                        dve.wait_ge(prod_ready.sem, prod_ready.at(t, c + 1))
                        dve.tensor_tensor(h_buf[:, 1 - par, c, :], cand[:, c, :], z_h[:, c, :], ALU.add).then_inc(h_ready.sem, 1)

            dve.wait_ge(zeroed.sem, 2)
            one, two = Chain(dve, chain1.sem), Chain(dve, chain2.sem)
            LEAD_LINKS = 2

            def of_lot(k, c, s):
                return mod[:, k + c, bass.ds(s * LOT_B, LOT_B)].rearrange("p (b o) -> p b o", o=1).to_broadcast([P, LOT_B, T])

            def tokens(ap):
                return ap.rearrange("p (b t) -> p b t", t=T)

            def moments(src, stats, mean_var, chain):
                for g in range(G):
                    ins = dve.bn_stats(stats[:, g, :], src[:, g, :])
                chain.link(ins)
                dve.memset(tick[:, 0:1], 0.0)
                for g in range(G):
                    ins = dve.bn_aggr(mean_var[:, g, :], stats[:, g, :])
                chain.link(ins)

            def normalise(s, k, src):
                moments(src, stats, mean_var, one)
                dve.tensor_scalar(spread[:, :], mean_var[:, :, 1], EPS, None, ALU.add).then_inc(spread_ready.sem, 1)
                dve.wait_ge(rstd_ready.sem, rstd_ready.at(s, k + 1))
                for g in range(G):
                    dve.tensor_scalar(xn[:, g, :], src[:, g, :], mean_var[:, g, 0:1], rstd[:, g:g + 1], ALU.subtract, ALU.mult)\
                       .then_inc(xn_ready.sem, 1)

            def normalise3(r):
                moments(x2_tok, stats3, mean_var3, two)
                two.link(dve.tensor_tensor(spread3[:, :], mean_var3[:, :, 0], mean_var3[:, :, 0], ALU.mult))
                dve.scalar_tensor_tensor(spread3[:, :], spread3[:, :], EPS, mean_var3[:, :, 1], ALU.add, ALU.add).then_inc(spread3_ready.sem, 1)
                dve.wait_ge(rstd3_ready.sem, rstd3_ready.at(r, 1))
                for g in range(G):
                    dve.tensor_scalar(xn3[:, g, :], x2_tok[:, g, :], rstd3[:, g:g + 1], None, ALU.mult).then_inc(xn3_ready.sem, 1)

            def modulate(ring, turn, name, dst, lot_of, scale, shift, ready):
                for c in range(C):
                    ps = ring.wait_filled(dve, turn, name, c)
                    dve.tensor_tensor(tokens(dst[:, c, :]), tokens(ps[:, :]), of_lot(scale, c, lot_of), ALU.mult).then_inc(ring.emptied_sem["dve"], 1)
                    ring.wait_emptied(dve, turn, name, c)
                    dve.tensor_tensor(tokens(dst[:, c, :]), tokens(dst[:, c, :]), of_lot(shift, c, lot_of), ALU.add).then_inc(ready.sem, 1)

            def heads(ap):
                return ap.rearrange("p (h t) -> p h t", t=T)

            def per_head(ap):
                return ap.rearrange("p (h o) -> p h o", o=1).to_broadcast([P, 16, T])

            def softmax(ring, turn, k, layer, prob, exp_ready, probT_ready, chain, before_turn):
                ps = ring.wait_filled(dve, turn, "s", k)
                chain.link(dve.tensor_reduce(soft_max[:, layer, :], heads(ps[:, :]), AX_X, ALU.max))
                dve.tensor_tensor(heads(prob), heads(ps[:, :]), per_head(soft_max[:, layer, :]), ALU.subtract).then_inc(ring.emptied_sem["dve"], 1)
                dve.wait_ge(exp_ready.sem, exp_ready.at(turn, k + 1))
                chain.link(dve.tensor_reduce(soft_sum[:, layer, :], heads(prob), AX_X, ALU.add))
                chain.link(dve.reciprocal(soft_inv[:, layer, :], soft_sum[:, layer, :]))
                chain.link(dve.tensor_tensor(heads(prob), heads(prob), per_head(soft_inv[:, layer, :]), ALU.mult))
                before_turn()
                for b in range(GB):
                    rows_b = slice(b * T, (b + 1) * T)
                    ins = dve.transpose(probT[rows_b, :, b * T:(b + 1) * T], heads(prob)[rows_b, :, :])
                ins.then_inc(probT_ready.sem, 1)

            def values(s, q):
                for g in range(G):
                    ps = ring1.wait_filled(dve, s, "v", G * q + g)
                    dve.tensor_copy(v_tok[:, g, :], ps[:, :]).then_inc(ring1.emptied_sem["dve"], 1)

            def gate(s, which, bias, k):
                dve.wait_ge(y_ready.sem, y_ready.at(s, which + 1))
                for c in range(C):
                    dve.scalar_tensor_tensor(tokens(yT[:, c, :]), tokens(y_bank[c][:, :]), column(bias, c), of_lot(k, c, s),
                                             ALU.add, ALU.mult).then_inc(yT_ready.sem, 1)

            def add_tokens(ring, turn, name, dst, other):
                for j in range(2):
                    ps = ring.wait_filled(dve, turn, name, j)
                    pair = slice(2 * j, 2 * j + 2)
                    dve.tensor_tensor(dst[:, pair, :].rearrange("p g d -> p (g d)"), ps[:, :],
                                      other[:, pair, :].rearrange("p g d -> p (g d)"), ALU.add).then_inc(ring.emptied_sem["dve"], 1)
                ring.wait_emptied(dve, turn, name, 1)

            def lead(s):
                ring1.wait_emptied(dve, s - 1, "xin", 1)
                normalise(s, 0, x0_tok)
                modulate(ring1, s - 1, "m1", xm, s, SCALE1, SHIFT1, mod_ready)

            def sum_squares(r):
                for g in range(G):
                    dve.wait_ge(sq_ready.sem, sq_ready.at(r, g + 1))
                    two.link(dve.tensor_reduce(ss2[:, g, :], qk_sq.rearrange("p (h d) -> p h d", d=DH2), AX_X, ALU.add))
                    dve.tensor_scalar(ss2[:, g, :], ss2[:, g, :], 1.0 / DH2, EPS, ALU.mult, ALU.add).then_inc(ss2_ready.sem, 1)

            def norm_heads(r, g):
                dve.wait_ge(rstd2_ready.sem, rstd2_ready.at(r, g + 1))
                qk = qk2[:, g, :].rearrange("p (h d) -> p h d", d=DH2)
                dve.tensor_tensor(qk, qk, rstd2[:, g, :].rearrange("p (h o) -> p h o", o=1).to_broadcast([P, 2 * H, DH2]), ALU.mult)\
                   .then_inc(qkn_ready.sem, 1)

            def widen(r, g):
                if g > 0:
                    ring2.wait_filled(dve, r, "s", g - 1)
                ps = ring2.wait_filled(dve, r, "t", g)
                dve.tensor_scalar(q2T[:, g % 2, :, :].rearrange("p c n -> p (c n)"), ps[:, 0:D], column("g_q"), None, ALU.mult)
                for c in range(C):
                    for b in range(GB):
                        src = ps[:, D + c * P + b * T:D + c * P + (b + 1) * T].rearrange("p (o t) -> p o t", o=1).to_broadcast([P, HC, T])
                        mask = k_mask[:, :].rearrange("p (h o) -> p h o", o=1).to_broadcast([P, HC, T])
                        ins = dve.tensor_tensor(k_wide[:, c, b, :, :], src, mask, ALU.mult)
                ins.then_inc(ring2.emptied_sem["dve"], 1)

            def add_out2(r, g):
                ps = ring2.wait_filled(dve, r, "w", g)
                dve.tensor_tensor(x2_tok[:, g, :], ps[:, 0:D], x2_tok[:, g, :], ALU.add).then_inc(ring2.emptied_sem["dve"], 1)

            def lot(s, r, ahead):
                if s is not None:
                    one.start(LEAD_LINKS + s * CHAIN1)
                if r is not None:
                    two.start(r * CHAIN2)
                    dve.wait_ge(doubled.sem, doubled.at(r, 1))
                    add_tokens(ring2, r, "f", x2_tok, x2_tok)
                    normalise3(r)
                    modulate(ring2, r, "m3", xm3, r, SCALE3, SHIFT3, mod3_ready)
                if s is not None:
                    values(s, 0)
                if r is not None:
                    sum_squares(r)
                for q in range(QUADS):
                    if s is not None:
                        def last_turned(q=q):
                            if r is not None and q > 0:
                                ring2.wait_filled(dve, r, "o", q - 1)

                        softmax(ring1, s, q, 0, prob, exp_ready, probT_ready, one, last_turned)
                    if r is not None:
                        if q > 0:
                            add_out2(r, q - 1)
                        norm_heads(r, q)
                        widen(r, q)

                        def last_turned2(q=q):
                            if s is not None:
                                ring1.wait_filled(dve, s, "o", QUAD * q + QUAD - 1)
                            elif q > 0:
                                ring2.wait_filled(dve, r, "o", q - 1)

                        softmax(ring2, r, q, 1, prob2, exp2_ready, probT2_ready, two, last_turned2)
                    if s is not None and q < QUADS - 1:
                        ring1.wait_filled(dve, s, "o", QUAD * q + QUAD - 1)
                        values(s, q + 1)
                if s is not None:
                    gate(s, 0, "out_b", GATE1)
                    add_tokens(ring1, s, "y", x_tok, x0_tok)
                if r is not None:
                    add_out2(r, QUADS - 1)
                if s is not None:
                    normalise(s, 1, x_tok)
                    modulate(ring1, s, "m2", xm, s, SCALE2, SHIFT2, mod_ready)
                if ahead is not None:
                    lead(ahead)
                if s is not None:
                    gate(s, 1, "ffn_b2", GATE2)
                assert s is None or ahead is None or one.k == CHAIN1, one.k
                assert r is None or two.k == CHAIN2, two.k

            one.start(0)
            lead(0)
            lot(0, None, 1)
            with dve.Fori(1, LOTS - 1) as s:
                lot(s, s - 1, s + 1)
            lot(LOTS - 1, LOTS - 2, None)
            lot(None, LOTS - 1, None)

            ring2.wait_emptied(dve, LOTS - 1, "xo", 1)
            for c in range(C):
                dve.tensor_copy(q_of[0][:, c, :], condT[:, c, :]).then_inc(q_ready.sem, 1)
            dve.tensor_copy(p_of[0], condT[:, :, :]).then_inc(p_ready.sem, 1)
            def net_step(t):
                for i in range(4):
                    if i == 3:
                        dve.wait_ge(q_part3_ready.sem, q_part3_ready.at(t, 1))
                        dve.wait_ge(q_ready.sem, q_ready.at(t, C * i + C))
                        dve.scalar_tensor_tensor(net["q_sum"], q_of[3], 1 / 3, net["q_part3"], ALU.mult, ALU.add).then_inc(q_sum_ready.sem, 1)

                    def raise_q(c, i=i):
                        dve.wait_ge(base_ready.sem, base_ready.at(t, C * i + c + 1))
                        dve.wait_ge(coupled.sem, coupled.at(t, C * i + c + 1))
                        dst = q_of[i + 1] if i < 3 else net["q_raw"]
                        dve.scalar_tensor_tensor(dst[:, c, :], bank[2 * (i % 2) + c][:, 0:B], STEP[i], net["base"][:, c, :], ALU.mult, ALU.add)\
                           .then_inc(q_ready.sem if i < 3 else q_raw_ready.sem, 1)
                        if i == 3:
                            dve.wait_ge(q_raw_ready.sem, q_raw_ready.at(t, c + 1))
                            dve.tensor_scalar(q_of[0][:, c, :], net["q_raw"][:, c, :], CLAMP, -CLAMP, ALU.min, ALU.max).then_inc(q_ready.sem, 1)

                    for c in range(C):
                        dve.wait_ge(q_sq_ready.sem, q_sq_ready.at(t, C * i + c + 1))
                        dve.scalar_tensor_tensor(net["v"][:, c, :], net["sq"][:, c, :], -3.0, q_of[i][:, c, :], ALU.add, ALU.mult).then_inc(v_ready.sem, 1)
                        if c == 1:
                            raise_q(0)
                        dve.wait_ge(v_ready.sem, v_ready.at(t, C * i + c + 1))
                        if i == 3 and c == 0:
                            dve.wait_ge(q_sum_ready.sem, q_sum_ready.at(t, 1))
                        dve.scalar_tensor_tensor(net["base"][:, c, :], net["v"][:, c, :], -STEP[i] / 3, (q_of[0] if i < 3 else net["q_sum"])[:, c, :],
                                                 ALU.mult, ALU.add).then_inc(base_ready.sem, 1)
                    raise_q(1)
                    dve.wait_ge(p_rest_ready.sem, p_rest_ready.at(t, i + 1))
                    if i < 3:
                        dve.scalar_tensor_tensor(p_of[i + 1], q_of[i], STEP[i] * EPSILON, net["p_rest"], ALU.mult, ALU.add).then_inc(p_ready.sem, 1)
                    else:
                        dve.scalar_tensor_tensor(net["p_raw"], q_of[3], DT / 2 * EPSILON, net["p_rest"], ALU.mult, ALU.add).then_inc(p_clip.sem, 1)
                        dve.wait_ge(p_clip.sem, p_clip.at(t, 1))
                        dve.tensor_scalar(net["p_raw"], net["p_raw"], 1 / 3, CLAMP, ALU.mult, ALU.min).then_inc(p_clip.sem, 1)
                        dve.wait_ge(p_clip.sem, p_clip.at(t, 2))
                        dve.tensor_scalar(p_of[0], net["p_raw"], -CLAMP, None, ALU.max).then_inc(p_ready.sem, 1)

            with dve.Fori(0, T) as t:
                net_step(t)


_INS = ["x", "cond_2048", "L0_cond_W_ih", "L0_cond_W_hh", "L0_cond_b_ih", "L0_cond_b_hh", "L1_cond_ada_w", "L1_cond_ada_b",
        "L1_cond_qkv_w", "L1_cond_qkv_b", "L1_cond_out_w", "L1_cond_out_b", "L1_cond_ffn_w1", "L1_cond_ffn_b1",
        "L1_cond_ffn_w2", "L1_cond_ffn_b2", "L2_cond_W_emb", "L2_cond_b_emb", "L2_cond_g_norm", "L2_cond_W_qkv",
        "L2_cond_g_q", "L2_cond_g_k", "L2_cond_W_out", "L3_cond_coupling", "L3_cond_bias"]


def kernel(**inputs):
    import numpy as _np
    import concourse.bacc as _bacc
    from concourse import mybir as _mybir
    from concourse.bass_utils import run_bass_kernel_spmd as _run

    nc = _bacc.Bacc("TRN2", target_bir_lowering=False, num_devices=1, dynamic_dma_scratch_size=1024)
    arrays, args = {}, {}
    for name in _INS:
        a = _np.ascontiguousarray(inputs[name])
        arrays[f"in_{name}"] = a
        args[name] = nc.dram_tensor(f"in_{name}", a.shape, _mybir.dt.from_np(a.dtype), kind="ExternalInput").ap()
    out = nc.dram_tensor("out_x", (B, T, D), F32, kind="ExternalOutput").ap()
    build(nc, args, out)
    r = _run(nc, [arrays], core_ids=[0])
    return r.results[0]["out_x"]
```

```python
from contextlib import ExitStack

import concourse.bass as bass
from concourse import mybir

ALU = mybir.AluOpType
ACT = mybir.ActivationFunctionType
F32 = mybir.dt.float32
F32R = mybir.dt.float32r
AX_X = mybir.AxisListType.X

B, T, D = 128, 32, 256
P = 128
C = D // P
LOT_B = 16
LOTS = B // LOT_B
LOT = LOT_B * T
G = LOT // P
GB = P // T
H = 16
DH1 = 128
DH2 = D // H
INNER = H * DH1
QUAD = 4
QUADS = H // QUAD
MLP = 4 * D
HC = P // DH2
EPS = 1e-6
PIECE = 512
PARTS = 3
UNIT = PARTS * C
PIECES = QUADS * UNIT

DT, EPSILON, ALPHA, BETA, CLAMP = 0.01, 0.08, 0.7, 0.8, 20.0
STEP = (DT / 2, DT / 2, DT, DT / 6)

ROWS = {}
for _name, _n in (("b_ih", 6), ("b_hh", 6), ("ada_b", 12), ("qkv_b", 48), ("out_b", 2), ("ffn_b1", 8),
                  ("ffn_b2", 2), ("b_emb", 4), ("g_norm", 2), ("bias", 2), ("g_q", 1), ("g_k", 1)):
    ROWS[_name] = (sum(n for _, n in ROWS.values()), _n)
N_ROWS = sum(n for _, n in ROWS.values())

SHIFT1, SCALE1, GATE1, SHIFT2, SCALE2, GATE2, SCALE3, SHIFT3 = range(0, 16, 2)


class Signal:

    def __init__(self, sem, per=0):
        self.sem, self.per = sem, per

    def at(self, turn, k):
        return turn * self.per + k


class Chain:

    def __init__(self, eng, sem):
        self.eng, self.sem, self.base, self.k = eng, sem, 0, 0

    def start(self, base):
        self.base, self.k = base, 0

    def link(self, ins):
        ins.then_inc(self.sem, 1)
        self.k += 1
        self.eng.wait_ge(self.sem, self.base + self.k)


def first_fills():
    def qk(q):
        return [(n, QUAD * q + h, "act") for h in range(QUAD) for n in ("q", "k")]

    def v(q):
        return [("v", G * q + g, "act") for g in range(G)]

    fills = qk(0) + v(0)
    for q in range(QUADS):
        fills += [("s", q, "dve")]
        if q < QUADS - 1:
            fills += qk(q + 1)
        fills += [("o", QUAD * q + h, "act") for h in range(QUAD)]
        if q < QUADS - 1:
            fills += v(q + 1)
    fills += [("y", 0, "dve"), ("y", 1, "dve"), ("m2", 0, "dve"), ("m2", 1, "dve")]
    fills += [("h", m, "act") for m in range(MLP // P)]
    return fills + [("xin", 0, "act"), ("xin", 1, "act"), ("m1", 0, "dve"), ("m1", 1, "dve")]


def second_fills():
    fills = [("f", 0, "dve"), ("f", 1, "dve"), ("m3", 0, "dve"), ("m3", 1, "dve")]
    fills += [("qk", g, "act") for g in range(G)]
    for g in range(G):
        if g > 0:
            fills += [("w", g - 1, "dve")]
        fills += [("t", g, "dve"), ("v", g, "act"), ("s", g, "dve"), ("o", g, "act")]
    return fills + [("w", G - 1, "dve"), ("xo", 0, "act"), ("xo", 1, "act")]


def last_fills():
    fills = [("f", 0, "dve"), ("f", 1, "dve"), ("m3", 0, "dve"), ("m3", 1, "dve")]
    fills += [("qk", g, "act") for g in range(G)] + [("t", 0, "dve"), ("v", 0, "act"), ("s", 0, "dve"), ("t", 1, "dve")]
    for g in range(G):
        fills += [("o", g, "act")]
        if g + 1 < G:
            fills += [("s", g + 1, "dve")]
        fills += [("w", g, "dve")]
        if g + 1 < G:
            fills += [("v", g + 1, "act")]
        if g + 2 < G:
            fills += [("t", g + 2, "dve")]
    return fills + [("xo", 0, "act"), ("xo", 1, "act")]


class Ring:

    def __init__(self, fills, banks, filled, emptied, lead=0, only=None):
        self.fills, self.banks, self.filled_sem, self.emptied_sem = fills, banks, filled, emptied
        self.only = only
        self.lead = lead
        self.ordinal = {f[:2]: k + 1 for k, f in enumerate(fills)}
        self.who = {f[:2]: f[2] for f in fills}
        self.per = {w: sum(f[2] == w for f in fills) for w in ("act", "dve")}
        first = fills[len(fills) - (lead or len(banks)):] if only is None else []
        self.ahead = {w: sum(f[2] == w for f in first) for w in ("act", "dve")}
        self.nth = {}
        for w in ("act", "dve"):
            for k, f in enumerate([f for f in fills if f[2] == w]):
                self.nth[f[:2]] = k + 1
        self.next = 0

    def bank(self, name, i):
        return self.banks[(self.ordinal[(name, i)] - 1 - len(self.fills)) % len(self.banks)]

    def filled(self, turn, name, i):
        return (0 if self.only is not None else turn * len(self.fills)) + (self.ordinal[(name, i)] + self.lead)

    def emptied(self, turn, name, i):
        return (0 if self.only is not None else turn * self.per[self.who[(name, i)]]) + (self.nth[(name, i)] + self.ahead[self.who[(name, i)]])

    def wait_filled(self, eng, turn, name, i):
        eng.wait_ge(self.filled_sem, self.filled(turn, name, i))
        return self.bank(name, i)

    def wait_emptied(self, eng, turn, name, i):
        eng.wait_ge(self.emptied_sem[self.who[(name, i)]], self.emptied(turn, name, i))

    def wait_free(self, eng, turn, name, i):
        k = self.ordinal[(name, i)] - 1
        same = [j for j in range(len(self.fills)) if (j - k) % len(self.banks) == 0 and j < k]
        if same:
            self.wait_emptied(eng, turn, *self.fills[same[-1]][:2])
        elif self.only is None:
            mine = self.bank(name, i)
            before = [f[:2] for f in self.fills if self.bank(*f[:2]) is mine]
            self.wait_emptied(eng, turn - 1, *before[-1])
        return self.bank(name, i)


CHAIN1, CHAIN2 = 20, 23


def build(nc, A, out):
    with ExitStack() as ctx:
        def sb(name, shape, dt=F32):
            return ctx.enter_context(nc.sbuf_tensor(name, shape, dt))

        def sem(name, per=0):
            return Signal(ctx.enter_context(nc.semaphore(name)), per)

        bank = [ctx.enter_context(nc.psum_tensor(f"bank{i}", [P, 512], F32)) for i in range(8)]
        y_bank = bank[4:6]

        x_feat = sb("x_feat", [P, C, T, B])
        w_ring = sb("w_ring", [P, 2, UNIT, 2, PIECE], F32R)
        xm_high, xm_low = sb("xm_high", [P, C, LOT], F32R), sb("xm_low", [P, C, LOT], F32R)
        w_out = sb("w_out", [P, H, D])
        w_f1 = sb("w_f1", [P, C, MLP])
        w_f2 = sb("w_f2", [P, MLP // P, D])
        w_qkv2 = sb("w_qkv2", [P, C, 3 * D])
        w_out2 = sb("w_out2", [P, C, D])
        mod = sb("mod", [P, 16, B])
        col = sb("col", [P, N_ROWS])
        bsum = sb("bsum", [P, 4])
        ident = sb("ident", [P, P])
        k_mask = sb("k_mask", [P, HC])
        minus_half = sb("minus_half", [P, 2 * H])

        ARENA = 21120
        arena = sb("arena", [P, ARENA])

        def view(name, at, size):
            assert at + size <= ARENA, name
            return arena[:, at:at + size]

        kept = view("kept", 10752, C * (D + B))
        coupT = kept[:, 0:C * D].rearrange("p (c n) -> p c n", c=C)
        condT = kept[:, C * D:].rearrange("p (c b) -> p c b", c=C)
        x_rows = view("x_rows", 0, T * D).rearrange("p (t d) -> p t d", t=T)
        ada_w = view("ada_w", 16384, 3072).rearrange("p (c n) -> p c n", c=C)
        w_emb = view("w_emb", 19456, 1024).rearrange("p (c n) -> p c n", c=C)
        coup_rows = view("coup_rows", 20480, 512).rearrange("p (c n) -> p c n", c=C)
        w_ih = view("w_ih", 11520, 1536).rearrange("p (c n) -> p c n", c=C)
        w_hh = view("w_hh", 13056, 1536).rearrange("p (c n) -> p c n", c=C)
        cond = view("cond", 15872, 256)
        rows = view("rows", 16128, 128)
        h_buf = view("h_buf", 0, 512).rearrange("p (s c b) -> p s c b", s=2, c=C)
        gate_r = view("gate_r", 512, 256).rearrange("p (c b) -> p c b", c=C)
        gate_z = view("gate_z", 768, 256).rearrange("p (c b) -> p c b", c=C)
        one_z = view("one_z", 1024, 256).rearrange("p (c b) -> p c b", c=C)
        z_h = view("z_h", 1280, 256).rearrange("p (c b) -> p c b", c=C)
        pre_n = view("pre_n", 1536, 256).rearrange("p (c b) -> p c b", c=C)
        cand = view("cand", 1792, 256).rearrange("p (c b) -> p c b", c=C)
        plain = [view("plain0", 2048, PIECES // 2 * PIECE), view("plain1", 14592, PIECES // 2 * PIECE)]
        split_out = view("split_out", 8192, 4 * PIECE).rearrange("p (s a n) -> p s a n", s=2, a=2).bitcast(F32R)
        no_low = view("no_low", 10240, PIECE)
        x0_tok = view("x0_tok", 0, 1024).rearrange("p (g d) -> p g d", g=G)
        xm = view("xm", 6144, 1024).rearrange("p (c n) -> p c n", c=C)
        xm_sum = view("xm_sum", 11776, 1024).rearrange("p (c n) -> p c n", c=C)
        qT = view("qT", 2048, 2048).rearrange("p (h n) -> p h n", h=QUAD)
        kT = view("kT", 4096, 2048).rearrange("p (h n) -> p h n", h=QUAD)
        hT = view("hT", 2048, 4096).rearrange("p (m n) -> p m n", m=MLP // P)
        v_tok = view("v_tok", 6144, 2048).rearrange("p (g n) -> p g n", g=G)
        yT = view("yT", 6144, 1024).rearrange("p (c n) -> p c n", c=C)
        x_tok = view("x_tok", 7168, 1024).rearrange("p (g d) -> p g d", g=G)
        prob = view("prob", 8192, 512)
        probT = view("probT", 8704, 2048).rearrange("p (h n) -> p h n", h=H)
        oT = view("oT", 10752, 2048).rearrange("p (h n) -> p h n", h=QUAD)
        x_lot = view("x_lot", 10752, 1024).rearrange("p (c n) -> p c n", c=C)
        xn = view("xn", 10752, 1024).rearrange("p (g d) -> p g d", g=G)
        xn3 = view("xn3", 11776, 1024).rearrange("p (g d) -> p g d", g=G)
        x2_tok = view("x2_tok", 12800, 1024).rearrange("p (g d) -> p g d", g=G)
        xm3 = view("xm3", 1024, 1024).rearrange("p (c n) -> p c n", c=C)
        qk2 = view("qk2", 13824, 2048).rearrange("p (g n) -> p g n", g=G)
        q2T = view("q2T", 15872, 512).rearrange("p (s c n) -> p s c n", s=2, c=C)
        prob2 = view("prob2", 16384, 512)
        qk_sq = prob2
        k_wide = view("k_wide", 16896, 2048).rearrange("p (c b h t) -> p c b h t", c=C, b=GB, h=HC)
        V_WIDE = 18944
        v_wide = view("v_wide", V_WIDE, H * T).rearrange("p (h n) -> p h n", h=H)
        q_of = [view(f"q{i}", 256 * i, 256).rearrange("p (c b) -> p c b", c=C) for i in range(4)]
        p_of = [view(f"p{i}", 1024 + 256 * i, 256).rearrange("p (c b) -> p c b", c=C) for i in range(4)]
        names = ("drive0", "drive1", "tanh", "sq", "v", "base", "q_rise", "q_rise3", "q_twice3", "q_part3", "q_raw",
                 "p_fall", "p_rest", "p_rise", "p_rise3", "p_twice3", "p_part3", "p_raw", "outT")
        net = {n: view(n, 2048 + 256 * k, 256).rearrange("p (c b) -> p c b", c=C) for k, n in enumerate(names)}
        drive_of = (net["drive0"], net["drive1"])
        minus_ident = view("minus_ident", 7424, P)
        out_rows = view("out_rows", 8192, 256)

        o2T = sb("o2T", [P, C, P])
        tick, pool_tick = sb("tick", [P, 4]), sb("pool_tick", [P, 2])
        stats = sb("stats", [P, G, 6])
        mean_var = sb("mean_var", [P, G, 2])
        spread = sb("spread", [P, G])
        rstd = sb("rstd", [P, G])
        stats3, mean_var3, spread3, rstd3 = (sb(n, s) for n, s in (("stats3", [P, G, 6]), ("mean_var3", [P, G, 2]), ("spread3", [P, G]), ("rstd3", [P, G])))
        soft_max = sb("soft_max", [P, 2, 16])
        soft_sum = sb("soft_sum", [P, 2, 16])
        soft_inv = sb("soft_inv", [P, 2, 16])
        ss2 = sb("ss2", [P, G, 2 * H])
        rstd2 = sb("rstd2", [P, G, 2 * H])

        cond_in, rows_in, ada_in, emb_in, coup_in = (sem(n) for n in ("cond_in", "rows_in", "ada_in", "emb_in", "coup_in"))
        gru_in = sem("gru_in")
        x_in = [sem(f"x_in{i}") for i in range(4)]
        lot_w_in, lot_w2_in = sem("lot_w_in"), sem("lot_w2_in")
        consts, ident_step = sem("consts"), sem("ident_step")
        set_filled, set_act, set_dve = sem("set_filled"), sem("set_act"), sem("set_dve")
        set_chain = sem("set_chain")
        gates_ready = sem("gates_ready", 3)
        r_ready, z_ready, n_ready = sem("r_ready", 2), sem("z_ready", 2), sem("n_ready", 2)
        r_used = sem("r_used", 2)
        pre_ready, one_z_ready = sem("pre_ready", 2), sem("one_z_ready", 1)
        z_h_ready, prod_ready = sem("z_h_ready", 1), sem("prod_ready", 2)
        h_ready, x_added = sem("h_ready", 2), sem("x_added", 1)
        plain_in, kept_out, kept_in = sem("plain_in"), sem("kept_out"), sem("kept_in")
        high_split, low_split, split_sent = sem("high_split", 1), sem("low_split", 1), [sem(f"split_sent{i}", 16) for i in range(2)]
        unit_in = [sem(f"unit_in{i}", 16 * QUADS // 2) for i in range(2)]
        xm_ready, xm_high_ready = sem("xm_ready", C), sem("xm_high_ready", C)
        staged = sem("staged", C)
        fills1, fills2 = first_fills(), second_fills()
        ring1 = Ring(fills1, bank[0:4], sem("filled1").sem, {w: sem(w + "_emptied1").sem for w in ("act", "dve")}, lead=4)
        ring2 = Ring(fills2, bank[6:8], sem("filled2").sem, {w: sem(w + "_emptied2").sem for w in ("act", "dve")})
        ring3 = Ring(last_fills(), bank[0:4] + bank[6:8], sem("filled3").sem, {w: sem(w + "_emptied3").sem for w in ("act", "dve")}, only=LOTS - 1)

        def ring_of(r):
            return ring3 if isinstance(r, int) and r == LOTS - 1 else ring2

        spread_ready, rstd_ready, xn_ready, mod_ready = sem("spread_ready", 2), sem("rstd_ready", 2), sem("xn_ready", 2 * G), sem("mod_ready", 2 * C)
        spread3_ready, rstd3_ready, xn3_ready, mod3_ready = sem("spread3_ready", 1), sem("rstd3_ready", 1), sem("xn3_ready", G), sem("mod3_ready", C)
        exp_ready, probT_ready = sem("exp_ready", QUADS), sem("probT_ready", QUADS)
        exp2_ready, probT2_ready = sem("exp2_ready", G), sem("probT2_ready", G)
        oT_used, y_ready, yT_ready = sem("oT_used", QUADS - 1), sem("y_ready", 2), sem("yT_ready", 4)
        doubled = sem("doubled", 1)
        sq_ready, ss2_ready, rstd2_ready, qkn_ready = sem("sq_ready", G), sem("ss2_ready", G), sem("rstd2_ready", G), sem("qkn_ready", G)
        chain1, chain2 = sem("chain1", CHAIN1), sem("chain2", CHAIN2)
        zeroed = sem("zeroed")
        drive_ready = sem("drive_ready", C)
        tanh_ready, q_sq_ready, coupled, q_ready = (sem(n, 4 * C) for n in ("tanh_ready", "q_sq_ready", "coupled", "q_ready"))
        v_ready, base_ready = sem("v_ready", 4 * C), sem("base_ready", 4 * C)
        p_ready, p_fall_ready, p_rest_ready = sem("p_ready", 4), sem("p_fall_ready", 4), sem("p_rest_ready", 4)
        q_rise_ready, q_rise3_ready, q_twice3_ready, q_part3_ready = (
            sem(n, 1) for n in ("q_rise_ready", "q_rise3_ready", "q_twice3_ready", "q_part3_ready"))
        p_rise_ready, p_rise3_ready, p_twice3_ready, p_part3_ready, p_raw_ready = (
            sem(n, 1) for n in ("p_rise_ready", "p_rise3_ready", "p_twice3_ready", "p_part3_ready", "p_raw_ready"))
        q_raw_ready, minus_ready = sem("q_raw_ready", C), sem("minus_ready")
        outT_ready, turned, out_ready, out_sent, rows_free = sem("outT_ready", 1), sem("turned", 1), sem("out_ready", 1), sem("out_sent", 16), sem("rows_free", 1)

        def row(name):
            at, n = ROWS[name]
            return rows[at:at + n, :]

        def column(name, k=0):
            at, _ = ROWS[name]
            return col[:, at + k:at + k + 1]

        w_parts = nc.dram_tensor("w_parts", (P, PIECES, 2, PIECE), F32).ap()
        kept_rows = nc.dram_tensor("kept_rows", (P, C * (D + B)), F32).ap()

        block = ctx.enter_context(nc.Block())

        X_PAIRS = T // 2
        order = ["turn", "coup"] + [f"x{i}" for i in range(X_PAIRS)] + [f"mod{i}" for i in range(4)]
        set_bank = {n: bank[i % 8] for i, n in enumerate(order)}
        set_who = {n: ("act" if n.startswith("x") and int(n[1:]) % 2 else "dve") for n in order}
        set_ord = {n: i + 1 for i, n in enumerate(order)}
        set_emptied = {}
        for who in ("act", "dve"):
            for k, n in enumerate([n for n in order if set_who[n] == who]):
                set_emptied[n] = k + 1
        SET_ACT, SET_DVE = (sum(set_who[n] == w for n in order) for w in ("act", "dve"))

        @block.sync
        def _(sp):
            sp.dma_start(cond, A["cond_2048"]).then_inc(cond_in.sem, 16)
            names = {"b_ih": "L0_cond_b_ih", "b_hh": "L0_cond_b_hh", "ada_b": "L1_cond_ada_b", "qkv_b": "L1_cond_qkv_b",
                     "out_b": "L1_cond_out_b", "ffn_b1": "L1_cond_ffn_b1", "ffn_b2": "L1_cond_ffn_b2",
                     "b_emb": "L2_cond_b_emb", "g_norm": "L2_cond_g_norm", "bias": "L3_cond_bias"}
            for name, arg in names.items():
                sp.dma_start(row(name), A[arg].rearrange("(c p) -> c p", p=P)).then_inc(rows_in.sem, 16)
            for name, arg in (("g_q", "L2_cond_g_q"), ("g_k", "L2_cond_g_k")):
                src = A[arg].rearrange("(a o d) -> a o d", a=1, o=1).to_broadcast([1, HC, DH2])
                sp.dma_start(row(name).rearrange("a (h d) -> a h d", d=DH2), src).then_inc(rows_in.sem, 16)
            for i in range(4):
                sp.dma_start(x_rows[:, 8 * i:8 * i + 8, :], A["x"][:, 8 * i:8 * i + 8, :]).then_inc(x_in[i].sem, 16)
                if i == 0:
                    sp.dma_start(coup_rows, A["L3_cond_coupling"].rearrange("(c p) n -> p c n", p=P)).then_inc(coup_in.sem, 16)
            sp.dma_start(ada_w, A["L1_cond_ada_w"].rearrange("(c p) n -> p c n", p=P)).then_inc(ada_in.sem, 16)
            sp.dma_start(w_emb, A["L2_cond_W_emb"].rearrange("(c p) n -> p c n", p=P)).then_inc(emb_in.sem, 16)
            sp.dma_start(w_ih, A["L0_cond_W_ih"].rearrange("(c p) n -> p c n", p=P)).then_inc(gru_in.sem, 16)
            sp.dma_start(w_hh, A["L0_cond_W_hh"].rearrange("(c p) n -> p c n", p=P)).then_inc(gru_in.sem, 16)
            sp.dma_start(w_out2[:, :, :], A["L2_cond_W_out"].rearrange("(c p) n -> p c n", p=P)).then_inc(lot_w2_in.sem, 16)
            sp.dma_start(w_qkv2[:, :, :], A["L2_cond_W_qkv"].rearrange("(c p) n -> p c n", p=P)).then_inc(lot_w_in.sem, 16)
            sp.dma_start(w_out[:, :, :], A["L1_cond_out_w"].rearrange("(h p) n -> p h n", p=P)).then_inc(lot_w_in.sem, 16)
            sp.dma_start(w_f1[:, :, :], A["L1_cond_ffn_w1"].rearrange("(c p) n -> p c n", p=P)).then_inc(lot_w_in.sem, 16)
            sp.dma_start(w_f2[:, :, :], A["L1_cond_ffn_w2"].rearrange("(m p) n -> p m n", p=P)).then_inc(lot_w_in.sem, 16)
            sp.wait_ge(set_act.sem, SET_ACT)
            sp.wait_ge(set_dve.sem, SET_DVE)
            sp.dma_start(kept_rows, kept).then_inc(kept_out.sem, 16)
            w_src = A["L1_cond_qkv_w"].rearrange("(c p) n -> p c n", p=P)
            for q in range(QUADS):
                for part in range(PARTS):
                    at = (q % 2 * PARTS + part) * C * PIECE
                    at_col = part * INNER + q * PIECE
                    sp.dma_start(plain[q // 2][:, at:at + C * PIECE].rearrange("p (c n) -> p c n", c=C), w_src[:, :, at_col:at_col + PIECE])\
                      .then_inc(plain_in.sem, 16)
            for par in range(2):
                sp.sem_inc(split_sent[par].sem, 16)

            def unit(q):
                sp.dma_start(w_ring[:, q % 2, :, :, :].bitcast(F32), w_parts[:, q * UNIT:(q + 1) * UNIT, :, :]).then_inc(unit_in[q % 2].sem, 16)

            for half in range(2):
                with sp.Fori(0, PIECES // 4) as i:
                    for par in range(2):
                        t = 2 * i + (half * (PIECES // 2) + par)
                        sp.wait_ge(low_split.sem, low_split.at(t, 1))
                        sp.dma_start(w_parts[:, bass.ds(t, 1), :, :].rearrange("p t a n -> p (t a) n"), split_out[:, par, :, :].bitcast(F32))\
                          .then_inc(split_sent[par].sem, 16)
                for par in range(2):
                    sp.wait_ge(split_sent[par].sem, split_sent[par].at((half + 1) * (PIECES // 4), 16))
                if half == 0:
                    unit(0)
                    unit(1)
            sp.wait_ge(kept_out.sem, 16)

            def lot_units(s, last):
                for q in range(QUADS):
                    if last and q >= QUADS - 2:
                        break
                    ring1.wait_filled(sp, s, "v", G * q + G - 1)
                    unit((q + 2) % QUADS)

            with sp.Fori(0, LOTS - 1) as s:
                lot_units(s, False)
            lot_units(LOTS - 1, True)
            ring1.wait_filled(sp, LOTS - 1, "m2", 1)
            sp.dma_start(kept, kept_rows).then_inc(kept_in.sem, 16)
            sp.sem_inc(rows_free.sem, 1)
            with sp.Fori(0, T) as t:
                sp.wait_ge(out_ready.sem, out_ready.at(t, 1))
                sp.dma_start(out[:, bass.ds(t, 1), :].rearrange("b t d -> b (t d)"), out_rows).then_inc(out_sent.sem, 16)
                sp.wait_ge(out_sent.sem, out_sent.at(t, 16))
                sp.sem_inc(rows_free.sem, 1)
            sp.wait_ge(out_sent.sem, 16 * T)

        @block.gpsimd
        def _(pool):
            pool.memset(ident[:, :], 0.0).then_inc(ident_step.sem, 1)
            pool.memset(k_mask[:, :], 1.0).then_inc(ident_step.sem, 1)
            pool.memset(minus_half[:, :], -0.5).then_inc(ident_step.sem, 1)
            pool.wait_ge(ident_step.sem, 3)
            pool.affine_select(out=k_mask[:, :], in_=k_mask[:, :], compare_op=ALU.is_ge, fill=0.0,
                               base=0, pattern=[[-DH2, HC]], channel_multiplier=1).then_inc(ident_step.sem, 1)
            pool.wait_ge(ident_step.sem, 4)
            pool.affine_select(out=k_mask[:, :], in_=k_mask[:, :], compare_op=ALU.is_ge, fill=0.0,
                               base=DH2 - 1, pattern=[[DH2, HC]], channel_multiplier=-1).then_inc(consts.sem, 1)
            pool.affine_select(out=ident[:, :], in_=ident[:, :], compare_op=ALU.not_equal, fill=1.0,
                               base=0, pattern=[[-1, P]], channel_multiplier=1).then_inc(consts.sem, 1)

            pool.sem_inc(x_added.sem, 2)

            def add_state(t, par):
                pool.wait_ge(h_ready.sem, h_ready.at(t, 4))
                xt = x_feat[:, :, bass.ds(t, 1), :].rearrange("p c t b -> p c (t b)")
                pool.tensor_tensor(xt, xt, h_buf[:, 1 - par], ALU.add).then_inc(x_added.sem, 1)

            def take_wait(k):
                pool.tensor_tensor(pool_tick[:, k:k + 1], minus_half[:, 0:1], minus_half[:, 0:1], ALU.add)

            def split(t, turn, par, half, k):
                w = plain[half][:, bass.ds(k * PIECE, PIECE)]
                pool.wait_ge(split_sent[par].sem, split_sent[par].at(turn, 16))
                take_wait(0)
                pool.tensor_tensor(split_out[:, par, 0, :], w, no_low, ALU.subtract).then_inc(high_split.sem, 1)
                pool.wait_ge(high_split.sem, high_split.at(t, 1))
                take_wait(1)
                pool.tensor_tensor(split_out[:, par, 1, :], w, split_out[:, par, 0, :].bitcast(F32), ALU.subtract).then_inc(low_split.sem, 1)

            with pool.Fori(0, (T - PIECES) // 2) as i:
                for par in range(2):
                    add_state(i * 2 + par, par)
            pool.memset(no_low, 0.0).then_inc(ident_step.sem, 1)
            pool.wait_ge(ident_step.sem, 5)
            pool.wait_ge(plain_in.sem, 16 * QUADS * PARTS)
            for half in range(2):
                with pool.Fori(0, PIECES // 4) as i:
                    for par in range(2):
                        add_state(i * 2 + (half * (PIECES // 2) + T - PIECES + par), par)
                        split(i * 2 + (half * (PIECES // 2) + par), i + half * (PIECES // 4), par, half, i * 2 + par)

            pool.wait_ge(x_added.sem, T + 2)
            def power(src, dst, dst_ready):
                n = src.shape[1]
                pool.tensor_tensor(dst, src, minus_half[:, 0:n], ALU.pow).then_inc(dst_ready.sem, 1)

            def lead_in(s):
                pool.wait_ge(spread_ready.sem, spread_ready.at(s, 1))
                power(spread[:, :], rstd[:, :], rstd_ready)

            def lot(s, r, ahead):
                if r is not None:
                    pool.wait_ge(spread3_ready.sem, spread3_ready.at(r, 1))
                    power(spread3[:, :], rstd3[:, :], rstd3_ready)
                    for g in range(G):
                        pool.wait_ge(ss2_ready.sem, ss2_ready.at(r, g + 1))
                        power(ss2[:, g, :], rstd2[:, g, :], rstd2_ready)
                if s is not None:
                    pool.wait_ge(spread_ready.sem, spread_ready.at(s, 2))
                    power(spread[:, :], rstd[:, :], rstd_ready)
                    if r is not None:
                        pool.wait_ge(ring_of(r).filled_sem, ring_of(r).filled(r, "xo", 1))
                    pool.tensor_tensor(x2_tok, x0_tok, x_tok, ALU.add).then_inc(doubled.sem, 1)
                if ahead is not None:
                    lead_in(ahead)

            lead_in(0)
            for par in range(2):
                pool.wait_ge(split_sent[par].sem, split_sent[par].at(PIECES // 2, 16))
            pool.memset(probT, 0.0).then_inc(zeroed.sem, 1)
            pool.memset(v_wide, 0.0).then_inc(zeroed.sem, 1)
            pool.wait_ge(zeroed.sem, 2)
            lot(0, None, 1)
            with pool.Fori(1, LOTS - 1) as s:
                lot(s, s - 1, s + 1)
            lot(LOTS - 1, LOTS - 2, None)
            lot(None, LOTS - 1, None)

            def sum_out(t):
                pool.wait_ge(q_ready.sem, q_ready.at(t, 4 * C + C))
                xt = x_feat[:, :, bass.ds(t, 1), :].rearrange("p c t b -> p c (t b)")
                pool.tensor_tensor(net["outT"], xt, q_of[0], ALU.add).then_inc(outT_ready.sem, 1)

            def rest(t, i):
                pool.wait_ge(p_fall_ready.sem, p_fall_ready.at(t, i + 1))
                pool.tensor_tensor(net["p_rest"], net["p_fall"], p_of[0] if i < 3 else net["p_part3"], ALU.add).then_inc(p_rest_ready.sem, 1)

            def net_step(t, before):
                rest(t, 0)
                if before is not None:
                    sum_out(before)
                rest(t, 1)
                pool.tensor_tensor(net["p_rise"], p_of[1], p_of[0], ALU.subtract).then_inc(p_rise_ready.sem, 1)
                pool.wait_ge(q_ready.sem, q_ready.at(t, C + C))
                pool.tensor_tensor(net["q_rise"], q_of[1], q_of[0], ALU.subtract).then_inc(q_rise_ready.sem, 1)
                rest(t, 2)
                pool.wait_ge(p_rise3_ready.sem, p_rise3_ready.at(t, 1))
                pool.wait_ge(p_twice3_ready.sem, p_twice3_ready.at(t, 1))
                pool.tensor_tensor(net["p_part3"], net["p_rise3"], net["p_twice3"], ALU.add).then_inc(p_part3_ready.sem, 1)
                pool.wait_ge(p_part3_ready.sem, p_part3_ready.at(t, 1))
                rest(t, 3)
                pool.wait_ge(q_rise3_ready.sem, q_rise3_ready.at(t, 1))
                pool.wait_ge(q_twice3_ready.sem, q_twice3_ready.at(t, 1))
                pool.tensor_tensor(net["q_part3"], net["q_rise3"], net["q_twice3"], ALU.add).then_inc(q_part3_ready.sem, 1)

            net_step(0, None)
            with pool.Fori(0, T // 2 - 1) as i:
                net_step(2 * i + 1, 2 * i)
                net_step(2 * i + 2, 2 * i + 1)
            net_step(T - 1, T - 2)
            sum_out(T - 1)

        def set_fill(pe, name):
            at = order.index(name)
            if at >= 8:
                before = order[at - 8]
                pe.wait_ge({"act": set_act, "dve": set_dve}[set_who[before]].sem, set_emptied[before])
            return set_bank[name]

        @block.tensor
        def _(pe):
            mm = pe.matmul
            pe.wait_ge(consts.sem, 2)
            pe.wait_ge(cond_in.sem, 16)
            pe.wait_ge(rows_in.sem, 16 * 12)
            ps = set_fill(pe, "turn")
            for c in range(C):
                pe.transpose(ps[:, c * P:(c + 1) * P], cond[:, c * P:(c + 1) * P], ident[:, :])
            pe.transpose(ps[:, 256:256 + N_ROWS], rows[0:N_ROWS, :], ident[0:N_ROWS, 0:N_ROWS]).then_inc(set_filled.sem, 1)
            pe.wait_ge(coup_in.sem, 16)
            ps = set_fill(pe, "coup")
            for c in range(C):
                for j in range(C):
                    last = pe.transpose(ps[:, c * D + j * P:c * D + (j + 1) * P], coup_rows[:, j, c * P:(c + 1) * P], ident[:, :])
            last.then_inc(set_filled.sem, 1)
            for i in range(X_PAIRS):
                if i % 4 == 0:
                    pe.wait_ge(x_in[i // 4].sem, 16)
                ps = set_fill(pe, f"x{i}")
                for tt in range(2):
                    for c in range(C):
                        last = pe.transpose(ps[:, (c * 2 + tt) * P:(c * 2 + tt + 1) * P], x_rows[:, 2 * i + tt, c * P:(c + 1) * P], ident[:, :])
                last.then_inc(set_filled.sem, 1)
            pe.wait_ge(ada_in.sem, 16)
            pe.wait_ge(emb_in.sem, 16)
            for j in range(16):
                if j % 4 == 0:
                    ps = set_fill(pe, f"mod{j // 4}")
                for c in range(C):
                    w = ada_w[:, c, j * P:(j + 1) * P] if j < 12 else w_emb[:, c, (j - 12) * P:(j - 11) * P]
                    last = mm(ps[:, (j % 4) * B:(j % 4 + 1) * B], w, condT[:, c, :], start=(c == 0), stop=(c == C - 1))
                if j % 4 == 3:
                    last.then_inc(set_filled.sem, 1)

            pe.wait_ge(gru_in.sem, 32)
            pe.wait_ge(set_act.sem, SET_ACT)
            pe.wait_ge(set_dve.sem, SET_DVE)

            def gru_input(par, t):
                xt = lambda c: x_feat[:, c, bass.ds(t, 1), :].rearrange("p t b -> p (t b)") if not isinstance(t, int) else x_feat[:, c, t, :]
                for k, j0 in ((0, 0), (1, 2), (2, 4)):
                    for j in range(2):
                        for c in range(C):
                            last = mm(bank[4 * par + k][:, j * B:(j + 1) * B], w_ih[:, c, (j0 + j) * P:(j0 + j + 1) * P], xt(c),
                                      start=(j == 0 and c == 0), stop=(k == 2 and j == 1 and c == 1), skip_group_check=True)
                return last

            def gru_hidden(par, t):
                pe.wait_ge(h_ready.sem, h_ready.at(t, 2))
                for k, j0 in ((0, 0), (3, 4), (1, 2)):
                    for c in range(C):
                        for j in range(2):
                            last = mm(bank[4 * par + k][:, j * B:(j + 1) * B], w_hh[:, c, (j0 + j) * P:(j0 + j + 1) * P], h_buf[:, par, c, :],
                                      start=(k == 3 and j == 0 and c == 0), stop=(j == 1 and c == 1), skip_group_check=True)
                    last.then_inc(gates_ready.sem, 1)

            gru_input(0, 0)
            with pe.Fori(0, T // 2 - 1) as i:
                gru_hidden(0, i * 2)
                gru_input(1, i * 2 + 1)
                gru_hidden(1, i * 2 + 1)
                gru_input(0, i * 2 + 2)
            gru_hidden(0, T - 2)
            gru_input(1, T - 1)
            gru_hidden(1, T - 1)

            pe.wait_ge(lot_w_in.sem, 16 * 4)
            pe.wait_ge(set_dve.sem, SET_DVE + 1)
            def begin(ring, s, name, i):
                if isinstance(s, int) and s < 0:
                    return ring.bank(name, i)
                return ring.wait_free(pe, s, name, i)

            def to_tokens(ring, s, name, src, ready, turn, before):
                for c in range(C):
                    pe.wait_ge(ready.sem, ready.at(turn, before + c + 1))
                    for j in range(2):
                        ps = begin(ring, s, name, j) if c == 0 else ring.bank(name, j)
                        for gg in range(2):
                            last = pe.transpose(ps[:, gg * D + c * P:gg * D + (c + 1) * P], src[:, c, (2 * j + gg) * P:(2 * j + gg + 1) * P], ident[:, :])
                        if c == C - 1:
                            last.then_inc(ring.filled_sem, 1)

            def to_features(ring, s, name, src, ready=None, turn=None, before=0):
                for g in range(G):
                    if ready is not None:
                        pe.wait_ge(ready.sem, ready.at(turn, before + g + 1))
                    for c in range(C):
                        ps = begin(ring, s, name, c) if g == 0 else ring.bank(name, c)
                        last = pe.transpose(ps[:, g * P:(g + 1) * P], src[:, g, c * P:(c + 1) * P], ident[:, :])
                        if g == G - 1:
                            last.then_inc(ring.filled_sem, 1)

            def project_split(ps, wide, narrow):
                last_pass = (C - 1, 1, 0)
                for c in range(C):
                    for n, w in ((0, 0), (0, 1), (1, 0)):
                        last = mm(ps[:, :], narrow(c, n), wide(c, w), start=((c, n, w) == (0, 0, 0)), stop=((c, n, w) == last_pass))
                last.then_inc(ring1.filled_sem, 1)

            def xm_part(c, part, at=slice(0, LOT)):
                return (xm_low if part else xm_high)[:, c, at]

            def project(s, name, i, w):
                ps = begin(ring1, s, name, i)
                for c in range(C):
                    last = mm(ps[:, :], w[:, c, :], xm[:, c, :], start=(c == 0), stop=(c == C - 1))
                last.then_inc(ring1.filled_sem, 1)

            def q_and_k(s, q, heads=range(QUAD)):
                pe.wait_ge(unit_in[q % 2].sem, unit_in[q % 2].at(s, 16 * (q // 2 + 1)))
                for h in heads:
                    for part, name in ((0, "q"), (1, "k")):
                        ps = begin(ring1, s, name, QUAD * q + h)
                        project_split(ps, xm_part, lambda c, n: w_ring[:, q % 2, part * C + c, n, h * DH1:(h + 1) * DH1])

            def values(s, q):
                for g in range(G):
                    ps = begin(ring1, s, "v", G * q + g)
                    project_split(ps, lambda c, n: w_ring[:, q % 2, 2 * C + c, n, :], lambda c, n: xm_part(c, n, slice(g * P, (g + 1) * P)))

            def scores(s, q):
                ring1.wait_emptied(pe, s, "k", QUAD * q + QUAD - 1)
                ps = begin(ring1, s, "s", q)
                for g in range(G):
                    for h in range(QUAD):
                        for b in range(GB):
                            tok = slice(g * P + b * T, g * P + (b + 1) * T)
                            at_col = (g * QUAD + h) * T
                            last = mm(ps[b * T:(b + 1) * T, at_col:at_col + T], qT[:, h, tok], kT[:, h, tok], start=True, stop=True)
                last.then_inc(ring1.filled_sem, 1)

            def attend(s, q):
                pe.wait_ge(probT_ready.sem, probT_ready.at(s, q + 1))
                ring1.wait_emptied(pe, s, "v", G * q + G - 1)
                for h in range(QUAD):
                    ps = begin(ring1, s, "o", QUAD * q + h)
                    for g in range(G):
                        last = mm(ps[:, g * P:(g + 1) * P], v_tok[:, g, h * DH1:(h + 1) * DH1], probT[:, g * QUAD + h, :], start=True, stop=True)
                    last.then_inc(ring1.filled_sem, 1)

            def project_out(s, q):
                for h in range(QUAD):
                    ring1.wait_emptied(pe, s, "o", QUAD * q + h)
                    for c in range(C):
                        last = mm(y_bank[c][:, :], w_out[:, QUAD * q + h, c * P:(c + 1) * P], oT[:, h, :],
                                  start=(q == 0 and h == 0), stop=(q == QUADS - 1 and h == QUAD - 1))
                last.then_inc((oT_used if q < QUADS - 1 else y_ready).sem, 1)

            def mlp(s, ahead):
                pe.wait_ge(mod_ready.sem, mod_ready.at(s, C + 1))
                first = []
                for m in range(2):
                    first.append(begin(ring1, s, "h", m))
                    mm(first[m][:, :], w_f1[:, 0, m * P:(m + 1) * P], xm[:, 0, :], start=True, stop=False)
                pe.wait_ge(mod_ready.sem, mod_ready.at(s, 2 * C))
                for m in range(MLP // P):
                    if m < 2:
                        mm(first[m][:, :], w_f1[:, 1, m * P:(m + 1) * P], xm[:, 1, :], start=False, stop=True).then_inc(ring1.filled_sem, 1)
                    else:
                        project(s, "h", m, w_f1[:, :, m * P:(m + 1) * P])
                if ahead is not None:
                    lead_tokens(ahead)
                for m in range(MLP // P):
                    ring1.wait_emptied(pe, s, "h", m)
                    for c in range(C):
                        last = mm(y_bank[c][:, :], w_f2[:, m, c * P:(c + 1) * P], hT[:, m, :], start=(m == 0), stop=(m == MLP // P - 1))
                    if m == 3 and ahead is not None:
                        lead_features(ahead)
                last.then_inc(y_ready.sem, 1)

            def lead_tokens(s):
                to_tokens(ring1, s - 1, "xin", x_lot, staged, s, 0)

            def lead_features(s):
                to_features(ring1, s - 1, "m1", xn, xn_ready, s, 0)

            def project2(r):
                for g in range(G):
                    ps = begin(ring_of(r), r, "qk", g)
                    for c in range(C):
                        last = mm(ps[:, :], xm3[:, c, g * P:(g + 1) * P], w_qkv2[:, c, 0:2 * D], start=(c == 0), stop=(c == C - 1))
                    last.then_inc(ring_of(r).filled_sem, 1)

            def turn2(r, g):
                pe.wait_ge(qkn_ready.sem, qkn_ready.at(r, g + 1))
                ps = begin(ring_of(r), r, "t", g)
                for k in range(4):
                    last = pe.transpose(ps[:, k * P:(k + 1) * P], qk2[:, g, k * P:(k + 1) * P], ident[:, :])
                last.then_inc(ring_of(r).filled_sem, 1)

            def values2(r, g):
                ps = begin(ring_of(r), r, "v", g)
                for c in range(C):
                    last = mm(ps[:, 0:D], xm3[:, c, g * P:(g + 1) * P], w_qkv2[:, c, 2 * D:3 * D], start=(c == 0), stop=(c == C - 1))
                last.then_inc(ring_of(r).filled_sem, 1)

            def scores2(r, g):
                ring_of(r).wait_emptied(pe, r, "t", g)
                ps = begin(ring_of(r), r, "s", g)
                for c in range(C):
                    for b in range(GB):
                        last = mm(ps[b * T:(b + 1) * T, c * D:(c + 1) * D], q2T[:, g % 2, c, b * T:(b + 1) * T],
                                  k_wide[:, c, b, :, :].rearrange("p h t -> p (h t)"), start=True, stop=True)
                last.then_inc(ring_of(r).filled_sem, 1)

            def attend2(r, g, chunks=range(C)):
                for c in chunks:
                    if c == 0:
                        pe.wait_ge(probT2_ready.sem, probT2_ready.at(r, g + 1))
                        ring_of(r).wait_emptied(pe, r, "v", g)
                        ps = begin(ring_of(r), r, "o", g)
                    else:
                        ps = ring_of(r).bank("o", g)
                    for k in range(2):
                        for pair in range(HC // 2):
                            h = c * HC + 2 * pair + k
                            last = mm(ps[pair * T:(pair + 1) * T, c * P:(c + 1) * P], v_wide[:, h, :], probT[:, h, :],
                                      start=(k == 0), stop=(k == 1), skip_group_check=True)
                if C - 1 in chunks:
                    last.then_inc(ring_of(r).filled_sem, 1)

            def project_out2(r, g):
                ring_of(r).wait_emptied(pe, r, "o", g)
                ps = begin(ring_of(r), r, "w", g)
                for c in range(C):
                    last = mm(ps[:, 0:D], o2T[:, c, :], w_out2[:, c, :], start=(c == 0), stop=(c == C - 1))
                last.then_inc(ring_of(r).filled_sem, 1)

            def leave2(r):
                ring_of(r).wait_emptied(pe, r, "w", G - 1)
                to_features(ring_of(r), r, "xo", x2_tok)

            def lot_alone(r):
                ring2.wait_emptied(pe, r - 1, "xo", 1)
                to_tokens(ring3, r, "f", yT, yT_ready, r, C)
                to_features(ring3, r, "m3", xn3, xn3_ready, r, 0)
                pe.wait_ge(mod3_ready.sem, mod3_ready.at(r, C))
                project2(r)
                turn2(r, 0)
                values2(r, 0)
                scores2(r, 0)
                turn2(r, 1)
                for g in range(G):
                    attend2(r, g)
                    if g + 1 < G:
                        scores2(r, g + 1)
                    project_out2(r, g)
                    if g + 1 < G:
                        values2(r, g + 1)
                    if g + 2 < G:
                        turn2(r, g + 2)
                leave2(r)

            def lot(s, r, ahead):
                second = r is not None
                pe.wait_ge(mod_ready.sem, mod_ready.at(s, C))
                q_and_k(s, 0, range(1))
                if second:
                    to_tokens(ring2, r, "f", yT, yT_ready, r, C)
                q_and_k(s, 0, range(1, QUAD))
                if second:
                    to_features(ring2, r, "m3", xn3, xn3_ready, r, 0)
                values(s, 0)
                if second:
                    pe.wait_ge(mod3_ready.sem, mod3_ready.at(r, C))
                    project2(r)
                for q in range(QUADS):
                    scores(s, q)
                    if second and q > 0:
                        attend2(r, q - 1)
                    if q > 0:
                        project_out(s, q - 1)
                    if second and q > 0:
                        project_out2(r, q - 1)
                    if q < QUADS - 1:
                        q_and_k(s, q + 1)
                    if second:
                        turn2(r, q)
                        values2(r, q)
                    attend(s, q)
                    if second:
                        scores2(r, q)
                    if q < QUADS - 1:
                        values(s, q + 1)
                project_out(s, QUADS - 1)
                if second:
                    attend2(r, QUADS - 1, range(1))
                to_tokens(ring1, s, "y", yT, yT_ready, s, 0)
                if second:
                    attend2(r, QUADS - 1, range(1, C))
                    project_out2(r, QUADS - 1)
                to_features(ring1, s, "m2", xn, xn_ready, s, G)
                if second:
                    leave2(r)
                mlp(s, ahead)

            lead_tokens(0)
            lead_features(0)
            lot(0, None, 1)
            with pe.Fori(1, LOTS - 1) as s:
                lot(s, s - 1, s + 1)
            lot(LOTS - 1, LOTS - 2, None)
            lot_alone(LOTS - 1)

            ring3.wait_emptied(pe, LOTS - 1, "xo", 1)
            def turn_out(t):
                pe.wait_ge(outT_ready.sem, outT_ready.at(t, 1))
                for c in range(C):
                    last = pe.transpose(bank[4][:, c * P:(c + 1) * P], net["outT"][:, c, :], ident[:, :])
                last.then_inc(turned.sem, 1)

            def net_step(t, par, before):
                for i in range(4):
                    pair = bank[2 * (i % 2):2 * (i % 2) + 2]
                    if i == 0:
                        pe.wait_ge(drive_ready.sem, drive_ready.at(t, C))
                    for j in range(C):
                        mm(pair[j][:, 0:B], ident[:, :], drive_of[par][:, j, :], start=True, stop=False, skip_group_check=True)
                    pe.wait_ge(p_ready.sem, p_ready.at(t, i + 1))
                    for j in range(C):
                        mm(pair[j][:, 0:B], minus_ident, p_of[i][:, j, :], start=False, stop=False, skip_group_check=True)
                    for k in range(C):
                        pe.wait_ge(tanh_ready.sem, tanh_ready.at(t, C * i + k + 1))
                        for j in range(C):
                            last = mm(pair[j][:, 0:B], coupT[:, k, j * P:(j + 1) * P], net["tanh"][:, k, :], start=False, stop=(k == C - 1), skip_group_check=True)
                            if k == C - 1:
                                last.then_inc(coupled.sem, 1)
                    if i == 1 and before is not None:
                        turn_out(before)

            pe.wait_ge(minus_ready.sem, 1)
            pe.wait_ge(kept_in.sem, 16)
            net_step(0, 0, None)
            with pe.Fori(0, T // 2 - 1) as i:
                net_step(2 * i + 1, 1, 2 * i)
                net_step(2 * i + 2, 0, 2 * i + 1)
            net_step(T - 1, 1, T - 2)
            pe.wait_ge(out_ready.sem, T - 1)
            turn_out(T - 1)

        @block.scalar
        def _(act):
            def filled_set(name):
                act.wait_ge(set_filled.sem, set_ord[name])
                return set_bank[name]

            for i in range(1, X_PAIRS, 2):
                ps = filled_set(f"x{i}")
                act.activation(x_feat[:, :, 2 * i:2 * i + 2, :], ps[:, :].rearrange("p (c t b) -> p c t b", c=C, t=2), ACT.Copy).then_inc(set_act.sem, 1)

            act.wait_ge(set_dve.sem, SET_DVE)
            with act.Fori(0, T // 2) as i:
                for par in range(2):
                    t = i * 2 + par
                    act.wait_ge(gates_ready.sem, gates_ready.at(t, 1))
                    for c in range(C):
                        act.activation(gate_r[:, c, :], bank[4 * par][:, c * B:(c + 1) * B], ACT.Sigmoid, bias=bsum[:, c:c + 1]).then_inc(r_ready.sem, 1)
                    act.wait_ge(gates_ready.sem, gates_ready.at(t, 3))
                    for c in range(C):
                        act.activation(gate_z[:, c, :], bank[4 * par + 1][:, c * B:(c + 1) * B], ACT.Sigmoid, bias=bsum[:, 2 + c:3 + c]).then_inc(z_ready.sem, 1)
                    for c in range(C):
                        act.wait_ge(pre_ready.sem, pre_ready.at(t, c + 1))
                        act.activation(cand[:, c, :], pre_n[:, c, :], ACT.Tanh).then_inc(n_ready.sem, 1)
                        if c == 0:
                            act.wait_ge(z_ready.sem, z_ready.at(t, 2))
                            act.activation(one_z, gate_z, ACT.Copy, scale=-1.0, bias=1.0).then_inc(one_z_ready.sem, 1)

            act.wait_ge(x_added.sem, T + 2)
            act.sem_inc(ring2.emptied_sem["act"], 2)

            def empty(ring, s, name, i, dst, width, func, **kw):
                ps = ring.wait_filled(act, s, name, i)
                act.activation(dst, ps[:, 0:width], func, **kw).then_inc(ring.emptied_sem["act"], 1)

            def stage(s):
                if not isinstance(s, int) or s > 0:
                    act.wait_ge(ring1.filled_sem, ring1.filled(s - 1, "m2", 1))
                    act.activation(tick[:, 3:4], minus_half[:, 0:1], ACT.Copy)
                for c in range(C):
                    act.activation(x_lot[:, c, :].rearrange("p (b t) -> p b t", t=T),
                                   x_feat[:, c, :, bass.ds(s * LOT_B, LOT_B)].rearrange("p t b -> p b t"), ACT.Copy).then_inc(staged.sem, 1)

            def lead(s):
                if not isinstance(s, int) or s > 0:
                    act.wait_ge(doubled.sem, doubled.at(s - 1, 1))
                for j in range(2):
                    empty(ring1, s - 1, "xin", j, x0_tok[:, 2 * j:2 * j + 2, :].rearrange("p g d -> p (g d)"), 512, ACT.Copy)
                for c in range(C):
                    act.wait_ge(xm_ready.sem, xm_ready.at(s, c + 1))
                    act.activation(xm_high[:, c, :], xm_sum[:, c, :], ACT.Copy).then_inc(xm_high_ready.sem, 1)

            def q_and_k(s, q):
                if q > 0:
                    ring1.wait_filled(act, s, "s", q - 1)
                for h in range(QUAD * q, QUAD * q + QUAD):
                    for name, dst, k in (("q", qT, h), ("k", kT, H + h)):
                        empty(ring1, s, name, h, dst[:, h % QUAD, :], 512, ACT.Identity, bias=column("qkv_b", k))

            def values(s, q):
                for g in range(G):
                    empty(ring1, s, "v", G * q + g, v_tok[:, g, :], 512, ACT.Copy)

            def exps(prob, shifted, ready, width):
                act.wait_ge(*shifted)
                act.activation(prob, prob, ACT.Exp, scale=float(width) ** -0.5).then_inc(ready.sem, 1)

            def outputs(s, q):
                if q > 0:
                    act.wait_ge(oT_used.sem, oT_used.at(s, q))
                for h in range(QUAD * q, QUAD * q + QUAD):
                    empty(ring1, s, "o", h, oT[:, h % QUAD, :], 512, ACT.Identity, bias=column("qkv_b", 2 * H + h))

            def project2(r):
                for g in range(G):
                    empty(ring_of(r), r, "qk", g, qk2[:, g, :], 512, ACT.Copy)
                    ring_of(r).wait_emptied(act, r, "qk", g)
                    if g > 0:
                        act.wait_ge(ss2_ready.sem, ss2_ready.at(r, g))
                    act.activation(qk_sq, qk2[:, g, :], ACT.Square).then_inc(sq_ready.sem, 1)

            def values2(r, g):
                ps = ring_of(r).wait_filled(act, r, "v", g)
                for k in range(2):
                    own = arena[:, V_WIDE + k * (T + DH2):V_WIDE + k * (T + DH2) + H // 2 * 2 * T].rearrange("p (h n) -> p h n", n=2 * T)[:, :, 0:DH2]
                    ins = act.activation(own, ps[:, 0:D].rearrange("p (h k d) -> p h k d", k=2, d=DH2)[:, :, k, :], ACT.Copy)
                ins.then_inc(ring_of(r).emptied_sem["act"], 1)

            def outputs2(r, g):
                empty(ring_of(r), r, "o", g, o2T[:, :, :].rearrange("p c n -> p (c n)"), D, ACT.Copy)

            def leave2(r):
                for c in range(C):
                    ps = ring_of(r).wait_filled(act, r, "xo", c)
                    act.activation(tick[:, 1 + c:2 + c], minus_half[:, 0:1], ACT.Copy)
                    act.activation(x_feat[:, c, :, bass.ds(r * LOT_B, LOT_B)], ps[:, :].rearrange("p (b t) -> p t b", t=T), ACT.Copy)\
                       .then_inc(ring_of(r).emptied_sem["act"], 1)

            def lot_alone(r):
                project2(r)
                values2(r, 0)
                for g in range(G):
                    exps(prob2, (ring3.emptied_sem["dve"], ring3.emptied(r, "s", g)), exp2_ready, DH2)
                    if g > 0:
                        values2(r, g)
                    outputs2(r, g)
                leave2(r)

            def lot(s, r, ahead):
                if s is not None:
                    q_and_k(s, 0)
                    values(s, 0)
                if r is not None:
                    project2(r)
                for q in range(QUADS):
                    if s is not None:
                        exps(prob, (ring1.emptied_sem["dve"], ring1.emptied(s, "s", q)), exp_ready, DH1)
                    if r is not None and q > 0:
                        outputs2(r, q - 1)
                    if s is not None:
                        if q < QUADS - 1:
                            q_and_k(s, q + 1)
                        else:
                            outputs(s, q)
                    if r is not None:
                        values2(r, q)
                    if s is not None and q < QUADS - 1:
                        outputs(s, q)
                    if r is not None:
                        exps(prob2, (ring_of(r).emptied_sem["dve"], ring_of(r).emptied(r, "s", q)), exp2_ready, DH2)
                    if s is not None and q < QUADS - 1:
                        values(s, q + 1)
                if r is not None:
                    outputs2(r, QUADS - 1)
                    leave2(r)
                if ahead is not None:
                    stage(ahead)
                if s is not None:
                    for m in range(MLP // P):
                        empty(ring1, s, "h", m, hT[:, m, :], 512, ACT.Gelu, bias=column("ffn_b1", m))
                if ahead is not None:
                    lead(ahead)

            stage(0)
            lead(0)
            act.wait_ge(zeroed.sem, 2)
            lot(0, None, 1)
            with act.Fori(1, LOTS - 1) as s:
                lot(s, s - 1, s + 1)
            lot(LOTS - 1, LOTS - 2, None)
            lot_alone(LOTS - 1)

            ring3.wait_emptied(act, LOTS - 1, "xo", 1)

            def send_out(t):
                act.wait_ge(turned.sem, turned.at(t, 1))
                act.wait_ge(rows_free.sem, rows_free.at(t, 1))
                act.activation(out_rows, bank[4][:, 0:D], ACT.Copy).then_inc(out_ready.sem, 1)

            def drive(t, par):
                for c in range(C):
                    act.activation(drive_of[par][:, c, :], x_feat[:, c, bass.ds(t, 1), :].rearrange("p t b -> p (t b)"), ACT.Identity,
                                   bias=column("bias", c)).then_inc(drive_ready.sem, 1)

            def fall(t, i):
                act.wait_ge(p_ready.sem, p_ready.at(t, i + 1))
                act.activation(net["p_fall"], p_of[i], ACT.Copy, scale=(1 / 3 if i == 3 else 0.0) - STEP[i] * EPSILON * BETA,
                               bias=STEP[i] * EPSILON * ALPHA).then_inc(p_fall_ready.sem, 1)

            def net_step(t, par, before, ahead):
                for i in range(4):
                    for c in range(C):
                        act.wait_ge(q_ready.sem, q_ready.at(t, C * i + c + 1))
                        act.activation(net["tanh"][:, c, :], q_of[i][:, c, :], ACT.Tanh).then_inc(tanh_ready.sem, 1)
                        act.activation(net["sq"][:, c, :], q_of[i][:, c, :], ACT.Square).then_inc(q_sq_ready.sem, 1)
                    if i < 3:
                        fall(t, i + 1)
                    elif ahead is not None:
                        fall(ahead, 0)
                    if i == 0 and ahead is not None:
                        drive(ahead, 1 - par)
                    if i == 1:
                        act.activation(net["p_twice3"], p_of[2], ACT.Copy, scale=2 / 3).then_inc(p_twice3_ready.sem, 1)
                        act.wait_ge(p_rise_ready.sem, p_rise_ready.at(t, 1))
                        act.activation(net["p_rise3"], net["p_rise"], ACT.Copy, scale=1 / 3).then_inc(p_rise3_ready.sem, 1)
                    if i == 2:
                        act.activation(net["q_twice3"], q_of[2], ACT.Copy, scale=2 / 3).then_inc(q_twice3_ready.sem, 1)
                        act.wait_ge(q_rise_ready.sem, q_rise_ready.at(t, 1))
                        act.activation(net["q_rise3"], net["q_rise"], ACT.Copy, scale=1 / 3).then_inc(q_rise3_ready.sem, 1)
                    if i == 3 and before is not None:
                        send_out(before)

            act.activation(minus_ident, ident[:, :], ACT.Copy, scale=-1.0).then_inc(minus_ready.sem, 1)
            drive(0, 0)
            fall(0, 0)
            net_step(0, 0, None, 1)
            with act.Fori(0, T // 2 - 1) as i:
                net_step(2 * i + 1, 1, 2 * i, 2 * i + 2)
                net_step(2 * i + 2, 0, 2 * i + 1, 2 * i + 3)
            net_step(T - 1, 1, T - 2, None)
            send_out(T - 1)

        @block.vector
        def _(dve):
            chain = Chain(dve, set_chain.sem)
            link = chain.link

            def filled_set(name):
                dve.wait_ge(set_filled.sem, set_ord[name])
                return set_bank[name]

            ps = filled_set("turn")
            dve.wait_ge(consts.sem, 2)
            link(dve.tensor_copy(condT[:, :, :].rearrange("p c b -> p (c b)"), ps[:, 0:C * B]))
            dve.tensor_copy(col[:, :], ps[:, 256:256 + N_ROWS]).then_inc(set_dve.sem, 1)
            dve.wait_ge(set_dve.sem, 1)
            at_ih, at_hh = ROWS["b_ih"][0], ROWS["b_hh"][0]
            link(dve.tensor_tensor(bsum[:, :], col[:, at_ih:at_ih + 4], col[:, at_hh:at_hh + 4], ALU.add))
            link(dve.tensor_scalar(k_mask[:, :], k_mask[:, :], column("g_k"), None, ALU.mult))
            ps = filled_set("coup")
            dve.tensor_copy(coupT[:, :, :].rearrange("p c n -> p (c n)"), ps[:, :]).then_inc(set_dve.sem, 1)
            for i in range(0, X_PAIRS, 2):
                ps = filled_set(f"x{i}")
                dve.tensor_copy(x_feat[:, :, 2 * i:2 * i + 2, :], ps[:, :].rearrange("p (c t b) -> p c t b", c=C, t=2)).then_inc(set_dve.sem, 1)
            for j in range(16):
                if j % 4 == 0:
                    ps = filled_set(f"mod{j // 4}")
                src = ps[:, (j % 4) * B:(j % 4 + 1) * B]
                bias = column("ada_b", j) if j < 12 else column("b_emb", j - 12)
                if j // 2 * 2 in (SCALE1, SCALE2, SCALE3):
                    ins = dve.tensor_scalar(mod[:, j, :], src, bias, 1.0, ALU.add, ALU.add)
                else:
                    ins = dve.tensor_scalar(mod[:, j, :], src, bias, None, ALU.add)
                if j % 4 == 3:
                    ins.then_inc(set_dve.sem, 1)
                else:
                    link(ins)
            for c in range(C):
                link(dve.tensor_scalar(mod[:, SCALE3 + c, :], mod[:, SCALE3 + c, :], column("g_norm", c), None, ALU.mult))
            dve.wait_ge(set_act.sem, SET_ACT)
            for c in range(C):
                dve.tensor_copy(h_buf[:, 0, c, :], condT[:, c, :]).then_inc(h_ready.sem, 1)
            dve.wait_ge(lot_w2_in.sem, 16)
            for c in range(C):
                ins = dve.tensor_tensor(w_out2[:, c, c * P:(c + 1) * P], w_out2[:, c, c * P:(c + 1) * P], ident[:, :], ALU.add)
                if c == C - 1:
                    ins.then_inc(set_dve.sem, 1)
                else:
                    link(ins)

            with dve.Fori(0, T // 2) as i:
                for par in range(2):
                    t = i * 2 + par
                    dve.wait_ge(gates_ready.sem, gates_ready.at(t, 2))
                    for c in range(C):
                        dve.wait_ge(r_ready.sem, r_ready.at(t, c + 1))
                        dve.scalar_tensor_tensor(pre_n[:, c, :], bank[4 * par + 3][:, c * B:(c + 1) * B], column("b_hh", 4 + c), gate_r[:, c, :],
                                                 ALU.add, ALU.mult).then_inc(r_used.sem, 1)
                    for c in range(C):
                        dve.wait_ge(r_used.sem, r_used.at(t, c + 1))
                        dve.scalar_tensor_tensor(pre_n[:, c, :], bank[4 * par + 2][:, c * B:(c + 1) * B], column("b_ih", 4 + c), pre_n[:, c, :],
                                                 ALU.add, ALU.add).then_inc(pre_ready.sem, 1)
                    dve.wait_ge(z_ready.sem, z_ready.at(t, 2))
                    dve.tensor_tensor(z_h, gate_z, h_buf[:, par], ALU.mult).then_inc(z_h_ready.sem, 1)
                    dve.wait_ge(one_z_ready.sem, one_z_ready.at(t, 1))
                    for c in range(C):
                        dve.wait_ge(n_ready.sem, n_ready.at(t, c + 1))
                        dve.tensor_tensor(cand[:, c, :], cand[:, c, :], one_z[:, c, :], ALU.mult).then_inc(prod_ready.sem, 1)
                    dve.wait_ge(x_added.sem, x_added.at(t, 1))
                    for c in range(C):
                        dve.wait_ge(prod_ready.sem, prod_ready.at(t, c + 1))
                        dve.tensor_tensor(h_buf[:, 1 - par, c, :], cand[:, c, :], z_h[:, c, :], ALU.add).then_inc(h_ready.sem, 1)

            one, two = Chain(dve, chain1.sem), Chain(dve, chain2.sem)
            LEAD_LINKS = 2

            def of_lot(k, c, s):
                return mod[:, k + c, bass.ds(s * LOT_B, LOT_B)].rearrange("p (b o) -> p b o", o=1).to_broadcast([P, LOT_B, T])

            def tokens(ap):
                return ap.rearrange("p (b t) -> p b t", t=T)

            def moments(src, stats, mean_var, chain):
                for g in range(G):
                    ins = dve.bn_stats(stats[:, g, :], src[:, g, :])
                chain.link(ins)
                dve.memset(tick[:, 0:1], 0.0)
                for g in range(G):
                    ins = dve.bn_aggr(mean_var[:, g, :], stats[:, g, :])
                chain.link(ins)

            def normalise(s, k, src, meanwhile=lambda: None):
                moments(src, stats, mean_var, one)
                dve.tensor_scalar(spread[:, :], mean_var[:, :, 1], EPS, None, ALU.add).then_inc(spread_ready.sem, 1)
                meanwhile()
                dve.wait_ge(rstd_ready.sem, rstd_ready.at(s, k + 1))
                for g in range(G):
                    dve.tensor_scalar(xn[:, g, :], src[:, g, :], mean_var[:, g, 0:1], rstd[:, g:g + 1], ALU.subtract, ALU.mult)\
                       .then_inc(xn_ready.sem, 1)

            def normalise3(r):
                moments(x2_tok, stats3, mean_var3, two)
                two.link(dve.tensor_tensor(spread3[:, :], mean_var3[:, :, 0], mean_var3[:, :, 0], ALU.mult))
                dve.scalar_tensor_tensor(spread3[:, :], spread3[:, :], EPS, mean_var3[:, :, 1], ALU.add, ALU.add).then_inc(spread3_ready.sem, 1)
                dve.wait_ge(rstd3_ready.sem, rstd3_ready.at(r, 1))
                for g in range(G):
                    dve.tensor_scalar(xn3[:, g, :], x2_tok[:, g, :], rstd3[:, g:g + 1], None, ALU.mult).then_inc(xn3_ready.sem, 1)

            def modulate(ring, turn, name, dst, lot_of, scale, shift, ready):
                for c in range(C):
                    ps = ring.wait_filled(dve, turn, name, c)
                    dve.tensor_tensor(tokens(dst[:, c, :]), tokens(ps[:, :]), of_lot(scale, c, lot_of), ALU.mult).then_inc(ring.emptied_sem["dve"], 1)
                    ring.wait_emptied(dve, turn, name, c)
                    dve.tensor_tensor(tokens(dst[:, c, :]), tokens(dst[:, c, :]), of_lot(shift, c, lot_of), ALU.add).then_inc(ready.sem, 1)

            def heads(ap):
                return ap.rearrange("p (h t) -> p h t", t=T)

            def per_head(ap):
                return ap.rearrange("p (h o) -> p h o", o=1).to_broadcast([P, 16, T])

            def shifted(ring, turn, k, layer, prob, chain):
                ps = ring.wait_filled(dve, turn, "s", k)
                chain.link(dve.tensor_reduce(soft_max[:, layer, :], heads(ps[:, :]), AX_X, ALU.max))
                dve.tensor_tensor(heads(prob), heads(ps[:, :]), per_head(soft_max[:, layer, :]), ALU.subtract).then_inc(ring.emptied_sem["dve"], 1)

            def shares(turn, k, layer, prob, exp_ready, probT_ready, chain, before_turn):
                dve.wait_ge(exp_ready.sem, exp_ready.at(turn, k + 1))
                chain.link(dve.tensor_reduce(soft_sum[:, layer, :], heads(prob), AX_X, ALU.add))
                chain.link(dve.reciprocal(soft_inv[:, layer, :], soft_sum[:, layer, :]))
                chain.link(dve.tensor_tensor(heads(prob), heads(prob), per_head(soft_inv[:, layer, :]), ALU.mult))
                before_turn()
                for b in range(GB):
                    rows_b = slice(b * T, (b + 1) * T)
                    ins = dve.transpose(probT[rows_b, :, b * T:(b + 1) * T], heads(prob)[rows_b, :, :])
                ins.then_inc(probT_ready.sem, 1)

            def gate(s, which, bias, k):
                dve.wait_ge(y_ready.sem, y_ready.at(s, which + 1))
                for c in range(C):
                    dve.scalar_tensor_tensor(tokens(yT[:, c, :]), tokens(y_bank[c][:, :]), column(bias, c), of_lot(k, c, s),
                                             ALU.add, ALU.mult).then_inc(yT_ready.sem, 1)

            def add_tokens(ring, turn, name, dst, other):
                for j in range(2):
                    ps = ring.wait_filled(dve, turn, name, j)
                    pair = slice(2 * j, 2 * j + 2)
                    dve.tensor_tensor(dst[:, pair, :].rearrange("p g d -> p (g d)"), ps[:, :],
                                      other[:, pair, :].rearrange("p g d -> p (g d)"), ALU.add).then_inc(ring.emptied_sem["dve"], 1)
                ring.wait_emptied(dve, turn, name, 1)

            def lead(s):
                ring1.wait_emptied(dve, s - 1, "xin", 1)
                normalise(s, 0, x0_tok)
                modulate(ring1, s - 1, "m1", xm_sum, s, SCALE1, SHIFT1, xm_ready)
                for c in range(C):
                    dve.wait_ge(xm_high_ready.sem, xm_high_ready.at(s, c + 1))
                    dve.tensor_tensor(xm_low[:, c, :], xm_sum[:, c, :], xm_high[:, c, :].bitcast(F32), ALU.subtract).then_inc(mod_ready.sem, 1)

            def sum_squares(r):
                for g in range(G):
                    dve.wait_ge(sq_ready.sem, sq_ready.at(r, g + 1))
                    two.link(dve.tensor_reduce(ss2[:, g, :], qk_sq.rearrange("p (h d) -> p h d", d=DH2), AX_X, ALU.add))
                    dve.tensor_scalar(ss2[:, g, :], ss2[:, g, :], 1.0 / DH2, EPS, ALU.mult, ALU.add).then_inc(ss2_ready.sem, 1)

            def norm_heads(r, g):
                dve.wait_ge(rstd2_ready.sem, rstd2_ready.at(r, g + 1))
                qk = qk2[:, g, :].rearrange("p (h d) -> p h d", d=DH2)
                dve.tensor_tensor(qk, qk, rstd2[:, g, :].rearrange("p (h o) -> p h o", o=1).to_broadcast([P, 2 * H, DH2]), ALU.mult)\
                   .then_inc(qkn_ready.sem, 1)

            def widen(r, g):
                if g > 0:
                    ring_of(r).wait_filled(dve, r, "s", g - 1)
                ps = ring_of(r).wait_filled(dve, r, "t", g)
                dve.tensor_scalar(q2T[:, g % 2, :, :].rearrange("p c n -> p (c n)"), ps[:, 0:D], column("g_q"), None, ALU.mult)
                mask = k_mask[:, :].rearrange("p (a h o) -> p a h o", a=1, o=1).to_broadcast([P, GB // 2, HC, T])
                for c in range(C):
                    for b in range(0, GB, 2):
                        src = ps[:, D + c * P + b * T:D + c * P + (b + 2) * T].rearrange("p (b o t) -> p b o t", b=2, o=1).to_broadcast([P, 2, HC, T])
                        ins = dve.tensor_tensor(k_wide[:, c, b:b + 2, :, :], src, mask, ALU.mult)
                ins.then_inc(ring_of(r).emptied_sem["dve"], 1)

            def add_out2(r, g):
                ps = ring_of(r).wait_filled(dve, r, "w", g)
                dve.tensor_tensor(x2_tok[:, g, :], ps[:, 0:D], x2_tok[:, g, :], ALU.add).then_inc(ring_of(r).emptied_sem["dve"], 1)

            def lot(s, r, ahead):
                if s is not None:
                    one.start(LEAD_LINKS + s * CHAIN1)
                if r is not None:
                    two.start(r * CHAIN2)
                    dve.wait_ge(doubled.sem, doubled.at(r, 1))
                    add_tokens(ring_of(r), r, "f", x2_tok, x2_tok)
                    normalise3(r)
                    modulate(ring_of(r), r, "m3", xm3, r, SCALE3, SHIFT3, mod3_ready)
                    sum_squares(r)
                if s is None:
                    norm_heads(r, 0)
                    widen(r, 0)
                    for g in range(G):
                        shifted(ring3, r, g, 1, prob2, two)
                        if g > 0:
                            add_out2(r, g - 1)
                        if g + 1 < G:
                            norm_heads(r, g + 1)

                        def last_turned3(g=g):
                            if g > 0:
                                ring3.wait_filled(dve, r, "o", g - 1)

                        shares(r, g, 1, prob2, exp2_ready, probT2_ready, two, last_turned3)
                        if g + 1 < G:
                            widen(r, g + 1)
                    add_out2(r, G - 1)
                    return
                for q in range(QUADS):
                    if s is not None:
                        def last_turned(q=q):
                            if r is not None and q > 0:
                                ring_of(r).wait_filled(dve, r, "o", q - 1)

                        shifted(ring1, s, q, 0, prob, one)
                        shares(s, q, 0, prob, exp_ready, probT_ready, one, last_turned)
                    if r is not None:
                        norm_heads(r, q)
                        if q > 0:
                            add_out2(r, q - 1)
                        widen(r, q)
                        shifted(ring_of(r), r, q, 1, prob2, two)

                        def last_turned2(q=q):
                            if s is not None:
                                ring1.wait_filled(dve, s, "o", QUAD * q + QUAD - 1)
                            elif q > 0:
                                ring_of(r).wait_filled(dve, r, "o", q - 1)

                        shares(r, q, 1, prob2, exp2_ready, probT2_ready, two, last_turned2)
                if s is not None:
                    gate(s, 0, "out_b", GATE1)
                    add_tokens(ring1, s, "y", x_tok, x0_tok)

                def last_added():
                    if r is not None:
                        add_out2(r, QUADS - 1)

                if s is not None:
                    normalise(s, 1, x_tok, last_added)
                    modulate(ring1, s, "m2", xm, s, SCALE2, SHIFT2, mod_ready)
                else:
                    last_added()
                if ahead is not None:
                    lead(ahead)
                if s is not None:
                    gate(s, 1, "ffn_b2", GATE2)
                assert s is None or ahead is None or one.k == CHAIN1, one.k
                assert r is None or two.k == CHAIN2, two.k

            one.start(0)
            lead(0)
            dve.wait_ge(zeroed.sem, 2)
            lot(0, None, 1)
            with dve.Fori(1, LOTS - 1) as s:
                lot(s, s - 1, s + 1)
            lot(LOTS - 1, LOTS - 2, None)
            lot(None, LOTS - 1, None)

            ring3.wait_emptied(dve, LOTS - 1, "xo", 1)
            dve.wait_ge(kept_in.sem, 16)
            for c in range(C):
                dve.tensor_copy(q_of[0][:, c, :], condT[:, c, :]).then_inc(q_ready.sem, 1)
            dve.tensor_copy(p_of[0], condT[:, :, :]).then_inc(p_ready.sem, 1)
            def cubed(t, i, c):
                dve.wait_ge(q_sq_ready.sem, q_sq_ready.at(t, C * i + c + 1))
                dve.scalar_tensor_tensor(net["v"][:, c, :], net["sq"][:, c, :], -3.0 - (1 / STEP[3] if i == 3 else 0.0), q_of[i][:, c, :],
                                         ALU.add, ALU.mult).then_inc(v_ready.sem, 1)

            def based(t, i, c):
                dve.wait_ge(v_ready.sem, v_ready.at(t, C * i + c + 1))
                if i == 3 and c == 0:
                    dve.wait_ge(q_part3_ready.sem, q_part3_ready.at(t, 1))
                dve.scalar_tensor_tensor(net["base"][:, c, :], net["v"][:, c, :], -STEP[i] / 3, (q_of[0] if i < 3 else net["q_part3"])[:, c, :],
                                         ALU.mult, ALU.add).then_inc(base_ready.sem, 1)

            def raised(t, i, c):
                dve.wait_ge(base_ready.sem, base_ready.at(t, C * i + c + 1))
                dve.wait_ge(coupled.sem, coupled.at(t, C * i + c + 1))
                dst = q_of[i + 1] if i < 3 else net["q_raw"]
                dve.scalar_tensor_tensor(dst[:, c, :], bank[2 * (i % 2) + c][:, 0:B], STEP[i], net["base"][:, c, :], ALU.mult, ALU.add)\
                   .then_inc(q_ready.sem if i < 3 else q_raw_ready.sem, 1)

            def clip_q(t, c):
                dve.wait_ge(q_raw_ready.sem, q_raw_ready.at(t, c + 1))
                dve.tensor_scalar(q_of[0][:, c, :], net["q_raw"][:, c, :], CLAMP, -CLAMP, ALU.min, ALU.max).then_inc(q_ready.sem, 1)

            def next_p(t, i):
                dve.wait_ge(q_ready.sem, q_ready.at(t, C * i + C))
                dve.wait_ge(p_rest_ready.sem, p_rest_ready.at(t, i + 1))
                dve.scalar_tensor_tensor(p_of[i + 1] if i < 3 else net["p_raw"], q_of[i], STEP[i] * EPSILON, net["p_rest"], ALU.mult, ALU.add)\
                   .then_inc(p_ready.sem if i < 3 else p_raw_ready.sem, 1)

            def clip_p(t):
                dve.wait_ge(p_raw_ready.sem, p_raw_ready.at(t, 1))
                dve.tensor_scalar(p_of[0], net["p_raw"], CLAMP, -CLAMP, ALU.min, ALU.max).then_inc(p_ready.sem, 1)

            def net_step(t):
                for i in range(4):
                    next_p(t, i)
                    cubed(t, i, 0)
                    if i == 3:
                        clip_p(t)
                    cubed(t, i, 1)
                    based(t, i, 0)
                    based(t, i, 1)
                    raised(t, i, 0)
                    if i == 3:
                        clip_q(t, 0)
                    raised(t, i, 1)
                    if i == 3:
                        clip_q(t, 1)

            net_step(0)
            with dve.Fori(0, T // 2 - 1) as i:
                net_step(2 * i + 1)
                net_step(2 * i + 2)
            net_step(T - 1)


_INS = ["x", "cond_2048", "L0_cond_W_ih", "L0_cond_W_hh", "L0_cond_b_ih", "L0_cond_b_hh", "L1_cond_ada_w", "L1_cond_ada_b",
        "L1_cond_qkv_w", "L1_cond_qkv_b", "L1_cond_out_w", "L1_cond_out_b", "L1_cond_ffn_w1", "L1_cond_ffn_b1",
        "L1_cond_ffn_w2", "L1_cond_ffn_b2", "L2_cond_W_emb", "L2_cond_b_emb", "L2_cond_g_norm", "L2_cond_W_qkv",
        "L2_cond_g_q", "L2_cond_g_k", "L2_cond_W_out", "L3_cond_coupling", "L3_cond_bias"]


def kernel(**inputs):
    import numpy as _np
    import concourse.bacc as _bacc
    from concourse import mybir as _mybir
    from concourse.bass_utils import run_bass_kernel_spmd as _run

    nc = _bacc.Bacc("TRN2", target_bir_lowering=False, num_devices=1, dynamic_dma_scratch_size=1024)
    arrays, args = {}, {}
    for name in _INS:
        a = _np.ascontiguousarray(inputs[name])
        arrays[f"in_{name}"] = a
        args[name] = nc.dram_tensor(f"in_{name}", a.shape, _mybir.dt.from_np(a.dtype), kind="ExternalInput").ap()
    out = nc.dram_tensor("out_x", (B, T, D), F32, kind="ExternalOutput").ap()
    build(nc, args, out)
    r = _run(nc, [arrays], core_ids=[0])
    return r.results[0]["out_x"]
```
